# Optimizing a Trainium2 kernel written in Bass

```python
import numpy as np
import jax
import jax.numpy as jnp

def _softmax(x, axis=-1):
    return jax.nn.softmax(x, axis=axis)

def _gelu(x):
    return jax.nn.gelu(x, approximate=True)

def _silu(x):
    return jax.nn.silu(x)

def _sigmoid(x):
    return jax.nn.sigmoid(x)

def _layernorm(x, axis=-1, eps=1e-05):
    m = jnp.mean(x, axis=axis, keepdims=True)
    v = jnp.var(x, axis=axis, keepdims=True)
    return (x - m) / jnp.sqrt(v + eps)

def _scatter_add(tgt, idx, src, axis=0):
    return tgt.at[idx].add(src)

def _segment_sum(src, seg, n):
    return jax.ops.segment_sum(src, seg, n)
kernel_name = 'mk_perceiver_d1_seqx_r4_85c551'

def setup_inputs(seed: int=0):
    np.random.seed(seed)
    _w = jnp.asarray

    def _rec_inputs():
        import jax
        import jax.numpy as jnp
        _rk = jax.random.key(seed)
        x = -0.0003929 + 0.9999 * jax.random.normal(jax.random.fold_in(_rk, 1), (64, 32, 256), jnp.float32)
        _lenS = 32 - jax.random.randint(jax.random.fold_in(_rk, 7), (64,), 0, max(1, 32 // 4) + 1, jnp.int32)
        _lenS2 = 257 - jax.random.randint(jax.random.fold_in(_rk, 8), (64,), 0, max(1, 257 // 4) + 1, jnp.int32)
        _ctx_1024P = jax.random.normal(jax.random.fold_in(_rk, 11), (64, 16, 256), jnp.float32)
        _ctx_1024c = jax.random.dirichlet(jax.random.fold_in(_rk, 511), 0.3 * jnp.ones((16,), jnp.float32), (64, 257))
        _ctx_1024t = jnp.einsum('bsk,bkd->bsd', _ctx_1024c, _ctx_1024P)
        _ctx_1024t = _ctx_1024t * jax.lax.rsqrt(jnp.mean(jnp.square(_ctx_1024t)) + 1e-12) * 0.953939
        ctx_1024 = 2.81802e-05 + 1.00001 * (_ctx_1024t + 0.3 * jax.random.normal(jax.random.fold_in(_rk, 611), (64, 257, 256), jnp.float32))
        return (x, ctx_1024)
    x, ctx_1024 = _rec_inputs()

    def _L0_xattn_setup():
        import jax, jax.numpy as jnp
        import numpy as np
        B, S, D_Q, D_K, D_V, D_H, D_O = (8, 512, 256, 256, 256, 256, 256)
        key = jax.random.key(seed)
        ks = jax.random.split(key, 9)
        lim_q = 1.0 / np.sqrt(D_Q)
        lim_k = 1.0 / np.sqrt(D_K)
        lim_v = 1.0 / np.sqrt(D_V)
        return {'input_query': jax.random.normal(ks[0], (B, S, D_Q), jnp.float32), 'input_key': jax.random.normal(ks[1], (B, S, D_K), jnp.float32), 'input_value': jax.random.normal(ks[2], (B, S, D_V), jnp.float32), 'Wq': jax.random.uniform(ks[3], (D_H, D_Q), jnp.float32, -lim_q, lim_q), 'bq': jax.random.uniform(ks[4], (D_H,), jnp.float32, -lim_q, lim_q), 'Wk': jax.random.uniform(ks[5], (D_H, D_K), jnp.float32, -lim_k, lim_k), 'bk': jax.random.uniform(ks[6], (D_H,), jnp.float32, -lim_k, lim_k), 'Wv': jax.random.uniform(ks[7], (D_O, D_V), jnp.float32, -lim_v, lim_v), 'bv': jax.random.uniform(ks[8], (D_O,), jnp.float32, -lim_v, lim_v)}
    _L0_xattn_all = _L0_xattn_setup()
    _L0_xattn_in = {k: v for k, v in _L0_xattn_all.items() if k in ('Wq', 'bq', 'Wk', 'bk', 'Wv', 'bv')}
    del _L0_xattn_all

    def _L0_attn_setup():
        import jax, jax.numpy as jnp
        import numpy as np
        N_HEAD = 16
        ROPE_BASE = 10000.0

        def _rope(Y, d_param):
            b, h, t, dh = Y.shape
            mid = d_param // 2
            Y1 = Y[:, :mid]
            Y2 = Y[:, mid:]
            Ym1 = jnp.concatenate([Y1, Y2], axis=1)
            Ym2 = jnp.concatenate([-Y2, Y1], axis=1)
            j = jnp.arange(t, dtype=Y.dtype)[:, None]
            i = jnp.arange(dh // 2, dtype=Y.dtype)[None, :]
            theta = j * jnp.power(jnp.asarray(ROPE_BASE, Y.dtype), -2.0 * i / dh)
            cos = jnp.cos(theta)
            sin = jnp.sin(theta)
            theta1 = jnp.concatenate([cos, cos], axis=1)
            theta2 = jnp.concatenate([sin, sin], axis=1)
            return Ym1 * theta1 + Ym2 * theta2
        key = jax.random.key(seed)
        ks = jax.random.split(key, 9)
        b, t, e = (2, 512, 256)
        s = 1.0 / np.sqrt(e)
        return {'x': jax.random.normal(ks[0], (b, t, e), dtype=jnp.float32), 'Wq': jax.random.normal(ks[1], (e, e), dtype=jnp.float32) * s, 'bq': jax.random.normal(ks[2], (e,), dtype=jnp.float32) * 0.01, 'Wk': jax.random.normal(ks[3], (e, e), dtype=jnp.float32) * s, 'bk': jax.random.normal(ks[4], (e,), dtype=jnp.float32) * 0.01, 'Wv': jax.random.normal(ks[5], (e, e), dtype=jnp.float32) * s, 'bv': jax.random.normal(ks[6], (e,), dtype=jnp.float32) * 0.01, 'Wo': jax.random.normal(ks[7], (e, e), dtype=jnp.float32) * s, 'bo': jax.random.normal(ks[8], (e,), dtype=jnp.float32) * 0.01}
    _L0_attn_all = _L0_attn_setup()
    _L0_attn_in = {k: v for k, v in _L0_attn_all.items() if k in ('Wq', 'bq', 'Wk', 'bk', 'Wv', 'bv', 'Wo', 'bo')}
    del _L0_attn_all

    def _L0_ffn_setup():
        import jax, jax.numpy as jnp
        import numpy as np
        TOP_K = 2
        N_EXPERTS = 8
        key = jax.random.key(seed)
        k_x, k_g, k_w1, k_w2 = jax.random.split(key, 4)
        B, S, d_in, d_hid, d_out, E = (8, 512, 256, 512, 256, N_EXPERTS)
        s_gate = float(np.sqrt(6.0 / (d_in + E)))
        s_w1 = float(np.sqrt(6.0 / (d_in + d_hid)))
        s_w2 = float(np.sqrt(6.0 / (d_hid + d_out)))
        x = jax.random.normal(k_x, (B, S, d_in), dtype=jnp.float32)
        gate_W = jax.random.uniform(k_g, (d_in, E), jnp.float32, -s_gate, s_gate)
        W1 = jax.random.uniform(k_w1, (E, d_in, d_hid), jnp.float32, -s_w1, s_w1)
        b1 = jnp.zeros((E, d_hid), jnp.float32)
        W2 = jax.random.uniform(k_w2, (E, d_hid, d_out), jnp.float32, -s_w2, s_w2)
        b2 = jnp.zeros((E, d_out), jnp.float32)
        return {'x': x, 'gate_W': gate_W, 'W1': W1, 'b1': b1, 'W2': W2, 'b2': b2}
    _L0_ffn_all = _L0_ffn_setup()
    _L0_ffn_in = {k: v for k, v in _L0_ffn_all.items() if k in ('gate_W', 'W1', 'b1', 'W2', 'b2')}
    del _L0_ffn_all
    return {'x': x, 'ctx_1024': ctx_1024, 'L0_xattn_Wq': _L0_xattn_in['Wq'], 'L0_xattn_bq': _L0_xattn_in['bq'], 'L0_xattn_Wk': _L0_xattn_in['Wk'], 'L0_xattn_bk': _L0_xattn_in['bk'], 'L0_xattn_Wv': _L0_xattn_in['Wv'], 'L0_xattn_bv': _L0_xattn_in['bv'], 'L0_attn_Wq': _L0_attn_in['Wq'], 'L0_attn_bq': _L0_attn_in['bq'], 'L0_attn_Wk': _L0_attn_in['Wk'], 'L0_attn_bk': _L0_attn_in['bk'], 'L0_attn_Wv': _L0_attn_in['Wv'], 'L0_attn_bv': _L0_attn_in['bv'], 'L0_attn_Wo': _L0_attn_in['Wo'], 'L0_attn_bo': _L0_attn_in['bo'], 'L0_ffn_gate_W': _L0_ffn_in['gate_W'], 'L0_ffn_W1': _L0_ffn_in['W1'], 'L0_ffn_b1': _L0_ffn_in['b1'], 'L0_ffn_W2': _L0_ffn_in['W2'], 'L0_ffn_b2': _L0_ffn_in['b2']}

def reference(x, ctx_1024, L0_xattn_Wq, L0_xattn_bq, L0_xattn_Wk, L0_xattn_bk, L0_xattn_Wv, L0_xattn_bv, L0_attn_Wq, L0_attn_bq, L0_attn_Wk, L0_attn_bk, L0_attn_Wv, L0_attn_bv, L0_attn_Wo, L0_attn_bo, L0_ffn_gate_W, L0_ffn_W1, L0_ffn_b1, L0_ffn_W2, L0_ffn_b2):
    import jax
    import jax.numpy as jnp

    def _L0_xattn_ref(input_query, input_key, input_value, Wq, bq, Wk, bk, Wv, bv):
        import jax, jax.numpy as jnp
        import numpy as np
        B, S, D_Q, D_K, D_V, D_H, D_O = (8, 512, 256, 256, 256, 256, 256)
        q = jnp.einsum('bsd,hd->bsh', input_query, Wq) + bq
        k = jnp.einsum('bsd,hd->bsh', input_key, Wk) + bk
        v = jnp.einsum('bsd,od->bso', input_value, Wv) + bv
        scale = 1.0 / jnp.sqrt(jnp.float32(q.shape[-1]))
        scores = jax.nn.softmax(jnp.einsum('bqh,bkh->bqk', q, k) * scale, axis=-1)
        out = jnp.einsum('bqk,bko->bqo', scores, v)
        return out

    def _L0_attn_ref(x, Wq, bq, Wk, bk, Wv, bv, Wo, bo):
        import jax, jax.numpy as jnp
        import numpy as np
        N_HEAD = 16
        ROPE_BASE = 10000.0

        def _rope(Y, d_param):
            b, h, t, dh = Y.shape
            mid = d_param // 2
            Y1 = Y[:, :mid]
            Y2 = Y[:, mid:]
            Ym1 = jnp.concatenate([Y1, Y2], axis=1)
            Ym2 = jnp.concatenate([-Y2, Y1], axis=1)
            j = jnp.arange(t, dtype=Y.dtype)[:, None]
            i = jnp.arange(dh // 2, dtype=Y.dtype)[None, :]
            theta = j * jnp.power(jnp.asarray(ROPE_BASE, Y.dtype), -2.0 * i / dh)
            cos = jnp.cos(theta)
            sin = jnp.sin(theta)
            theta1 = jnp.concatenate([cos, cos], axis=1)
            theta2 = jnp.concatenate([sin, sin], axis=1)
            return Ym1 * theta1 + Ym2 * theta2
        b, t, e = x.shape
        h = N_HEAD
        dh = e // h

        def proj(W, bias):
            y = jnp.einsum('bte,fe->btf', x, W) + bias
            return y.reshape(b, t, h, dh).transpose(0, 2, 1, 3)
        q = _rope(proj(Wq, bq), e)
        k = _rope(proj(Wk, bk), e)
        v = proj(Wv, bv)
        scale = jnp.sqrt(jnp.asarray(dh, x.dtype))
        att = jnp.einsum('bhqd,bhkd->bhqk', q, k) / scale
        causal = jnp.tril(jnp.ones((t, t), dtype=bool))
        att = jnp.where(causal[None, None], att, -jnp.inf)
        att = jax.nn.softmax(att, axis=-1)
        y = jnp.einsum('bhqk,bhkd->bhqd', att, v)
        y = y.transpose(0, 2, 1, 3).reshape(b, t, e)
        return jnp.einsum('bte,fe->btf', y, Wo) + bo

    def _L0_ffn_ref(x, gate_W, W1, b1, W2, b2):
        import jax, jax.numpy as jnp
        import numpy as np
        TOP_K = 2
        N_EXPERTS = 8
        E = W1.shape[0]
        d_in = x.shape[-1]
        d_out = W2.shape[-1]
        x_flat = x.reshape(-1, d_in)
        logits = x_flat @ gate_W
        gates = jax.nn.softmax(logits, axis=-1)
        tk_g, tk_i = jax.lax.top_k(gates, TOP_K)
        tk_g = tk_g / (jnp.sum(tk_g, axis=-1, keepdims=True) + 1e-08)
        cw = jnp.sum(jax.nn.one_hot(tk_i, E, dtype=x.dtype) * tk_g[..., None], axis=1)
        out = x_flat
        for e in range(E):
            h = jax.nn.relu(x_flat @ W1[e] + b1[e])
            out = out + cw[:, e:e + 1] * (h @ W2[e] + b2[e])
        return out.reshape(x.shape[:-1] + (d_out,))
    x = x + _L0_xattn_ref(_layernorm(x, axis=-1), ctx_1024, ctx_1024, L0_xattn_Wq, L0_xattn_bq, L0_xattn_Wk, L0_xattn_bk, L0_xattn_Wv, L0_xattn_bv)
    x = x + _L0_attn_ref(_layernorm(x, axis=-1), L0_attn_Wq, L0_attn_bq, L0_attn_Wk, L0_attn_bk, L0_attn_Wv, L0_attn_bv, L0_attn_Wo, L0_attn_bo)
    x = x + _L0_ffn_ref(_layernorm(x, axis=-1), L0_ffn_gate_W, L0_ffn_W1, L0_ffn_b1, L0_ffn_W2, L0_ffn_b2)
    return x

_drawn_inputs = setup_inputs


def setup_inputs(seed=0):
    import zlib

    import numpy as np

    out = dict(_drawn_inputs(seed))
    spreads = {'L0_ffn_b1': (0.0, 0.288), 'L0_ffn_b2': (0.0, 0.1)}
    factors = {'L0_xattn_bq': 8.0,
     'L0_xattn_bk': 64.0,
     'L0_attn_bq': 8.0,
     'L0_attn_bk': 24.939,
     'L0_attn_bv': 3.436,
     'L0_attn_bo': 4.652}
    for name, (base, spread) in spreads.items():
        noise = np.random.default_rng([zlib.crc32(name.encode()), seed]).standard_normal(out[name].shape)
        drawn = base * np.exp(spread * noise) if base else spread * noise
        out[name] = jnp.asarray(drawn.astype(out[name].dtype))
    for name, factor in factors.items():
        out[name] = (out[name] * factor).astype(out[name].dtype)
    return out
```

```python
from contextlib import ExitStack

import numpy as np

import concourse.bass as bass
from concourse import mybir

ALU = mybir.AluOpType
ACT = mybir.ActivationFunctionType
AX = mybir.AxisListType
F32 = mybir.dt.float32
BF16 = mybir.dt.bfloat16
I32 = mybir.dt.int32
U32 = mybir.dt.uint32

P = 128
B, T, D = 64, 32, 256
S = 257
H, DH = 16, 16
E, HID = 8, 512
N = B * T
GB = P // T
G = N // P
DC = D // P
SK = (S - 1) // P
HC = P // DH
HQ = P // T
TOP = 2
TILES = (N * TOP - E) // P + E
LOOK = 4
TABLE = TILES + 1
SLOTS = E * N + TABLE * P
ROPE_BASE = 10000.0
LN_EPS = 1e-5
MASKED = -1e30

C_IDENT = 0
C_ROPE = C_IDENT + P
C_HEAD = C_ROPE + T
C_VHEAD = C_HEAD + HC
C_CAUSAL = C_VHEAD + HQ
C_EXPERT = C_CAUSAL + T
C_FIRST = C_EXPERT + E
C_TOKEN = C_FIRST + E
C_TILE = C_TOKEN + 1
C_FULL = C_TILE + TABLE
C_EARLIER = C_FULL + N // P
C_END = C_EARLIER + P


def shape_constants():
    c = np.zeros((P, C_END), np.float32)
    p = np.arange(P)
    c[:, C_IDENT:C_IDENT + P] = np.eye(P)
    t = np.arange(T)[None, :]
    theta = t * ROPE_BASE ** (-2.0 * (p % (DH // 2))[:, None] / DH)
    c[:, C_ROPE:C_ROPE + T] = np.cos(theta) + np.sin(theta)
    c[:, C_HEAD:C_HEAD + HC] = (p // DH)[:, None] == np.arange(HC)[None, :]
    c[:, C_VHEAD:C_VHEAD + HQ] = (p // T)[:, None] == np.arange(HQ)[None, :]
    c[:, C_CAUSAL:C_CAUSAL + T] = np.where(np.arange(T)[None, :] > (p % T)[:, None], MASKED, 0.0)
    c[:, C_EXPERT:C_EXPERT + E] = np.arange(E)
    c[:, C_FIRST:C_FIRST + E] = np.arange(E) * N
    c[:, C_TOKEN] = p
    c[:, C_TILE:C_TILE + TABLE] = np.arange(TABLE)
    c[:, C_FULL:C_FULL + N // P] = np.arange(N // P) * P
    c[:, C_EARLIER:C_EARLIER + P] = p[:, None] < p[None, :]
    return c


def empty_slots():
    slots = np.zeros((SLOTS, 2), np.int32)
    slots[:, 0] = N + np.arange(SLOTS) % P
    return slots


class Group:

    def __init__(self, i, c):
        self.i, self.c, self.p = i, c, c % 2

    def count(self, before=0):
        return self.i * 2 + (self.c + 1 - before)

    def visits(self):
        return self.i + (self.c // 2 + 1)

    def index(self):
        return self.i * 2 + self.c


class Tile:

    def __init__(self, i, c):
        self.i, self.c, self.pair, self.slot = i, c, c % 2, c % LOOK

    def index(self):
        return self.i * LOOK + self.c

    def count(self, before=0):
        return self.i * LOOK + (self.c + 1 - before)

    def pair_visits(self):
        return self.i * (LOOK // 2) + (self.c // 2 + 1)

    def slot_visits(self):
        return self.i + (self.c // LOOK + 1)

    def ahead(self, n):
        return Tile(self.i, self.c + n)


def tiles(engine, step):
    whole = (TILES - 2) // LOOK
    for c in range(LOOK):
        t = Tile(0, c)
        step(t, t.ahead(1), t.ahead(2))
    with engine.Fori(1, whole) as i:
        for c in range(LOOK):
            t = Tile(i, c)
            step(t, t.ahead(1), t.ahead(2))
    for n in range(whole * LOOK, TILES):
        t = Tile(n // LOOK, n % LOOK)
        step(t, *(t.ahead(k) if n + k < TILES else None for k in (1, 2)))


def wait(engine, semaphore, value):
    if not (isinstance(value, int) and value <= 0):
        engine.wait_ge(semaphore, value)


def pipeline(engine, slot):
    def groups(i, u, known):
        def group(c):
            if known is None:
                return Group(i, c)
            g = 2 * known + c
            return Group(known, c) if 0 <= g < G else None
        return group(u), group(u - 1), group(u - 2), group(u + 1)

    for t in range(4):
        slot(*groups(t // 2, t % 2, t // 2))
    with engine.Fori(2, G // 2 - 1) as i:
        for u in range(2):
            slot(*groups(i, u, None))
    for s in range(G - 2, G + 2):
        slot(*groups(s // 2, s % 2, s // 2))


def wait_apart(engine, semaphore, value, passed):
    wait(engine, semaphore, value)
    if not isinstance(value, int):
        engine.sem_inc(passed, 1)


def perceiver_layer(nc, x, ctx, consts, slots_init, xWq, xbq, xWk, xbk, xWvT, xbv, WqT, bq, WkT, bk, WvT, bv, WoT, bo,
                    gate_W, W1, b1, W2, b2, out):
    SCALE = float(D) ** -0.5
    ATT_SCALE = float(DH) ** -0.5

    with ExitStack() as stack:
        slots = nc.dram_tensor("slots", (SLOTS, 2), I32, kind="Internal").ap()
        normed_rows = nc.dram_tensor("normed_rows", (N + P, D), F32, kind="Internal").ap()

        def sb(name, shape, dt=F32):
            return stack.enter_context(nc.sbuf_tensor(name, shape, dt))

        def ps(name, shape=(P, 512), dt=F32):
            return stack.enter_context(nc.psum_tensor(name, list(shape), dt))

        def sem(name):
            return stack.enter_context(nc.semaphore(name))

        cst = sb("cst", [P, C_END])
        ident = cst[:, C_IDENT:C_IDENT + P]
        rope = cst[:, C_ROPE:C_ROPE + T]
        head_mask = cst[:, C_HEAD:C_HEAD + HC]
        vhead_mask = cst[:, C_VHEAD:C_VHEAD + HQ]
        causal = cst[:, C_CAUSAL:C_CAUSAL + T]
        raw_wq = sb("raw_wq", [P, DC, D])
        raw_wk = sb("raw_wk", [P, DC, D])
        raw_b = sb("raw_b", [P, 2, DC])
        wqk = sb("wqk", [P, DC, D])
        wqbk_rows = sb("wqbk_rows", [P, D])
        bqbk = sb("bqbk", [P, 1])
        bqk = sb("bqk", [P, DC])
        w_xv = sb("w_xv", [P, DC, D])
        w_q = sb("w_q", [P, DC, D])
        w_k = sb("w_k", [P, DC, D])
        w_v = sb("w_v", [P, DC, D])
        w_o = sb("w_o", [P, DC, D])
        b_cols = sb("b_cols", [P, 3, DC])
        xbv_rows = sb("xbv_rows", [P, D])
        bo_rows = sb("bo_rows", [P, D])
        power = sb("power", [P, 1])
        eps = sb("eps", [P, 1])

        x_in = sb("x_in", [P, 2, D])
        ctx_in = sb("ctx_in", [P, 2, GB, SK, D])
        ctx_last = sb("ctx_last", [P, 2, D])
        stats = sb("stats", [P, 3, 6])
        mean_var = sb("mean_var", [P, 3, 2])
        var_eps = sb("var_eps", [P, 3, 1])
        rstd = sb("rstd", [P, 3, 1])
        xn1 = sb("xn1", [P, 2, D])
        xn1T = sb("xn1T", [P, DC, P])
        x_bv = sb("x_bv", [P, 2, D])
        junk = sb("junk", [P, D])
        qbk = sb("qbk", [P, 2, 2])
        qkT = sb("qkT", [P, DC, P])
        ctxT = sb("ctxT", [P, 2, GB, DC, S])
        smax = sb("smax", [P, 2])
        ebias = sb("ebias", [P, 1])
        probs = sb("probs", [P, S])
        ssum = sb("ssum", [P, 2])
        probsT = sb("probsT", [P, SK, P])
        mix = sb("mix", [P, D])
        mixT = sb("mixT", [P, DC, P])
        x1 = sb("x1", [P, 2, D])
        xn2 = sb("xn2", [P, D])
        xn2T = sb("xn2T", [P, DC, P])
        x1_bo = sb("x1_bo", [P, 2, D])
        qT = sb("qT", [P, DC, P])
        kT = sb("kT", [P, DC, P])
        vT = sb("vT", [P, DC, GB, HQ, T])
        k_heads = sb("k_heads", [P, DC, GB, HC * T])
        v_heads = sb("v_heads", [P, GB, D])
        att = sb("att", [P, H, T])
        att_max = sb("att_max", [P, H])
        att_sub = sb("att_sub", [P, H, T])
        att_exp = sb("att_exp", [P, H, T])
        att_sum = sb("att_sum", [P, 2, H])
        attT = sb("attT", [P, H // HQ, P])
        y = sb("y", [P, D])
        yT = sb("yT", [P, DC, P])
        x2 = sb("x2", [P, 2, D])
        xn3 = sb("xn3", [P, 2, D])
        x3 = sb("x3", [P, 2, D])

        xn3T = sb("xn3T", [P, DC, P])
        gate_w = sb("gate_w", [P, DC, E])
        logitsT = sb("logitsT", [E, P])
        logit_bias = sb("logit_bias", [P, 1])
        gate_exp = sb("gate_exp", [P, E])
        gate_sum = sb("gate_sum", [P, 2])
        gates = sb("gates", [P, E])
        top_gates = sb("top_gates", [P, 8])
        top_experts = sb("top_experts", [P, 8], U32)
        top_expert = sb("top_expert", [P, TOP])
        top_sum = sb("top_sum", [P, 2])
        chosen = sb("chosen", [P, TOP, E])
        routed = sb("routed", [P, E], BF16)
        routed_before = sb("routed_before", [P, 2, E], BF16)
        earlier = sb("earlier", [P, P], BF16)
        ones = sb("ones", [P, P], BF16)
        places = sb("places", [P, E])
        place = sb("place", [P, TOP])
        place_slot = sb("place_slot", [P, 2, TOP], I32)
        token = sb("token", [P, 2])
        slot_row = sb("slot_row", [P, 2, TOP, 2], I32)
        counts = sb("counts", [1, E])
        started = sb("started", [1, E, N // P])
        tile_count = sb("tile_count", [1, E])
        tile_end = sb("tile_end", [1, E])
        row_skip = sb("row_skip", [1, E])
        passed = sb("passed", [1, TABLE, E])
        passed_rows = sb("passed_rows", [1, TABLE, E])
        tile_expert = sb("tile_expert", [1, 2, TABLE])
        tile_row = sb("tile_row", [1, 2, TABLE])
        table = sb("table", [1, 2, TABLE], I32)
        w1 = sb("w1", [P, E, DC, HID])
        w2 = sb("w2", [P, E, HID // P, D])
        b1_rows = sb("b1_rows", [P, E, HID])
        b2_rows = sb("b2_rows", [P, E, D])
        ids = sb("ids", [P, LOOK, 2], I32)
        reused = ctxT[:].rearrange("p g b c s -> p (g b c s)")
        xg = reused[:, 0:2 * D].rearrange("p (t d) -> p t d", t=2)
        xgT = reused[:, 2 * D:4 * D].rearrange("p (t c n) -> p t c n", t=2, c=DC)
        exp_out = reused[:, 4 * D:6 * D].rearrange("p (t d) -> p t d", t=2)
        hid = reused[:, 6 * D:6 * D + 2 * HID].rearrange("p (t d) -> p t d", t=2)
        hidT = reused[:, 6 * D + 2 * HID:6 * D + 4 * HID].rearrange("p (t c n) -> p t c n", t=2, c=HID // P)
        exp_scaled = sb("exp_scaled", [P, 2, D])

        turn = [ps("turn0"), ps("turn1")]
        xa = [ps("xa0"), ps("xa1")]
        sa = [ps("sa0"), ps("sa1"), ps("sa2")]
        gp = ps("gp")
        exp_bank = [sa[2], gp]

        consts_in, xw_in, sw_in, rows_in = sem("consts_in"), sem("xw_in"), sem("sw_in"), sem("rows_in")
        x_loaded = [sem("x_loaded0"), sem("x_loaded1")]
        ctx_loaded = [sem("ctx_loaded0"), sem("ctx_loaded1")]
        out_stored = [sem("out_stored0"), sem("out_stored1")]
        power_set, fused, fused_copied, fused_sum = sem("power_set"), sem("fused"), sem("fused_copied"), sem("fused_sum")
        names = ("stats1 mv1 eps1 rstd1 xn1 xn1T_ps xn1T_ready x_bv_ready qbk0 qbk_ready qkT_ps qkT_ready "
                 "turned ctxT_a ctxT_b scores smax0 smax1 ebias_ready probs_ready recip1 probsT_ps probsT_ready "
                 "mix_ps mix_ready mixT_ps mixT_ready xv_ps x1_ready "
                 "stats2 mv2 eps2 rstd2 xn2_ready xn2T_ps xn2T_ready x1_bo_ready qk_ps v_ps qT_ready kT_ready vT_ready "
                 "k_heads0 k_heads1 vrep_ps v_heads_ready att_ps att_masked att_max_ready att_sub_ready att_exp_ready "
                 "att_sum_ready recip2 attT_ps attT_ready y_ps y_ready yT_ps yT_ready o_ps x2_ready "
                 "stats3 mv3 eps3 rstd3 xn3_ready x3_ready "
                 "xn3T_ps xn3T_ready logitsT_ps logitsT_ready logits_ps logit_bias_ready gate_exp_ready "
                 "gate_recip gates_ready top_gates_ready top_index top_expert_ready chosen_ready routed_ready "
                 "routed_sum rank_ps places_ready place_ready place_slot_ready top_sum_ready top_recip row_ready token_ready "
                 "counts_ps counts_ready started_ready tile_count_ready tile_end_ready row_skip_ready passed_ready "
                 "passed_rows_ready tile_sums tile_rows table_ready "
                 "xgT_ps xgT_ready hid_ps hid_ready hidT_ps hidT_ready exp_ps exp_out_ready exp_scaled_ready")
        rows_stored = [sem("rows_stored0"), sem("rows_stored1")]
        slots_empty, spare_set, spare_stored, gate_in, w1_in, w2_in, b12_in, tri_ready = (
            sem(n) for n in ("slots_empty", "spare_set", "spare_stored", "gate_in", "w1_in", "w2_in", "b12_in", "tri_ready"))
        scattered = [sem("scattered0"), sem("scattered1")]
        ids_loaded = [sem(f"ids_loaded{n}") for n in range(LOOK)]
        gathered = [sem("gathered0"), sem("gathered1")]
        added = sem("added")
        dve_passed, pool_passed, pe_passed = sem("dve_passed"), sem("pool_passed"), sem("pe_passed")
        s = {n: sem(n) for n in names.split()}
        block = stack.enter_context(nc.Block())

        def as_heads(ap, h, w):
            return ap.rearrange("p (h w) -> p h w", h=h, w=w)

        @block.sync
        def _(sp):
            sp.dma_start(raw_wq[:], xWq.rearrange("(c p) d -> p c d", p=P)).then_inc(xw_in, 16)
            sp.dma_start(raw_wk[:], xWk.rearrange("(c p) d -> p c d", p=P)).then_inc(xw_in, 16)
            with nc.allow_non_contiguous_dma(reason="bias columns"):
                sp.dma_start(raw_b[:, 0], xbq.rearrange("(c p) -> p c", p=P)).then_inc(xw_in, 16)
                sp.dma_start(raw_b[:, 1], xbk.rearrange("(c p) -> p c", p=P)).then_inc(xw_in, 16)
            sp.dma_start(cst[:], consts).then_inc(consts_in, 16)

            def load(g):
                if not (isinstance(g.i, int) and g.index() < 2):
                    sp.wait_ge(s["x1_ready"], g.count(2))
                rows = bass.ds(g.index() * P, P)
                sp.dma_start(x_in[:, g.p], x[rows]).then_inc(x_loaded[g.p], 16)
                src = ctx[bass.ds(g.index() * GB, GB)]
                sp.dma_start(ctx_in[:, g.p].rearrange("p b s d -> p b (s d)"),
                             src[:, 0:S - 1].rearrange("b (p s) d -> p b (s d)", s=SK)).then_inc(ctx_loaded[g.p], 16)
                sp.dma_start(ctx_last[:, g.p],
                             src[:, S - 1:S].broadcast_to([GB, T, D])).then_inc(ctx_loaded[g.p], 16)

            load(Group(0, 0))
            for w, src in ((w_xv, xWvT), (w_q, WqT), (w_k, WkT), (w_v, WvT), (w_o, WoT)):
                sp.dma_start(w[:], src.rearrange("(c p) d -> p c d", p=P)).then_inc(sw_in, 16)
            with nc.allow_non_contiguous_dma(reason="bias columns"):
                for j, src in enumerate((bq, bk, bv)):
                    sp.dma_start(b_cols[:, j], src.rearrange("(c p) -> p c", p=P)).then_inc(sw_in, 16)
            sp.dma_start(xbv_rows[:], xbv.unsqueeze(0).broadcast_to([P, D])).then_inc(rows_in, 16)
            sp.dma_start(bo_rows[:], bo.unsqueeze(0).broadcast_to([P, D])).then_inc(rows_in, 16)
            sp.dma_start(gate_w[:], gate_W.rearrange("(c p) e -> p c e", p=P)).then_inc(gate_in, 16)
            sp.dma_start(slots.rearrange("(a b) c -> a (b c)", a=P), slots_init.rearrange("(a b) c -> a (b c)", a=P)).then_inc(slots_empty, 16)
            load(Group(0, 1))
            sp.wait_ge(spare_set, 1)
            sp.dma_start(out[N:N + P], exp_scaled[:, 0]).then_inc(spare_stored, 16)
            sp.dma_start(normed_rows[N:N + P], exp_scaled[:, 0]).then_inc(spare_stored, 16)

            def slot(a, b, c, following):
                if c is not None:
                    sp.wait_ge(s["xn3_ready"], c.count())
                    sp.dma_start(normed_rows[bass.ds(c.index() * P, P)], xn3[:, c.p]).then_inc(rows_stored[c.p], 16)
                    sp.wait_ge(s["x3_ready"], c.count())
                    sp.dma_start(out[bass.ds(c.index() * P, P)], x3[:, c.p]).then_inc(out_stored[c.p], 16)
                if a is not None and not (isinstance(a.i, int) and a.index() + 2 >= G):
                    load(Group(a.i, a.c + 2))
                if a is not None and isinstance(a.i, int) and a.index() == 0:
                    for k in range(DC):
                        sp.dma_start(w1[:, :, k], W1[:, k * P:(k + 1) * P].rearrange("e p n -> p e n")).then_inc(w1_in, 16)
                    for src, dst in ((b1, b1_rows), (b2, b2_rows)):
                        sp.dma_start(dst[:].rearrange("p e n -> p (e n)"),
                                     src.rearrange("e n -> (e n)").unsqueeze(0).broadcast_to([P, E * src.shape[1]])).then_inc(b12_in, 16)
                if a is not None and isinstance(a.i, int) and a.index() == 1:
                    for k in range(HID // P):
                        sp.dma_start(w2[:, :, k], W2[:, k * P:(k + 1) * P].rearrange("e p n -> p e n")).then_inc(w2_in, 16)
            pipeline(sp, slot)

            for sm in scattered:
                sp.wait_ge(sm, 16 * TOP * (G // 2))
            sp.wait_ge(s["table_ready"], 1)

            def load_ids(t):
                first = sp.value_load(table[0:1, 1, bass.ds(t.index(), 1)], min_val=0, max_val=SLOTS - P)
                sp.dma_start(ids[:, t.slot], slots[bass.ds(first, P)]).then_inc(ids_loaded[t.slot], 16)

            for n in range(LOOK):
                load_ids(Tile(0, n))

            with sp.Fori(0, (TABLE - LOOK) // LOOK) as i:
                for c in range(LOOK):
                    t = Tile(i, c)
                    sp.wait_ge(added, t.count() * 16)
                    load_ids(t.ahead(LOOK))
            sp.wait_ge(ids_loaded[(TABLE - 1) % LOOK], 16 * (TABLE // LOOK))
            sp.wait_ge(added, 16 * TILES)

        @block.gpsimd
        def _(pool):
            nc.gpsimd.memset(eps[:], LN_EPS)
            nc.gpsimd.memset(power[:], -0.5).then_inc(power_set, 1)
            pool.wait_ge(power_set, 1)
            nc.gpsimd.memset(exp_scaled[:, 0], 0.0).then_inc(spare_set, 1)
            nc.gpsimd.memset(ones[:], 1.0)
            nc.gpsimd.memset(routed_before[:], 0.0)
            pool.wait_ge(consts_in, 16)
            nc.gpsimd.tensor_copy(earlier[:], cst[:, C_EARLIER:C_EARLIER + P]).then_inc(tri_ready, 1)

            def rstd_of(g, n):
                pool.wait_ge(s[f"mv{n}"], g.count())
                nc.gpsimd.tensor_tensor(var_eps[:, n - 1], mean_var[:, n - 1, 1:2], eps[:], ALU.add).then_inc(s[f"eps{n}"], 1)
                pool.wait_ge(s[f"eps{n}"], g.count())
                nc.gpsimd.tensor_tensor(rstd[:, n - 1], var_eps[:, n - 1], power[:], ALU.pow).then_inc(s[f"rstd{n}"], 1)

            def residual1(g):
                pool.wait_ge(x_loaded[g.p], g.visits() * 16)
                nc.gpsimd.tensor_tensor(x_bv[:, g.p], x_in[:, g.p], xbv_rows[:], ALU.add).then_inc(s["x_bv_ready"], 1)

            pool.wait_ge(rows_in, 32)
            rstd_of(Group(0, 0), 1)
            residual1(Group(0, 0))

            def slot(a, b, c, following):
                if b is not None:
                    pool.wait_ge(s["kT_ready"], b.count())
                    nc.gpsimd.tensor_tensor(
                        k_heads[:, 1].rearrange("p b (h k) -> p b h k", h=HC),
                        kT[:, 1].rearrange("p (b k) -> p b k", b=GB).unsqueeze(2).broadcast_to([P, GB, HC, T]),
                        head_mask.unsqueeze(1).unsqueeze(3).broadcast_to([P, GB, HC, T]), ALU.mult).then_inc(s["k_heads1"], 1)
                if following is not None:
                    rstd_of(following, 1)
                    residual1(following)
                if b is not None:
                    pool.wait_ge(s["att_max_ready"], b.count())
                    nc.gpsimd.tensor_tensor(att_sub[:], att[:], att_max[:].unsqueeze(2).broadcast_to([P, H, T]),
                                            ALU.subtract).then_inc(s["att_sub_ready"], 1)
                if a is not None:
                    rstd_of(a, 2)
                    nc.gpsimd.tensor_tensor(x1_bo[:, a.p], x1[:, a.p], bo_rows[:], ALU.add).then_inc(s["x1_bo_ready"], 1)
                if b is not None:
                    rstd_of(b, 3)
                if b is not None:
                    pool.wait_ge(s["xn3_ready"], b.count())
                    if not (isinstance(b.i, int) and b.index() < 2):
                        pool.wait_ge(out_stored[b.p], b.visits() * 16 - 16)
                    nc.gpsimd.tensor_tensor(x3[:, b.p], x2[:, b.p], xn3[:, b.p], ALU.add).then_inc(s["x3_ready"], 1)
                if c is not None:
                    if isinstance(c.i, int) and c.index() == 0:
                        pool.wait_ge(slots_empty, 16)
                    pool.wait_ge(s["row_ready"], c.count())
                    wait_apart(pool, s["place_slot_ready"], c.count(), pool_passed)
                    for k in range(TOP):
                        nc.gpsimd.indirect_dma_start(
                            out=slots, out_offset=bass.IndirectOffsetOnAxis(ap=place_slot[:, c.p, k:k + 1], axis=0),
                            in_=slot_row[:, c.p, k], in_offset=None).then_inc(scattered[c.p], 16)
            pipeline(pool, slot)

            for sm in rows_stored + out_stored:
                pool.wait_ge(sm, 16 * (G // 2))
            pool.wait_ge(spare_stored, 32)

            def gather(t):
                wait_apart(pool, ids_loaded[t.slot], t.slot_visits() * 16, pool_passed)
                nc.gpsimd.indirect_dma_start(
                    out=xg[:, t.pair], out_offset=None, in_=normed_rows,
                    in_offset=bass.IndirectOffsetOnAxis(ap=ids[:, t.slot, 0:1], axis=0)).then_inc(gathered[t.pair], 16)

            gather(Tile(0, 0))
            gather(Tile(0, 1))

            def step(t, following, after):
                if after is not None:
                    pool.wait_ge(s["xgT_ps"], t.count())
                    gather(after)
                pool.wait_ge(s["exp_scaled_ready"], t.count())
                wait_apart(pool, added, t.count(1) * 16, pool_passed)
                nc.gpsimd.indirect_dma_start(
                    out=out, out_offset=bass.IndirectOffsetOnAxis(ap=ids[:, t.slot, 0:1], axis=0),
                    in_=exp_scaled[:, t.pair], in_offset=None, compute_op=ALU.add).then_inc(added, 16)
            tiles(pool, step)

        @block.scalar
        def _(act):
            act.wait_ge(fused, 1)
            nc.scalar.copy(wqk[:], xa[0][:].rearrange("p (c d) -> p c d", c=DC)).then_inc(fused_copied, 1)

            def copy_out(dst, bank, cols, ready, done, g):
                act.wait_ge(s[ready], g.count())
                nc.scalar.copy(dst, bank[:, 0:cols]).then_inc(s[done], 1)

            def with_bias(dst, bank, bias, ready, done, g):
                act.wait_ge(s[ready], g.count())
                for c in range(DC):
                    last = nc.scalar.activation(dst[:, c], bank[:, c * P:(c + 1) * P], ACT.Identity, bias=bias[:, c:c + 1])
                last.then_inc(s[done], 1)

            def turned_even(g, b):
                act.wait_ge(s["turned"], g.count(1) * 5 + (b + 1))
                nc.scalar.copy(ctxT[:, g.p, b, :, 0:S - 1], turn[0][:].rearrange("p (c k) -> p c k", c=DC)).then_inc(s["ctxT_a"], 1)

            def turned_last(g):
                act.wait_ge(s["turned"], g.count(1) * 5 + 5)
                nc.scalar.copy(ctxT[:, g.p, :, :, S - 1],
                               turn[0][:, 0:2 * P].rearrange("p (c b t) -> p b c t", c=DC, b=GB)[:, :, :, 0]).then_inc(s["ctxT_a"], 1)

            g0 = Group(0, 0)
            turned_even(g0, 0)
            turned_even(g0, 2)
            turned_last(g0)

            def slot(a, b, c, following):
                if a is not None:
                    copy_out(xn1T[:].rearrange("p c t -> p (c t)"), xa[0], D, "xn1T_ps", "xn1T_ready", a)
                if b is not None:
                    copy_out(xn2T[:].rearrange("p c t -> p (c t)"), sa[0], D, "xn2T_ps", "xn2T_ready", b)
                if c is not None:
                    copy_out(xn3T[:].rearrange("p c t -> p (c t)"), gp, D, "xn3T_ps", "xn3T_ready", c)
                if a is not None:
                    if isinstance(a.i, int) and a.index() == 0:
                        act.wait_ge(fused_sum, 1)
                    with_bias(qkT, xa[1], bqk, "qkT_ps", "qkT_ready", a)
                if b is not None:
                    act.wait_ge(s["v_ps"], b.count())
                    for k in range(DC):
                        last = nc.scalar.activation(
                            vT[:, k], sa[1][:, k * P:(k + 1) * P].rearrange("p (b t) -> p b t", b=GB).unsqueeze(2).broadcast_to([P, GB, HQ, T]),
                            ACT.Identity, bias=b_cols[:, 2, k:k + 1])
                    last.then_inc(s["vT_ready"], 1)
                if a is not None:
                    act.wait_ge(s["ebias_ready"], a.count())
                    nc.scalar.activation(probs[:], xa[0][:, 0:S], ACT.Exp, bias=ebias[:], scale=SCALE,
                                         accum_out=ssum[:, 0:1]).then_inc(s["probs_ready"], 1)
                if following is not None:
                    turned_even(following, 0)
                if a is not None:
                    copy_out(probsT[:].rearrange("p c t -> p (c t)"), xa[1], D, "probsT_ps", "probsT_ready", a)
                if c is not None:
                    act.wait_ge(s["logit_bias_ready"], c.count())
                    nc.scalar.activation(gate_exp[:], gp[:, 3 * P:3 * P + E], ACT.Exp, bias=logit_bias[:],
                                         accum_out=gate_sum[:, 0:1]).then_inc(s["gate_exp_ready"], 1)
                if b is not None:
                    act.wait_ge(s["att_sub_ready"], b.count())
                    nc.scalar.activation(att_exp[:], att_sub[:], ACT.Exp, scale=ATT_SCALE).then_inc(s["att_exp_ready"], 1)
                if following is not None:
                    turned_even(following, 2)
                    turned_last(following)
                if b is not None:
                    copy_out(attT[:].rearrange("p c t -> p (c t)"), sa[0], 512, "attT_ps", "attT_ready", b)
                if a is not None:
                    copy_out(mixT[:].rearrange("p c t -> p (c t)"), xa[0], D, "mixT_ps", "mixT_ready", a)
                if b is not None:
                    copy_out(yT[:].rearrange("p c t -> p (c t)"), sa[0], D, "yT_ps", "yT_ready", b)
            pipeline(act, slot)

            def step(t, following, after):
                act.wait_ge(s["hidT_ps"], t.count())
                nc.scalar.activation(hidT[:, t.pair], sa[t.pair][:].rearrange("p (c t) -> p c t", c=HID // P), ACT.Relu).then_inc(s["hidT_ready"], 1)
                if after is not None:
                    expert_xT(after)

            def expert_xT(t):
                act.wait_ge(s["xgT_ps"], t.count())
                nc.scalar.copy(xgT[:, t.pair], turn[t.pair][:, 0:D].rearrange("p (c t) -> p c t", c=DC)).then_inc(s["xgT_ready"], 1)

            expert_xT(Tile(0, 0))
            expert_xT(Tile(0, 1))
            tiles(act, step)

        @block.vector
        def _(dve):
            dve.wait_ge(fused, 1)
            nc.vector.tensor_copy(wqbk_rows[:], xa[1][:, 0:D]).then_inc(fused_sum, 1)
            nc.vector.tensor_copy(bqbk[:], xa[1][:, D:D + 1])
            nc.vector.tensor_copy(bqk[:], xa[1][:, D + 2:D + 2 + DC]).then_inc(fused_sum, 1)
            dve.wait_ge(fused_sum, 2)
            dve.wait_ge(consts_in, 16)
            dve.wait_ge(sw_in, 16 * 8)

            def norm(g, n, src):
                nc.vector.bn_stats(stats[:, n - 1], src).then_inc(s[f"stats{n}"], 1)
                wait_apart(dve, s[f"stats{n}"], g.count(), dve_passed)
                nc.vector.bn_aggr(mean_var[:, n - 1], stats[:, n - 1]).then_inc(s[f"mv{n}"], 1)

            def normed(g, n, src, dst, done):
                dve.wait_ge(s[f"rstd{n}"], g.count())
                nc.vector.tensor_scalar(dst, src, mean_var[:, n - 1, 0:1], rstd[:, n - 1], ALU.subtract, ALU.mult).then_inc(s[done], 1)

            def norm1(g):
                dve.wait_ge(x_loaded[g.p], g.visits() * 16)
                norm(g, 1, x_in[:, g.p])

            def normed1(g):
                normed(g, 1, x_in[:, g.p], xn1[:, g.p], "xn1")
                dve.wait_ge(s["xn1"], g.count())
                nc.vector.tensor_tensor_reduce(out=junk[:], in0=xn1[:, g.p], in1=wqbk_rows[:], scale=1.0, scalar=0.0,
                                               op0=ALU.mult, op1=ALU.add, accum_out=qbk[:, g.p, 0:1]).then_inc(s["qbk0"], 1)
                dve.wait_ge(s["qbk0"], g.count())
                nc.vector.tensor_tensor(qbk[:, g.p, 1:2], qbk[:, g.p, 0:1], bqbk[:], ALU.add).then_inc(s["qbk_ready"], 1)

            def turned_odd(g, b):
                dve.wait_ge(s["turned"], g.count(1) * 5 + (b + 1))
                nc.vector.tensor_copy(ctxT[:, g.p, b, :, 0:S - 1], turn[1][:].rearrange("p (c k) -> p c k", c=DC)).then_inc(s["ctxT_b"], 1)

            g0 = Group(0, 0)
            norm1(g0)
            normed1(g0)
            turned_odd(g0, 1)
            turned_odd(g0, 3)

            def rotated(g, bank, at, j, dst, done):
                for c in range(DC):
                    last = nc.vector.scalar_tensor_tensor(
                        out=dst[:, c].rearrange("p (b t) -> p b t", b=GB),
                        in0=bank[:, at + c * P:at + (c + 1) * P].rearrange("p (b t) -> p b t", b=GB),
                        scalar=b_cols[:, j, c:c + 1], in1=rope.unsqueeze(1).broadcast_to([P, GB, T]),
                        op0=ALU.add, op1=ALU.mult)
                last.then_inc(s[done], 1)

            def gate_softmax(c):
                dve.wait_ge(s["gate_exp_ready"], c.count())
                nc.vector.reciprocal(gate_sum[:, 1:2], gate_sum[:, 0:1]).then_inc(s["gate_recip"], 1)
                dve.wait_ge(s["gate_recip"], c.count())
                nc.vector.tensor_scalar(gates[:], gate_exp[:], gate_sum[:, 1:2], None, ALU.mult).then_inc(s["gates_ready"], 1)
                wait_apart(dve, s["gates_ready"], c.count(), dve_passed)
                nc.vector.max(top_gates[:], gates[:]).then_inc(s["top_gates_ready"], 1)
                wait_apart(dve, s["top_gates_ready"], c.count(), dve_passed)
                nc.vector.max_index(top_experts[:], top_gates[:], gates[:]).then_inc(s["top_index"], 1)
                nc.vector.tensor_scalar(top_sum[:, 0:1], top_gates[:, 0:1], top_gates[:, 1:2], 1e-8, ALU.add, ALU.add).then_inc(s["top_sum_ready"], 1)
                dve.wait_ge(s["top_index"], c.count())
                nc.vector.tensor_copy(top_expert[:], top_experts[:, 0:TOP]).then_inc(s["top_expert_ready"], 1)
                dve.wait_ge(s["top_sum_ready"], c.count())
                nc.vector.reciprocal(top_sum[:, 1:2], top_sum[:, 0:1]).then_inc(s["top_recip"], 1)
                dve.wait_ge(s["top_expert_ready"], c.count())
                for k in range(TOP):
                    nc.vector.tensor_scalar(chosen[:, k], cst[:, C_EXPERT:C_EXPERT + E], top_expert[:, k:k + 1], None,
                                            ALU.is_equal).then_inc(s["chosen_ready"], 1)
                dve.wait_ge(s["chosen_ready"], c.count() * TOP)
                nc.vector.tensor_tensor(routed[:], chosen[:, 0], chosen[:, 1], ALU.add).then_inc(s["routed_ready"], 1)
                if not (isinstance(c.i, int) and c.index() < 2):
                    dve.wait_ge(scattered[c.p], c.visits() * (16 * TOP) - 16 * TOP)
                dve.wait_ge(s["top_recip"], c.count())
                nc.vector.tensor_scalar(slot_row[:, c.p, :, 1].bitcast(F32), top_gates[:, 0:TOP], top_sum[:, 1:2], None, ALU.mult)
                nc.vector.tensor_copy(slot_row[:, c.p, :, 0], token[:, 0:1].broadcast_to([P, TOP])).then_inc(s["row_ready"], 1)
                dve.wait_ge(s["row_ready"], c.count())
                nc.vector.tensor_scalar(token[:, 0:1], token[:, 0:1], float(P), None, ALU.add).then_inc(s["token_ready"], 1)
                dve.wait_ge(s["routed_ready"], c.count())
                nc.vector.tensor_tensor(routed_before[:, 1 - c.p], routed_before[:, c.p], routed[:], ALU.add).then_inc(s["routed_sum"], 1)

            def gate_places(c):
                dve.wait_ge(s["rank_ps"], c.count())
                nc.vector.tensor_tensor(places[:], gp[:, 3 * P + E:3 * P + 2 * E], cst[:, C_FIRST:C_FIRST + E], ALU.add).then_inc(s["places_ready"], 1)
                dve.wait_ge(s["places_ready"], c.count())
                for k in range(TOP):
                    nc.vector.tensor_tensor_reduce(out=junk[:, k * E:(k + 1) * E], in0=chosen[:, k], in1=places[:], scale=1.0, scalar=0.0,
                                                   op0=ALU.mult, op1=ALU.add, accum_out=place[:, k:k + 1]).then_inc(s["place_ready"], 1)
                dve.wait_ge(s["place_ready"], c.count() * TOP)
                nc.vector.tensor_copy(place_slot[:, c.p], place[:]).then_inc(s["place_slot_ready"], 1)

            nc.vector.tensor_copy(token[:, 0:1], cst[:, C_TOKEN:C_TOKEN + 1]).then_inc(s["token_ready"], 1)

            def slot(a, b, c, following):
                if b is not None:
                    dve.wait_ge(s["qk_ps"], b.count())
                    rotated(b, sa[0], D, 1, kT, "kT_ready")
                    rotated(b, sa[0], 0, 0, qT, "qT_ready")
                    dve.wait_ge(s["kT_ready"], b.count())
                    nc.vector.tensor_tensor(
                        k_heads[:, 0].rearrange("p b (h k) -> p b h k", h=HC),
                        kT[:, 0].rearrange("p (b k) -> p b k", b=GB).unsqueeze(2).broadcast_to([P, GB, HC, T]),
                        head_mask.unsqueeze(1).unsqueeze(3).broadcast_to([P, GB, HC, T]), ALU.mult).then_inc(s["k_heads0"], 1)
                if c is not None:
                    dve.wait_ge(s["logitsT_ps"], c.count())
                    nc.vector.tensor_copy(logitsT[:], gp[0:E, 2 * P:3 * P]).then_inc(s["logitsT_ready"], 1)
                if a is not None:
                    dve.wait_ge(s["scores"], a.count())
                    nc.vector.tensor_reduce(smax[:, 0:1], xa[0][:, 0:S], AX.X, ALU.max).then_inc(s["smax0"], 1)
                    dve.wait_ge(s["smax0"], a.count())
                    nc.vector.tensor_tensor(smax[:, 1:2], smax[:, 0:1], qbk[:, a.p, 1:2], ALU.add).then_inc(s["smax1"], 1)
                    dve.wait_ge(s["smax1"], a.count())
                    nc.vector.tensor_scalar(ebias[:], smax[:, 1:2], qbk[:, a.p, 1:2], -SCALE, ALU.subtract, ALU.mult).then_inc(s["ebias_ready"], 1)
                if b is not None:
                    for n in range(2):
                        dve.wait_ge(s["vrep_ps"], b.count(1) * 2 + (n + 1))
                        last = nc.vector.tensor_tensor(
                            v_heads[:, 2 * n:2 * n + 2].rearrange("p b (c h w) -> p (b c) h w", h=HQ, w=DH),
                            sa[1 + n][:].rearrange("p (c h w) -> p c h w", h=HQ, w=DH),
                            vhead_mask.unsqueeze(1).unsqueeze(3).broadcast_to([P, 2 * H // HQ, HQ, DH]), ALU.mult)
                    last.then_inc(s["v_heads_ready"], 1)
                    dve.wait_ge(s["att_ps"], b.count())
                    nc.vector.tensor_tensor(att[:], as_heads(sa[0][:], H, T), causal.unsqueeze(1).broadcast_to([P, H, T]),
                                            ALU.add).then_inc(s["att_masked"], 1)
                    dve.wait_ge(s["att_masked"], b.count())
                    nc.vector.tensor_reduce(att_max[:], att[:], AX.X, ALU.max).then_inc(s["att_max_ready"], 1)
                if c is not None:
                    dve.wait_ge(s["logits_ps"], c.count())
                    nc.vector.tensor_reduce(logit_bias[:], gp[:, 3 * P:3 * P + E], AX.X, ALU.max, negate=True).then_inc(s["logit_bias_ready"], 1)
                if a is not None:
                    dve.wait_ge(s["probs_ready"], a.count())
                    nc.vector.reciprocal(ssum[:, 1:2], ssum[:, 0:1]).then_inc(s["recip1"], 1)
                if following is not None:
                    turned_odd(following, 1)
                    norm1(following)
                if a is not None:
                    dve.wait_ge(s["mix_ps"], a.count())
                    nc.vector.scalar_tensor_tensor(out=mix[:], in0=ctx_last[:, a.p], scalar=probs[:, S - 1:S],
                                                   in1=xa[0][:, 0:D], op0=ALU.mult, op1=ALU.add).then_inc(s["mix_ready"], 1)
                if b is not None:
                    dve.wait_ge(s["att_exp_ready"], b.count())
                    nc.vector.tensor_reduce(att_sum[:, 0], att_exp[:], AX.X, ALU.add).then_inc(s["att_sum_ready"], 1)
                    dve.wait_ge(s["att_sum_ready"], b.count())
                    nc.vector.reciprocal(att_sum[:, 1], att_sum[:, 0]).then_inc(s["recip2"], 1)
                if c is not None:
                    gate_softmax(c)
                if following is not None:
                    turned_odd(following, 3)
                    normed1(following)
                if a is not None:
                    dve.wait_ge(s["xv_ps"], a.count())
                    dve.wait_ge(s["x_bv_ready"], a.count())
                    nc.vector.scalar_tensor_tensor(out=x1[:, a.p], in0=xa[1][:, 0:D], scalar=ssum[:, 1:2], in1=x_bv[:, a.p],
                                                   op0=ALU.mult, op1=ALU.add).then_inc(s["x1_ready"], 1)
                    dve.wait_ge(s["x1_ready"], a.count())
                    norm(a, 2, x1[:, a.p])
                if b is not None:
                    dve.wait_ge(s["y_ps"], b.count())
                    dve.wait_ge(s["recip2"], b.count())
                    nc.vector.tensor_tensor(as_heads(y[:], H, DH), as_heads(sa[1][:, 0:D], H, DH),
                                            att_sum[:, 1].unsqueeze(2).broadcast_to([P, H, DH]), ALU.mult).then_inc(s["y_ready"], 1)
                if a is not None:
                    normed(a, 2, x1[:, a.p], xn2[:], "xn2_ready")
                if b is not None:
                    dve.wait_ge(s["o_ps"], b.count())
                    dve.wait_ge(s["x1_bo_ready"], b.count())
                    nc.vector.tensor_tensor(x2[:, b.p], sa[1][:, 0:D], x1_bo[:, b.p], ALU.add).then_inc(s["x2_ready"], 1)
                    dve.wait_ge(s["x2_ready"], b.count())
                    norm(b, 3, x2[:, b.p])
                    if not (isinstance(b.i, int) and b.index() < 2):
                        dve.wait_ge(rows_stored[b.p], b.visits() * 16 - 16)
                    normed(b, 3, x2[:, b.p], xn3[:, b.p], "xn3_ready")
                if c is not None:
                    gate_places(c)
            pipeline(dve, slot)

            dve.wait_ge(s["counts_ps"], 1)
            nc.vector.tensor_copy(counts[:], gp[0:1, 0:E]).then_inc(s["counts_ready"], 1)
            dve.wait_ge(s["counts_ready"], 1)
            nc.vector.tensor_tensor(started[:], counts[:].unsqueeze(2).broadcast_to([1, E, N // P]),
                                    cst[0:1, C_FULL:C_FULL + N // P].unsqueeze(1).broadcast_to([1, E, N // P]),
                                    ALU.is_gt).then_inc(s["started_ready"], 1)
            dve.wait_ge(s["started_ready"], 1)
            nc.vector.tensor_reduce(tile_count[:], started[:], AX.X, ALU.add).then_inc(s["tile_count_ready"], 1)
            dve.wait_ge(s["tile_count_ready"], 1)
            nc.vector.tensor_copy(tile_end[:], tile_count[:]).then_inc(s["tile_end_ready"], 1)
            for e in range(1, E):
                dve.wait_ge(s["tile_end_ready"], e)
                nc.vector.tensor_tensor(tile_end[:, e:e + 1], tile_end[:, e:e + 1], tile_end[:, e - 1:e], ALU.add).then_inc(s["tile_end_ready"], 1)
            nc.vector.tensor_scalar(row_skip[:], tile_count[:], -float(P), float(N), ALU.mult, ALU.add).then_inc(s["row_skip_ready"], 1)
            dve.wait_ge(s["tile_end_ready"], E)
            tile_number = cst[0:1, C_TILE:C_TILE + TABLE]
            nc.vector.tensor_tensor(passed[:], tile_number.unsqueeze(2).broadcast_to([1, TABLE, E]),
                                    tile_end[:].unsqueeze(1).broadcast_to([1, TABLE, E]), ALU.is_ge).then_inc(s["passed_ready"], 1)
            dve.wait_ge(s["passed_ready"], 1)
            dve.wait_ge(s["row_skip_ready"], 1)
            nc.vector.tensor_tensor(passed_rows[:], passed[:], row_skip[:].unsqueeze(1).broadcast_to([1, TABLE, E]),
                                    ALU.mult).then_inc(s["passed_rows_ready"], 1)
            nc.vector.tensor_reduce(tile_expert[:, 0], passed[:], AX.X, ALU.add).then_inc(s["tile_sums"], 1)
            dve.wait_ge(s["passed_rows_ready"], 1)
            nc.vector.tensor_reduce(tile_row[:, 0], passed_rows[:], AX.X, ALU.add).then_inc(s["tile_sums"], 1)
            dve.wait_ge(s["tile_sums"], 2)
            nc.vector.tensor_scalar(table[:, 0], tile_expert[:, 0], float(E - 1), None, ALU.min)
            nc.vector.scalar_tensor_tensor(out=table[:, 1], in0=tile_number, scalar=float(P), in1=tile_row[:, 0],
                                           op0=ALU.mult, op1=ALU.add).then_inc(s["table_ready"], 1)
            dve.wait_ge(s["table_ready"], 1)
            dve.wait_ge(b12_in, 32)

            def expert_of(t):
                return dve.value_load(table[0:1, 0, bass.ds(t.index(), 1)], min_val=0, max_val=E - 1)

            def hidden(t):
                e = expert_of(t)
                dve.wait_ge(s["hid_ps"], t.count())
                nc.vector.tensor_tensor(hid[:, t.pair].unsqueeze(1), xa[t.pair][:].unsqueeze(1), b1_rows[:, bass.ds(e, 1)], ALU.add).then_inc(s["hid_ready"], 1)

            def step(t, following, after):
                if following is not None:
                    hidden(following)
                e = expert_of(t)
                dve.wait_ge(s["exp_ps"], t.count())
                nc.vector.tensor_tensor(exp_out[:, t.pair].unsqueeze(1), exp_bank[t.pair][:, 0:D].unsqueeze(1), b2_rows[:, bass.ds(e, 1)], ALU.add).then_inc(s["exp_out_ready"], 1)
                dve.wait_ge(s["exp_out_ready"], t.count())
                wait(dve, added, t.count(2) * 16)
                nc.vector.tensor_scalar(exp_scaled[:, t.pair], exp_out[:, t.pair], ids[:, t.slot, 1:2].bitcast(F32), None, ALU.mult).then_inc(s["exp_scaled_ready"], 1)

            hidden(Tile(0, 0))
            tiles(dve, step)

        @block.tensor
        def _(pe):
            mm = nc.tensor.matmul

            def transposes(bank, src, n=DC):
                for c in range(n):
                    last = nc.tensor.transpose(bank[:, c * P:(c + 1) * P], src[:, c * P:(c + 1) * P], ident)
                return last

            pe.wait_ge(xw_in, 64)
            for m in range(DC):
                for k in range(DC):
                    mm(xa[0][:, m * D:(m + 1) * D], raw_wq[:, k, m * P:(m + 1) * P], raw_wk[:, k], start=(k == 0), stop=(k == DC - 1))
            for k in range(DC):
                bk_all = raw_b[:, 1, k:k + 1].broadcast_to([P, P])
                mm(xa[1][:, 0:D], bk_all, raw_wq[:, k], start=(k == 0), stop=(k == DC - 1))
            for k in range(DC):
                bk_all = raw_b[:, 1, k:k + 1].broadcast_to([P, P])
                mm(xa[1][:, D:D + 1], bk_all, raw_b[:, 0, k:k + 1], start=(k == 0), stop=(k == DC - 1))
            for m in range(DC):
                for k in range(DC):
                    last = mm(xa[1][:, D + 2 + m:D + 3 + m], raw_wk[:, k, m * P:(m + 1) * P], raw_b[:, 0, k:k + 1],
                              start=(k == 0), stop=(k == DC - 1))
            last.then_inc(fused, 1)
            pe.wait_ge(consts_in, 16)

            def turn_context(g, batches):
                for b in batches:
                    if b == 0:
                        pe.wait_ge(ctx_loaded[g.p], g.visits() * 32)
                        wait(pe, s["ctxT_a"], g.count(1) * 3)
                    elif b == 1:
                        wait(pe, s["ctxT_b"], g.count(1) * 2)
                    elif b == 2:
                        pe.wait_ge(s["ctxT_a"], g.count(1) * 3 + 1)
                    else:
                        pe.wait_ge(s["ctxT_b"], g.count(1) * 2 + 1)
                    for c in range(DC):
                        for k in range(SK):
                            last = nc.tensor.transpose(turn[b % 2][:, (c * SK + k) * P:(c * SK + k + 1) * P],
                                                       ctx_in[:, g.p, b, k, c * P:(c + 1) * P], ident)
                    last.then_inc(s["turned"], 1)

            def turn_last(g):
                pe.wait_ge(s["ctxT_a"], g.count(1) * 3 + 2)
                transposes(turn[0], ctx_last[:, g.p]).then_inc(s["turned"], 1)

            turn_context(Group(0, 0), range(GB))
            turn_last(Group(0, 0))
            pe.wait_ge(fused_copied, 1)
            pe.wait_ge(fused_sum, 2)

            def project(bank, at, w, src):
                for m in range(DC):
                    for k in range(DC):
                        last = mm(bank[:, at + m * P:at + (m + 1) * P], w[:, k, m * P:(m + 1) * P], src[:, k],
                                  start=(k == 0), stop=(k == DC - 1))
                return last

            def slot(a, b, c, following):
                if a is not None:
                    pe.wait_ge(s["xn1"], a.count())
                    transposes(xa[0], xn1[:, a.p]).then_inc(s["xn1T_ps"], 1)
                if b is not None:
                    pe.wait_ge(s["xn2_ready"], b.count())
                    transposes(sa[0], xn2[:]).then_inc(s["xn2T_ps"], 1)
                if a is not None:
                    pe.wait_ge(s["xn1T_ready"], a.count())
                    wait(pe, s["x1_ready"], a.count(1))
                    project(xa[1], 0, wqk, xn1T).then_inc(s["qkT_ps"], 1)
                if c is not None:
                    pe.wait_ge(s["xn3_ready"], c.count())
                    wait(pe, s["places_ready"], c.count(1))
                    transposes(gp, xn3[:, c.p]).then_inc(s["xn3T_ps"], 1)
                if b is not None:
                    if isinstance(b.i, int) and b.index() == 0:
                        pe.wait_ge(sw_in, 16 * 8)
                    pe.wait_ge(s["xn2T_ready"], b.count())
                    project(sa[0], D, w_k, xn2T)
                    project(sa[0], 0, w_q, xn2T).then_inc(s["qk_ps"], 1)
                    wait(pe, s["x2_ready"], b.count(1))
                    project(sa[1], 0, w_v, xn2T).then_inc(s["v_ps"], 1)
                if c is not None:
                    if isinstance(c.i, int) and c.index() == 0:
                        pe.wait_ge(gate_in, 16)
                        pe.wait_ge(tri_ready, 1)
                    pe.wait_ge(s["xn3T_ready"], c.count())
                    for k in range(DC):
                        last = mm(gp[0:E, 2 * P:3 * P], gate_w[:, k], xn3T[:, k], start=(k == 0), stop=(k == DC - 1))
                    last.then_inc(s["logitsT_ps"], 1)
                if a is not None:
                    pe.wait_ge(s["qkT_ready"], a.count())
                    pe.wait_ge(s["ctxT_a"], a.count() * 3)
                    pe.wait_ge(s["ctxT_b"], a.count() * 2)
                    for k in range(DC):
                        for j in range(GB):
                            last = mm(xa[0][T * j:T * j + T, 0:S], qkT[:, k, T * j:T * j + T], ctxT[:, a.p, j, k],
                                      start=(k == 0), stop=(k == DC - 1), tile_position=(0, T * j))
                    last.then_inc(s["scores"], 1)
                if b is not None:
                    pe.wait_ge(s["vT_ready"], b.count())
                    for j in range(GB):
                        for k in range(DC):
                            src = vT[:, k, j].rearrange("p r t -> p (r t)")
                            last = nc.tensor.transpose(sa[1 + j // 2][:, (j % 2) * D + k * P:(j % 2) * D + (k + 1) * P], src, ident)
                        if j % 2:
                            last.then_inc(s["vrep_ps"], 1)
                    pe.wait_ge(s["qT_ready"], b.count())
                    pe.wait_ge(s["k_heads0"], b.count())
                    pe.wait_ge(s["k_heads1"], b.count())
                    for k in range(DC):
                        for j in range(GB):
                            last = mm(sa[0][T * j:T * j + T, k * HC * T:(k + 1) * HC * T], qT[:, k, T * j:T * j + T],
                                      k_heads[:, k, j], start=True, stop=True, tile_position=(0, T * j))
                    last.then_inc(s["att_ps"], 1)
                if c is not None:
                    wait_apart(pe, s["logitsT_ready"], c.count(), pe_passed)
                    nc.tensor.transpose(gp[:, 3 * P:3 * P + E], logitsT[:], ident[0:E, 0:E]).then_inc(s["logits_ps"], 1)
                if following is not None:
                    turn_context(following, (0, 1))
                if a is not None:
                    pe.wait_ge(s["probs_ready"], a.count())
                    transposes(xa[1], probs[:], SK).then_inc(s["probsT_ps"], 1)
                if following is not None:
                    turn_context(following, (2,))
                if a is not None:
                    pe.wait_ge(s["probsT_ready"], a.count())
                    for k in range(SK):
                        for j in range(GB):
                            last = mm(xa[0][T * j:T * j + T, 0:D], probsT[:, k, T * j:T * j + T], ctx_in[:, a.p, j, k],
                                      start=(k == 0), stop=(k == SK - 1), tile_position=(0, T * j))
                    last.then_inc(s["mix_ps"], 1)
                if following is not None:
                    turn_context(following, (3,))
                    turn_last(following)
                if b is not None:
                    pe.wait_ge(s["att_exp_ready"], b.count())
                    transposes(sa[0], att_exp[:].rearrange("p h k -> p (h k)"), H // HQ).then_inc(s["attT_ps"], 1)
                if a is not None:
                    pe.wait_ge(s["mix_ready"], a.count())
                    transposes(xa[0], mix[:]).then_inc(s["mixT_ps"], 1)
                if b is not None:
                    pe.wait_ge(s["attT_ready"], b.count())
                    pe.wait_ge(s["v_heads_ready"], b.count())
                    for c4 in range(H // HQ):
                        for j in range(GB):
                            w = HQ * DH
                            last = mm(sa[1][T * j:T * j + T, c4 * w:(c4 + 1) * w], attT[:, c4, T * j:T * j + T],
                                      v_heads[:, j, c4 * w:(c4 + 1) * w], start=True, stop=True, tile_position=(0, T * j))
                    last.then_inc(s["y_ps"], 1)
                if a is not None:
                    pe.wait_ge(s["mixT_ready"], a.count())
                    if isinstance(a.i, int) and a.index() == 0:
                        pe.wait_ge(sw_in, 16 * 8)
                    for k in range(DC):
                        last = mm(xa[1][:, 0:D], mixT[:, k], w_xv[:, k], start=(k == 0), stop=(k == DC - 1))
                    last.then_inc(s["xv_ps"], 1)
                if b is not None:
                    pe.wait_ge(s["y_ready"], b.count())
                    transposes(sa[0], y[:]).then_inc(s["yT_ps"], 1)
                    pe.wait_ge(s["yT_ready"], b.count())
                    for k in range(DC):
                        last = mm(sa[1][:, 0:D], yT[:, k], w_o[:, k], start=(k == 0), stop=(k == DC - 1))
                    last.then_inc(s["o_ps"], 1)
                if c is not None:
                    pe.wait_ge(s["routed_ready"], c.count())
                    wait(pe, s["routed_sum"], c.count(1))
                    rank = gp[:, 3 * P + E:3 * P + 2 * E]
                    mm(rank, earlier[:], routed[:], start=True, stop=False)
                    mm(rank, ones[:], routed_before[:, c.p], start=False, stop=True).then_inc(s["rank_ps"], 1)
            pipeline(pe, slot)

            pe.wait_ge(s["routed_sum"], G)
            pe.wait_ge(s["places_ready"], G)
            mm(gp[0:1, 0:E], ones[:, 0:1], routed_before[:, G % 2], start=True, stop=True).then_inc(s["counts_ps"], 1)
            for sm, n in ((w1_in, DC), (w2_in, HID // P)):
                pe.wait_ge(sm, n * 16)
            pe.wait_ge(s["table_ready"], 1)

            def expert_of(t):
                return pe.value_load(table[0:1, 0, bass.ds(t.index(), 1)], min_val=0, max_val=E - 1)

            def turn_rows(t):
                pe.wait_ge(gathered[t.pair], t.pair_visits() * 16)
                transposes(turn[t.pair], xg[:, t.pair]).then_inc(s["xgT_ps"], 1)

            def up(t):
                e = expert_of(t)
                pe.wait_ge(s["xgT_ready"], t.count())
                for k in range(DC):
                    last = mm(xa[t.pair][:].unsqueeze(1), xgT[:, t.pair, k], w1[:, bass.ds(e, 1), k], start=(k == 0), stop=(k == DC - 1))
                last.then_inc(s["hid_ps"], 1)

            def step(t, following, after):
                pe.wait_ge(s["hid_ready"], t.count())
                transposes(sa[t.pair], hid[:, t.pair], HID // P).then_inc(s["hidT_ps"], 1)
                if following is not None:
                    up(following)
                e = expert_of(t)
                pe.wait_ge(s["hidT_ready"], t.count())
                for k in range(HID // P):
                    last = mm(exp_bank[t.pair][:, 0:D].unsqueeze(1), hidT[:, t.pair, k], w2[:, bass.ds(e, 1), k], start=(k == 0), stop=(k == HID // P - 1))
                last.then_inc(s["exp_ps"], 1)
                if after is not None:
                    turn_rows(after)

            turn_rows(Tile(0, 0))
            turn_rows(Tile(0, 1))
            up(Tile(0, 0))
            tiles(pe, step)


def kernel(x, ctx_1024, L0_xattn_Wq, L0_xattn_bq, L0_xattn_Wk, L0_xattn_bk, L0_xattn_Wv, L0_xattn_bv,
           L0_attn_Wq, L0_attn_bq, L0_attn_Wk, L0_attn_bk, L0_attn_Wv, L0_attn_bv, L0_attn_Wo, L0_attn_bo,
           L0_ffn_gate_W, L0_ffn_W1, L0_ffn_b1, L0_ffn_W2, L0_ffn_b2):
    from concourse import bacc
    from concourse.bass_utils import run_bass_kernel_spmd

    arrays = {
        "x": np.asarray(x).reshape(N, D), "ctx": ctx_1024,
        "consts": shape_constants(), "slots_init": empty_slots(),
        "xWq": L0_xattn_Wq, "xbq": L0_xattn_bq, "xWk": L0_xattn_Wk, "xbk": L0_xattn_bk,
        "xWvT": np.asarray(L0_xattn_Wv).T, "xbv": L0_xattn_bv,
        "WqT": np.asarray(L0_attn_Wq).T, "bq": L0_attn_bq, "WkT": np.asarray(L0_attn_Wk).T, "bk": L0_attn_bk,
        "WvT": np.asarray(L0_attn_Wv).T, "bv": L0_attn_bv, "WoT": np.asarray(L0_attn_Wo).T, "bo": L0_attn_bo,
        "gate_W": L0_ffn_gate_W, "W1": L0_ffn_W1, "b1": L0_ffn_b1, "W2": L0_ffn_W2, "b2": L0_ffn_b2,
    }
    nc = bacc.Bacc("TRN2", target_bir_lowering=False, num_devices=1)
    in_map, args = {}, []
    for name, a in arrays.items():
        a = np.ascontiguousarray(a)
        in_map[f"in_{name}"] = a
        args.append(nc.dram_tensor(f"in_{name}", a.shape, mybir.dt.from_np(a.dtype), kind="ExternalInput").ap())
    out = nc.dram_tensor("out", (N + P, D), F32, kind="ExternalOutput").ap()
    perceiver_layer(nc, *args, out)
    r = run_bass_kernel_spmd(nc, [in_map], core_ids=[0])
    return r.results[0]["out"][:N].reshape(B, T, D)
```

```python
from contextlib import ExitStack

import numpy as np

import concourse.bass as bass
from concourse import mybir

ALU = mybir.AluOpType
ACT = mybir.ActivationFunctionType
AX = mybir.AxisListType
F32 = mybir.dt.float32
BF16 = mybir.dt.bfloat16
I32 = mybir.dt.int32
U32 = mybir.dt.uint32

P = 128
B, T, D = 64, 32, 256
S = 257
H, DH = 16, 16
E, HID = 8, 512
N = B * T
GB = P // T
G = N // P
DC = D // P
SK = (S - 1) // P
HC = P // DH
HQ = P // T
TOP = 2
TILES = (N * TOP - E) // P + E
LOOK = 6
TABLE = -(-TILES // LOOK) * LOOK
SLOTS = E * N + TABLE * P
ROPE_BASE = 10000.0
LN_EPS = 1e-5
MASKED = -1e30

C_IDENT = 0
C_ROPE = C_IDENT + P
C_HEAD = C_ROPE + T
C_VHEAD = C_HEAD + HC
C_CAUSAL = C_VHEAD + HQ
C_EXPERT = C_CAUSAL + T
C_FIRST = C_EXPERT + E
C_TOKEN = C_FIRST + E
C_TILE = C_TOKEN + 1
C_FULL = C_TILE + TABLE
C_EARLIER = C_FULL + N // P
C_UP_TO = C_EARLIER + P
C_END = C_UP_TO + E * E


def shape_constants():
    c = np.zeros((P, C_END), np.float32)
    p = np.arange(P)
    c[:, C_IDENT:C_IDENT + P] = np.eye(P)
    t = np.arange(T)[None, :]
    theta = t * ROPE_BASE ** (-2.0 * (p % (DH // 2))[:, None] / DH)
    c[:, C_ROPE:C_ROPE + T] = np.cos(theta) + np.sin(theta)
    c[:, C_HEAD:C_HEAD + HC] = (p // DH)[:, None] == np.arange(HC)[None, :]
    c[:, C_VHEAD:C_VHEAD + HQ] = (p // T)[:, None] == np.arange(HQ)[None, :]
    c[:, C_CAUSAL:C_CAUSAL + T] = np.where(np.arange(T)[None, :] > (p % T)[:, None], MASKED, 0.0)
    c[:, C_EXPERT:C_EXPERT + E] = np.arange(E)
    c[:, C_FIRST:C_FIRST + E] = np.arange(E) * N
    c[:, C_TOKEN] = p
    c[:, C_TILE:C_TILE + TABLE] = np.arange(TABLE)
    c[:, C_FULL:C_FULL + N // P] = np.arange(N // P) * P
    c[:, C_EARLIER:C_EARLIER + P] = p[:, None] < p[None, :]
    c[:, C_UP_TO:C_END] = np.tri(E).reshape(1, E * E)
    return c


def empty_slots():
    slots = np.zeros((SLOTS, 2), np.int32)
    slots[:, 0] = N + np.arange(SLOTS) % P
    return slots


class Group:

    def __init__(self, i, c):
        self.i, self.c, self.p = i, c, c % 2

    def count(self, before=0):
        return self.i * 2 + (self.c + 1 - before)

    def visits(self):
        return self.i + (self.c // 2 + 1)

    def index(self):
        return self.i * 2 + self.c


class Tile:

    def __init__(self, i, c):
        self.i, self.c, self.pair, self.third, self.slot = i, c, c % 2, c % 3, c % LOOK

    def index(self):
        return self.i * LOOK + self.c

    def count(self, before=0):
        return self.i * LOOK + (self.c + 1 - before)

    def third_visits(self):
        return self.i * (LOOK // 3) + (self.c // 3 + 1)

    def slot_visits(self):
        return self.i + (self.c // LOOK + 1)

    def ahead(self, n):
        return Tile(self.i, self.c + n)


def tiles(engine, step):
    whole = (TILES - 2) // LOOK
    for c in range(LOOK):
        t = Tile(0, c)
        step(t, t.ahead(1), t.ahead(2))
    with engine.Fori(1, whole) as i:
        for c in range(LOOK):
            t = Tile(i, c)
            step(t, t.ahead(1), t.ahead(2))
    for n in range(whole * LOOK, TILES):
        t = Tile(n // LOOK, n % LOOK)
        step(t, *(t.ahead(k) if n + k < TILES else None for k in (1, 2)))


def wait(engine, semaphore, value):
    if not (isinstance(value, int) and value <= 0):
        engine.wait_ge(semaphore, value)


def pipeline(engine, slot):
    def groups(i, u, known):
        return [Group(i, u - lag) if not known or 0 <= 2 * i + u - lag < G else None for lag in (0, 1, 2, 3, -1)]

    for t in range(4):
        slot(*groups(t // 2, t % 2, True))
    with engine.Fori(2, G // 2 - 1) as i:
        for u in range(2):
            slot(*groups(i, u, False))
    for t in range(G - 2, G + 3):
        slot(*groups(t // 2, t % 2, True))


def run(*steps):
    for step, group in steps:
        if group is not None:
            step(group)


def wait_apart(engine, semaphore, value, passed):
    wait(engine, semaphore, value)
    if not isinstance(value, int):
        engine.sem_inc(passed, 1)


def perceiver_layer(nc, x, ctx, consts, slots_init, xWq, xbq, xWk, xbk, xWvT, xbv, WqT, bq, WkT, bk, WvT, bv, WoT, bo,
                    gate_W, W1, b1, W2, b2, out):
    SCALE = float(D) ** -0.5
    ATT_SCALE = float(DH) ** -0.5

    with ExitStack() as stack:
        slots = nc.dram_tensor("slots", (SLOTS, 2), I32, kind="Internal").ap()
        normed_rows = nc.dram_tensor("normed_rows", (N + P, D), F32, kind="Internal").ap()

        def sb(name, shape, dt=F32):
            return stack.enter_context(nc.sbuf_tensor(name, shape, dt))

        def ps(name, shape=(P, 512), dt=F32):
            return stack.enter_context(nc.psum_tensor(name, list(shape), dt))

        def sem(name):
            return stack.enter_context(nc.semaphore(name))

        cst = sb("cst", [P, C_END])
        ident = cst[:, C_IDENT:C_IDENT + P]
        rope = cst[:, C_ROPE:C_ROPE + T]
        head_mask = cst[:, C_HEAD:C_HEAD + HC]
        vhead_mask = cst[:, C_VHEAD:C_VHEAD + HQ]
        causal = cst[:, C_CAUSAL:C_CAUSAL + T]
        raw_wq = sb("raw_wq", [P, DC, D])
        raw_wk = sb("raw_wk", [P, DC, D])
        raw_b = sb("raw_b", [P, 2, DC])
        wqk = sb("wqk", [P, DC, D])
        wqbk_rows = sb("wqbk_rows", [P, D])
        bqbk = sb("bqbk", [P, 1])
        bqk = sb("bqk", [P, DC])
        w_xv = sb("w_xv", [P, DC, D])
        w_q = sb("w_q", [P, DC, D])
        w_k = sb("w_k", [P, DC, D])
        w_v = sb("w_v", [P, DC, D])
        w_o = sb("w_o", [P, DC, D])
        b_cols = sb("b_cols", [P, 3, DC])
        xbv_rows = sb("xbv_rows", [P, D])
        bo_rows = sb("bo_rows", [P, D])
        power = sb("power", [P, 1])
        eps = sb("eps", [P, 1])

        x_in = sb("x_in", [P, 2, D])
        ctx_in = sb("ctx_in", [P, 2, GB, SK, D])
        ctx_last = sb("ctx_last", [P, 2, D])
        stats = sb("stats", [P, 3, 6])
        mean_var = sb("mean_var", [P, 3, 2])
        var_eps = sb("var_eps", [P, 3, 1])
        rstd = sb("rstd", [P, 3, 1])
        xn1 = sb("xn1", [P, 2, D])
        xn1T = sb("xn1T", [P, DC, P])
        x_bv = sb("x_bv", [P, 2, D])
        junk = sb("junk", [P, D])
        qbk = sb("qbk", [P, 2, 2])
        qkT = sb("qkT", [P, DC, P])
        ctxT = sb("ctxT", [P, 2, GB, DC, S])
        smax = sb("smax", [P, 2])
        ebias = sb("ebias", [P, 1])
        probs = sb("probs", [P, S])
        ssum = sb("ssum", [P, 2])
        probsT = sb("probsT", [P, SK, P])
        mix = sb("mix", [P, D])
        mixT = sb("mixT", [P, DC, P])
        x1 = sb("x1", [P, 2, D])
        xn2 = sb("xn2", [P, D])
        xn2T = sb("xn2T", [P, DC, P])
        x1_bo = sb("x1_bo", [P, 2, D])
        qT = sb("qT", [P, DC, P])
        kT = sb("kT", [P, DC, P])
        vT = sb("vT", [P, DC, GB, HQ, T])
        k_heads = sb("k_heads", [P, DC, GB, HC * T])
        v_heads = sb("v_heads", [P, GB, H // HQ, HQ, DH + 1])
        att = sb("att", [P, H, T])
        att_max = sb("att_max", [P, H])
        att_sub = sb("att_sub", [P, H, T])
        att_exp = sb("att_exp", [P, H, T])
        att_scale = sb("att_scale", [P, H])
        attT = sb("attT", [P, H // HQ, P])
        y = sb("y", [P, D])
        yT = sb("yT", [P, DC, P])
        x2 = sb("x2", [P, 2, D])
        xn3 = sb("xn3", [P, 2, D])
        x3 = sb("x3", [P, 2, D])

        xn3T = sb("xn3T", [P, DC, P])
        gate_w = sb("gate_w", [P, DC, E])
        logitsT = sb("logitsT", [E, P])
        logit_bias = sb("logit_bias", [P, 1])
        gate_exp = sb("gate_exp", [P, E])
        gate_sum = sb("gate_sum", [P, 2])
        gates = sb("gates", [P, E])
        top_gates = sb("top_gates", [P, 8])
        top_experts = sb("top_experts", [P, 8], U32)
        top_expert = sb("top_expert", [P, TOP])
        top_sum = sb("top_sum", [P, 2])
        chosen = sb("chosen", [P, TOP, E])
        routed = sb("routed", [P, E], BF16)
        routed_before = sb("routed_before", [P, 2, E], BF16)
        earlier = sb("earlier", [P, P], BF16)
        ones = sb("ones", [P, P], BF16)
        places = sb("places", [P, E])
        place = sb("place", [P, TOP])
        place_slot = sb("place_slot", [P, TOP], I32)
        token = sb("token", [P, 2])
        slot_row = sb("slot_row", [P, TOP, 2], I32)
        counts = sb("counts", [1, E])
        started = sb("started", [1, E, N // P])
        tile_count = sb("tile_count", [1, E])
        up_to = sb("up_to", [1, E, E])
        tile_end = sb("tile_end", [1, E])
        row_skip = sb("row_skip", [1, E])
        passed = sb("passed", [1, TABLE, E])
        passed_rows = sb("passed_rows", [1, TABLE, E])
        tile_expert = sb("tile_expert", [1, 2, TABLE])
        tile_row = sb("tile_row", [1, 2, TABLE])
        table = sb("table", [1, 2, TABLE], I32)
        w1 = sb("w1", [P, E, DC, HID])
        w2 = sb("w2", [P, E, HID // P, D])
        b1_rows = sb("b1_rows", [P, E, HID])
        b2_rows = sb("b2_rows", [P, E, D])
        ids = sb("ids", [P, LOOK, 2], I32)
        reused = ctxT[:].rearrange("p g b c s -> p (g b c s)")
        xg = reused[:, 0:3 * D].rearrange("p (t d) -> p t d", t=3)
        xgT = reused[:, 3 * D:5 * D].rearrange("p (t c n) -> p t c n", t=2, c=DC)
        exp_out = reused[:, 5 * D:7 * D].rearrange("p (t d) -> p t d", t=2)
        hid = reused[:, 7 * D:7 * D + 2 * HID].rearrange("p (t d) -> p t d", t=2)
        hidT = reused[:, 7 * D + 2 * HID:7 * D + 4 * HID].rearrange("p (t c n) -> p t c n", t=2, c=HID // P)
        exp_scaled = sb("exp_scaled", [P, 2, D])

        turn = [ps("turn0"), ps("turn1")]
        xa = [ps("xa0"), ps("xa1")]
        sa = [ps("sa0"), ps("sa1"), ps("sa2")]
        gp = ps("gp")
        exp_bank = [sa[2], gp]

        consts_in, xw_in, sw_in, rows_in = sem("consts_in"), sem("xw_in"), sem("sw_in"), sem("rows_in")
        x_loaded = [sem("x_loaded0"), sem("x_loaded1")]
        ctx_loaded = [sem("ctx_loaded0"), sem("ctx_loaded1")]
        out_stored = [sem("out_stored0"), sem("out_stored1")]
        power_set, fused, fused_copied, fused_sum = sem("power_set"), sem("fused"), sem("fused_copied"), sem("fused_sum")
        names = ("stats1 mv1 eps1 rstd1 xn1 xn1T_ps xn1T_ready x_bv_ready qbk0 qbk_ready qkT_ps qkT_ready "
                 "turned ctxT_ready scores smax0 smax1 ebias_ready probs_ready recip1 probsT_ps probsT_ready "
                 "mix_ps mix_ready mixT_ps mixT_ready xv_ps x1_ready "
                 "stats2 mv2 eps2 rstd2 xn2_ready xn2T_ps xn2T_ready x1_bo_ready qk_ps v_ps qT_ready kT_ready vT_ready "
                 "k_heads0 k_heads1 k_heads2 vrep_ps v_heads_ready att_ps att_masked att_max_ready att_sub_ready att_exp_ready "
                 "att_scale_ready attT_ps attT_ready y_ps y_ready yT_ps yT_ready o_ps x2_ready "
                 "stats3 mv3 eps3 rstd3 xn3_ready x3_ready "
                 "xn3T_ps xn3T_ready logitsT_ps logitsT_ready logits_ps logit_bias_ready gate_exp_ready "
                 "gate_recip gates_ready top_gates_ready top_index top_expert_ready chosen_ready routed_ready "
                 "routed_sum rank_ps places_ready place_ready place_slot_ready top_sum_ready top_recip row_ready token_ready "
                 "counts_ps counts_ready started_ready tile_count_ready up_to_ready tile_end_ready row_skip_ready passed_ready "
                 "passed_rows_ready tile_sums tile_rows table_ready "
                 "xgT_ps xgT_ready hid_ps hid_ready hidT_ps hidT_ready exp_ps exp_out_ready exp_scaled_ready")
        rows_stored = [sem("rows_stored0"), sem("rows_stored1")]
        slots_empty, spare_set, spare_stored, gate_in, w1_in, w2_in, b12_in, tri_ready = (
            sem(n) for n in ("slots_empty", "spare_set", "spare_stored", "gate_in", "w1_in", "w2_in", "b12_in", "tri_ready"))
        scattered = sem("scattered")
        ids_loaded = [sem(f"ids_loaded{n}") for n in range(LOOK)]
        gathered = [sem("gathered0"), sem("gathered1"), sem("gathered2")]
        added = sem("added")
        dve_passed, pool_passed, pe_passed = sem("dve_passed"), sem("pool_passed"), sem("pe_passed")
        s = {n: sem(n) for n in names.split()}
        block = stack.enter_context(nc.Block())

        def as_heads(ap, h, w):
            return ap.rearrange("p (h w) -> p h w", h=h, w=w)

        @block.sync
        def _(sp):
            sp.dma_start(raw_wq[:], xWq.rearrange("(c p) d -> p c d", p=P)).then_inc(xw_in, 16)
            sp.dma_start(raw_wk[:], xWk.rearrange("(c p) d -> p c d", p=P)).then_inc(xw_in, 16)
            with nc.allow_non_contiguous_dma(reason="bias columns"):
                sp.dma_start(raw_b[:, 0], xbq.rearrange("(c p) -> p c", p=P)).then_inc(xw_in, 16)
                sp.dma_start(raw_b[:, 1], xbk.rearrange("(c p) -> p c", p=P)).then_inc(xw_in, 16)
            sp.dma_start(cst[:], consts).then_inc(consts_in, 16)

            def load(g):
                if not (isinstance(g.i, int) and g.index() < 2):
                    sp.wait_ge(s["x1_ready"], g.count(2))
                rows = bass.ds(g.index() * P, P)
                sp.dma_start(x_in[:, g.p], x[rows]).then_inc(x_loaded[g.p], 16)
                src = ctx[bass.ds(g.index() * GB, GB)]
                sp.dma_start(ctx_in[:, g.p].rearrange("p b s d -> p b (s d)"),
                             src[:, 0:S - 1].rearrange("b (p s) d -> p b (s d)", s=SK)).then_inc(ctx_loaded[g.p], 16)
                sp.dma_start(ctx_last[:, g.p],
                             src[:, S - 1:S].broadcast_to([GB, T, D])).then_inc(ctx_loaded[g.p], 16)

            load(Group(0, 0))
            for w, src in ((w_xv, xWvT), (w_q, WqT), (w_k, WkT), (w_v, WvT), (w_o, WoT)):
                sp.dma_start(w[:], src.rearrange("(c p) d -> p c d", p=P)).then_inc(sw_in, 16)
            with nc.allow_non_contiguous_dma(reason="bias columns"):
                for j, src in enumerate((bq, bk, bv)):
                    sp.dma_start(b_cols[:, j], src.rearrange("(c p) -> p c", p=P)).then_inc(sw_in, 16)
            sp.dma_start(xbv_rows[:], xbv.unsqueeze(0).broadcast_to([P, D])).then_inc(rows_in, 16)
            sp.dma_start(bo_rows[:], bo.unsqueeze(0).broadcast_to([P, D])).then_inc(rows_in, 16)
            sp.dma_start(gate_w[:], gate_W.rearrange("(c p) e -> p c e", p=P)).then_inc(gate_in, 16)
            sp.dma_start(slots.rearrange("(a b) c -> a (b c)", a=P), slots_init.rearrange("(a b) c -> a (b c)", a=P)).then_inc(slots_empty, 16)
            load(Group(0, 1))
            sp.wait_ge(spare_set, 1)
            sp.dma_start(out[N:N + P], exp_scaled[:, 0]).then_inc(spare_stored, 16)
            sp.dma_start(normed_rows[N:N + P], exp_scaled[:, 0]).then_inc(spare_stored, 16)

            def store(d):
                sp.wait_ge(s["xn3_ready"], d.count())
                sp.dma_start(normed_rows[bass.ds(d.index() * P, P)], xn3[:, d.p]).then_inc(rows_stored[d.p], 16)
                sp.wait_ge(s["x3_ready"], d.count())
                sp.dma_start(out[bass.ds(d.index() * P, P)], x3[:, d.p]).then_inc(out_stored[d.p], 16)

            def slot(a, b, d, c, f):
                run((store, d))
                if a is not None and not (isinstance(a.i, int) and a.index() + 2 >= G):
                    load(Group(a.i, a.c + 2))
                if a is not None and isinstance(a.i, int) and a.index() == 0:
                    for k in range(DC):
                        sp.dma_start(w1[:, :, k], W1[:, k * P:(k + 1) * P].rearrange("e p n -> p e n")).then_inc(w1_in, 16)
                    for src, dst in ((b1, b1_rows), (b2, b2_rows)):
                        sp.dma_start(dst[:].rearrange("p e n -> p (e n)"),
                                     src.rearrange("e n -> (e n)").unsqueeze(0).broadcast_to([P, E * src.shape[1]])).then_inc(b12_in, 16)
                if a is not None and isinstance(a.i, int) and a.index() == 1:
                    for k in range(HID // P):
                        sp.dma_start(w2[:, :, k], W2[:, k * P:(k + 1) * P].rearrange("e p n -> p e n")).then_inc(w2_in, 16)
            pipeline(sp, slot)

            sp.wait_ge(scattered, 16 * TOP * G)
            sp.wait_ge(s["table_ready"], 1)

            def load_ids(t):
                first = sp.value_load(table[0:1, 1, bass.ds(t.index(), 1)], min_val=0, max_val=SLOTS - P)
                sp.dma_start(ids[:, t.slot], slots[bass.ds(first, P)]).then_inc(ids_loaded[t.slot], 16)

            for n in range(LOOK):
                load_ids(Tile(0, n))

            with sp.Fori(0, (TABLE - LOOK) // LOOK) as i:
                for c in range(LOOK):
                    t = Tile(i, c)
                    sp.wait_ge(added, t.count() * 16)
                    load_ids(t.ahead(LOOK))
            for n in range(TILES, TABLE):
                sp.wait_ge(ids_loaded[n % LOOK], 16 * (TABLE // LOOK))
            sp.wait_ge(added, 16 * TILES)

        @block.gpsimd
        def _(pool):
            nc.gpsimd.memset(eps[:], LN_EPS)
            nc.gpsimd.memset(power[:], -0.5).then_inc(power_set, 1)
            pool.wait_ge(power_set, 1)
            nc.gpsimd.memset(exp_scaled[:, 0], 0.0).then_inc(spare_set, 1)
            nc.gpsimd.memset(ones[:], 1.0)
            nc.gpsimd.memset(routed_before[:], 0.0)
            pool.wait_ge(consts_in, 16)
            nc.gpsimd.tensor_copy(earlier[:], cst[:, C_EARLIER:C_EARLIER + P]).then_inc(tri_ready, 1)

            def rstd_of(g, n):
                pool.wait_ge(s[f"mv{n}"], g.count())
                nc.gpsimd.tensor_tensor(var_eps[:, n - 1], mean_var[:, n - 1, 1:2], eps[:], ALU.add).then_inc(s[f"eps{n}"], 1)
                pool.wait_ge(s[f"eps{n}"], g.count())
                nc.gpsimd.tensor_tensor(rstd[:, n - 1], var_eps[:, n - 1], power[:], ALU.pow).then_inc(s[f"rstd{n}"], 1)

            def residual1(g):
                pool.wait_ge(x_loaded[g.p], g.visits() * 16)
                nc.gpsimd.tensor_tensor(x_bv[:, g.p], x_in[:, g.p], xbv_rows[:], ALU.add).then_inc(s["x_bv_ready"], 1)

            pool.wait_ge(rows_in, 32)
            rstd_of(Group(0, 0), 1)
            residual1(Group(0, 0))

            def key_heads(b):
                pool.wait_ge(s["kT_ready"], b.count())
                nc.gpsimd.tensor_tensor(
                    k_heads[:, 1].rearrange("p b (h k) -> p b h k", h=HC)[:, :, 0:HC // 2],
                    kT[:, 1].rearrange("p (b k) -> p b k", b=GB).unsqueeze(2).broadcast_to([P, GB, HC // 2, T]),
                    head_mask[:, 0:HC // 2].unsqueeze(1).unsqueeze(3).broadcast_to([P, GB, HC // 2, T]), ALU.mult).then_inc(s["k_heads1"], 1)

            def less_largest(b):
                pool.wait_ge(s["att_max_ready"], b.count())
                nc.gpsimd.tensor_tensor(att_sub[:], att[:], att_max[:].unsqueeze(2).broadcast_to([P, H, T]),
                                        ALU.subtract).then_inc(s["att_sub_ready"], 1)

            def residual2(a):
                pool.wait_ge(s["x1_ready"], a.count())
                nc.gpsimd.tensor_tensor(x1_bo[:, a.p], x1[:, a.p], bo_rows[:], ALU.add).then_inc(s["x1_bo_ready"], 1)

            def residual3(d):
                pool.wait_ge(s["xn3_ready"], d.count())
                if not (isinstance(d.i, int) and d.index() < 2):
                    pool.wait_ge(out_stored[d.p], d.visits() * 16 - 16)
                nc.gpsimd.tensor_tensor(x3[:, d.p], x2[:, d.p], xn3[:, d.p], ALU.add).then_inc(s["x3_ready"], 1)

            def scatter(c):
                if isinstance(c.i, int) and c.index() == 0:
                    pool.wait_ge(slots_empty, 16)
                pool.wait_ge(s["row_ready"], c.count())
                wait_apart(pool, s["place_slot_ready"], c.count(), pool_passed)
                for k in range(TOP):
                    nc.gpsimd.indirect_dma_start(
                        out=slots, out_offset=bass.IndirectOffsetOnAxis(ap=place_slot[:, k:k + 1], axis=0),
                        in_=slot_row[:, k], in_offset=None).then_inc(scattered, 16)

            def slot(a, b, d, c, f):
                run((key_heads, b), (lambda g: rstd_of(g, 3), d), (lambda g: rstd_of(g, 1), f), (residual1, f),
                    (residual3, d), (less_largest, b), (lambda g: rstd_of(g, 2), a), (residual2, a), (scatter, c))
            pipeline(pool, slot)

            for sm in rows_stored + out_stored:
                pool.wait_ge(sm, 16 * (G // 2))
            pool.wait_ge(spare_stored, 32)

            def gather(t):
                wait_apart(pool, ids_loaded[t.slot], t.slot_visits() * 16, pool_passed)
                nc.gpsimd.indirect_dma_start(
                    out=xg[:, t.third], out_offset=None, in_=normed_rows,
                    in_offset=bass.IndirectOffsetOnAxis(ap=ids[:, t.slot, 0:1], axis=0)).then_inc(gathered[t.third], 16)

            gather(Tile(0, 0))
            gather(Tile(0, 1))

            def step(t, following, after):
                if after is not None:
                    wait(pool, s["xgT_ps"], t.count(1))
                    gather(after)
                pool.wait_ge(s["exp_scaled_ready"], t.count())
                wait_apart(pool, added, t.count(1) * 16, pool_passed)
                nc.gpsimd.indirect_dma_start(
                    out=out, out_offset=bass.IndirectOffsetOnAxis(ap=ids[:, t.slot, 0:1], axis=0),
                    in_=exp_scaled[:, t.pair], in_offset=None, compute_op=ALU.add).then_inc(added, 16)
            tiles(pool, step)

        @block.scalar
        def _(act):
            act.wait_ge(fused, 1)
            nc.scalar.copy(wqk[:], xa[0][:].rearrange("p (c d) -> p c d", c=DC)).then_inc(fused_copied, 1)

            def copy_out(dst, bank, cols, ready, done, g):
                act.wait_ge(s[ready], g.count())
                nc.scalar.copy(dst, bank[:, 0:cols]).then_inc(s[done], 1)

            def with_bias(dst, bank, bias, ready, done, g):
                act.wait_ge(s[ready], g.count())
                for c in range(DC):
                    last = nc.scalar.activation(dst[:, c], bank[:, c * P:(c + 1) * P], ACT.Identity, bias=bias[:, c:c + 1])
                last.then_inc(s[done], 1)

            def turned(g, b):
                act.wait_ge(s["turned"], g.count(1) * 5 + (b + 1))
                nc.scalar.copy(ctxT[:, g.p, b, :, 0:S - 1], turn[b % 2][:].rearrange("p (c k) -> p c k", c=DC)).then_inc(s["ctxT_ready"], 1)

            def turned_last(g):
                act.wait_ge(s["turned"], g.count(1) * 5 + 5)
                nc.scalar.copy(ctxT[:, g.p, :, :, S - 1],
                               turn[0][:, 0:2 * P].rearrange("p (c b t) -> p b c t", c=DC, b=GB)[:, :, :, 0]).then_inc(s["ctxT_ready"], 1)

            for b in range(GB):
                turned(Group(0, 0), b)
            turned_last(Group(0, 0))

            def flat(ap):
                return ap[:].rearrange("p c t -> p (c t)")

            def norm1T(a):
                copy_out(flat(xn1T), xa[0], D, "xn1T_ps", "xn1T_ready", a)

            def norm2T(b):
                copy_out(flat(xn2T), sa[0], D, "xn2T_ps", "xn2T_ready", b)

            def norm3T(c):
                copy_out(flat(xn3T), gp, D, "xn3T_ps", "xn3T_ready", c)

            def queries(a):
                if isinstance(a.i, int) and a.index() == 0:
                    act.wait_ge(fused_sum, 2)
                with_bias(qkT, xa[1], bqk, "qkT_ps", "qkT_ready", a)

            def values(b):
                if isinstance(b.i, int) and b.index() == 0:
                    act.wait_ge(sw_in, 16 * 8)
                act.wait_ge(s["v_ps"], b.count())
                for k in range(DC):
                    last = nc.scalar.activation(
                        vT[:, k], sa[1][:, k * P:(k + 1) * P].rearrange("p (b t) -> p b t", b=GB).unsqueeze(2).broadcast_to([P, GB, HQ, T]),
                        ACT.Identity, bias=b_cols[:, 2, k:k + 1])
                last.then_inc(s["vT_ready"], 1)

            def key_heads(b):
                act.wait_ge(s["kT_ready"], b.count())
                for h in range(HC // 2, HC):
                    last = nc.scalar.activation(k_heads[:, 1, :, h * T:(h + 1) * T], kT[:, 1].rearrange("p (b k) -> p b k", b=GB),
                                                ACT.Copy, scale=head_mask[:, h:h + 1])
                last.then_inc(s["k_heads2"], 1)

            def cross_exp(a):
                act.wait_ge(s["ebias_ready"], a.count())
                nc.scalar.activation(probs[:], xa[0][:, 0:S], ACT.Exp, bias=ebias[:], scale=SCALE,
                                     accum_out=ssum[:, 0:1]).then_inc(s["probs_ready"], 1)

            def cross_probsT(a):
                copy_out(flat(probsT), xa[1], D, "probsT_ps", "probsT_ready", a)

            def cross_mixT(a):
                copy_out(flat(mixT), xa[0], D, "mixT_ps", "mixT_ready", a)

            def gates_exp(c):
                act.wait_ge(s["logit_bias_ready"], c.count())
                nc.scalar.activation(gate_exp[:], gp[:, 3 * P:3 * P + E], ACT.Exp, bias=logit_bias[:],
                                     accum_out=gate_sum[:, 0:1]).then_inc(s["gate_exp_ready"], 1)

            def self_exp(b):
                act.wait_ge(s["att_sub_ready"], b.count())
                nc.scalar.activation(att_exp[:], att_sub[:], ACT.Exp, scale=ATT_SCALE).then_inc(s["att_exp_ready"], 1)

            def self_weightsT(d):
                copy_out(flat(attT), sa[2], 512, "attT_ps", "attT_ready", d)

            def self_yT(d):
                copy_out(flat(yT), sa[2], D, "yT_ps", "yT_ready", d)

            def slot(a, b, d, c, f):
                run((norm1T, a), (self_weightsT, d), (queries, a), (norm3T, c), (norm2T, b), (cross_exp, a), (self_yT, d),
                    (lambda g: turned(g, 0), f), (values, b), (key_heads, b), (cross_probsT, a), (gates_exp, c),
                    (lambda g: turned(g, 1), f), (lambda g: turned(g, 2), f), (cross_mixT, a),
                    (lambda g: turned(g, 3), f), (turned_last, f), (self_exp, b))
            pipeline(act, slot)

            def step(t, following, after):
                act.wait_ge(s["hidT_ps"], t.count())
                nc.scalar.activation(hidT[:, t.pair], sa[t.pair][:].rearrange("p (c t) -> p c t", c=HID // P), ACT.Relu).then_inc(s["hidT_ready"], 1)
                if after is not None:
                    expert_xT(after)

            def expert_xT(t):
                act.wait_ge(s["xgT_ps"], t.count())
                nc.scalar.copy(xgT[:, t.pair], turn[t.pair][:, 0:D].rearrange("p (c t) -> p c t", c=DC)).then_inc(s["xgT_ready"], 1)

            expert_xT(Tile(0, 0))
            expert_xT(Tile(0, 1))
            tiles(act, step)

        @block.vector
        def _(dve):
            dve.wait_ge(fused, 1)
            nc.vector.tensor_copy(wqbk_rows[:], xa[1][:, 0:D]).then_inc(fused_sum, 1)
            nc.vector.tensor_copy(bqbk[:], xa[1][:, D:D + 1])
            nc.vector.tensor_copy(bqk[:], xa[1][:, D + 2:D + 2 + DC]).then_inc(fused_sum, 1)
            dve.wait_ge(fused_sum, 2)
            dve.wait_ge(consts_in, 16)
            nc.vector.tensor_copy(v_heads[:, :, :, :, DH].rearrange("p b c h -> p (b c) h"),
                                  vhead_mask.unsqueeze(1).broadcast_to([P, GB * H // HQ, HQ]))

            def norm(g, n, src):
                nc.vector.bn_stats(stats[:, n - 1], src).then_inc(s[f"stats{n}"], 1)
                wait_apart(dve, s[f"stats{n}"], g.count(), dve_passed)
                nc.vector.bn_aggr(mean_var[:, n - 1], stats[:, n - 1]).then_inc(s[f"mv{n}"], 1)

            def normed(g, n, src, dst, done):
                dve.wait_ge(s[f"rstd{n}"], g.count())
                nc.vector.tensor_scalar(dst, src, mean_var[:, n - 1, 0:1], rstd[:, n - 1], ALU.subtract, ALU.mult).then_inc(s[done], 1)

            def norm1(g):
                dve.wait_ge(x_loaded[g.p], g.visits() * 16)
                norm(g, 1, x_in[:, g.p])

            def normed1(g):
                normed(g, 1, x_in[:, g.p], xn1[:, g.p], "xn1")
                dve.wait_ge(s["xn1"], g.count())
                nc.vector.tensor_tensor_reduce(out=junk[:], in0=xn1[:, g.p], in1=wqbk_rows[:], scale=1.0, scalar=0.0,
                                               op0=ALU.mult, op1=ALU.add, accum_out=qbk[:, g.p, 0:1]).then_inc(s["qbk0"], 1)
                dve.wait_ge(s["qbk0"], g.count())
                nc.vector.tensor_tensor(qbk[:, g.p, 1:2], qbk[:, g.p, 0:1], bqbk[:], ALU.add).then_inc(s["qbk_ready"], 1)

            norm1(Group(0, 0))
            normed1(Group(0, 0))

            def rotated(g, bank, at, j, dst, done):
                for c in range(DC):
                    last = nc.vector.scalar_tensor_tensor(
                        out=dst[:, c].rearrange("p (b t) -> p b t", b=GB),
                        in0=bank[:, at + c * P:at + (c + 1) * P].rearrange("p (b t) -> p b t", b=GB),
                        scalar=b_cols[:, j, c:c + 1], in1=rope.unsqueeze(1).broadcast_to([P, GB, T]),
                        op0=ALU.add, op1=ALU.mult)
                last.then_inc(s[done], 1)

            def gate_softmax(c):
                dve.wait_ge(s["gate_exp_ready"], c.count())
                nc.vector.reciprocal(gate_sum[:, 1:2], gate_sum[:, 0:1]).then_inc(s["gate_recip"], 1)
                dve.wait_ge(s["gate_recip"], c.count())
                nc.vector.tensor_scalar(gates[:], gate_exp[:], gate_sum[:, 1:2], None, ALU.mult).then_inc(s["gates_ready"], 1)
                wait_apart(dve, s["gates_ready"], c.count(), dve_passed)
                nc.vector.max(top_gates[:], gates[:]).then_inc(s["top_gates_ready"], 1)
                wait_apart(dve, s["top_gates_ready"], c.count(), dve_passed)
                nc.vector.max_index(top_experts[:], top_gates[:], gates[:]).then_inc(s["top_index"], 1)
                nc.vector.tensor_scalar(top_sum[:, 0:1], top_gates[:, 0:1], top_gates[:, 1:2], 1e-8, ALU.add, ALU.add).then_inc(s["top_sum_ready"], 1)
                dve.wait_ge(s["top_index"], c.count())
                nc.vector.tensor_copy(top_expert[:], top_experts[:, 0:TOP]).then_inc(s["top_expert_ready"], 1)
                dve.wait_ge(s["top_sum_ready"], c.count())
                nc.vector.reciprocal(top_sum[:, 1:2], top_sum[:, 0:1]).then_inc(s["top_recip"], 1)
                dve.wait_ge(s["top_expert_ready"], c.count())
                for k in range(TOP):
                    nc.vector.tensor_scalar(chosen[:, k], cst[:, C_EXPERT:C_EXPERT + E], top_expert[:, k:k + 1], None,
                                            ALU.is_equal).then_inc(s["chosen_ready"], 1)
                dve.wait_ge(s["chosen_ready"], c.count() * TOP)
                nc.vector.tensor_tensor(routed[:], chosen[:, 0], chosen[:, 1], ALU.add).then_inc(s["routed_ready"], 1)
                wait(dve, scattered, c.count(1) * (16 * TOP))
                dve.wait_ge(s["top_recip"], c.count())
                nc.vector.tensor_scalar(slot_row[:, :, 1].bitcast(F32), top_gates[:, 0:TOP], top_sum[:, 1:2], None, ALU.mult)
                nc.vector.tensor_copy(slot_row[:, :, 0], token[:, 0:1].broadcast_to([P, TOP])).then_inc(s["row_ready"], 1)
                dve.wait_ge(s["row_ready"], c.count())
                nc.vector.tensor_scalar(token[:, 0:1], token[:, 0:1], float(P), None, ALU.add).then_inc(s["token_ready"], 1)
                dve.wait_ge(s["routed_ready"], c.count())
                nc.vector.tensor_tensor(routed_before[:, 1 - c.p], routed_before[:, c.p], routed[:], ALU.add).then_inc(s["routed_sum"], 1)

            def gate_places(c):
                dve.wait_ge(s["rank_ps"], c.count())
                nc.vector.tensor_tensor(places[:], gp[:, 3 * P + E:3 * P + 2 * E], cst[:, C_FIRST:C_FIRST + E], ALU.add).then_inc(s["places_ready"], 1)
                dve.wait_ge(s["places_ready"], c.count())
                for k in range(TOP):
                    nc.vector.tensor_tensor_reduce(out=junk[:, k * E:(k + 1) * E], in0=chosen[:, k], in1=places[:], scale=1.0, scalar=0.0,
                                                   op0=ALU.mult, op1=ALU.add, accum_out=place[:, k:k + 1]).then_inc(s["place_ready"], 1)
                dve.wait_ge(s["place_ready"], c.count() * TOP)
                nc.vector.tensor_copy(place_slot[:], place[:]).then_inc(s["place_slot_ready"], 1)

            nc.vector.tensor_copy(token[:, 0:1], cst[:, C_TOKEN:C_TOKEN + 1]).then_inc(s["token_ready"], 1)

            def keys_queries(b):
                if isinstance(b.i, int) and b.index() == 0:
                    dve.wait_ge(sw_in, 16 * 8)
                dve.wait_ge(s["qk_ps"], b.count())
                rotated(b, sa[0], D, 1, kT, "kT_ready")
                rotated(b, sa[0], 0, 0, qT, "qT_ready")
                dve.wait_ge(s["kT_ready"], b.count())
                nc.vector.tensor_tensor(
                    k_heads[:, 0].rearrange("p b (h k) -> p b h k", h=HC),
                    kT[:, 0].rearrange("p (b k) -> p b k", b=GB).unsqueeze(2).broadcast_to([P, GB, HC, T]),
                    head_mask.unsqueeze(1).unsqueeze(3).broadcast_to([P, GB, HC, T]), ALU.mult).then_inc(s["k_heads0"], 1)

            def logits_rows(c):
                dve.wait_ge(s["logitsT_ps"], c.count())
                nc.vector.tensor_copy(logitsT[:], gp[0:E, 2 * P:3 * P]).then_inc(s["logitsT_ready"], 1)

            def cross_largest(a):
                dve.wait_ge(s["scores"], a.count())
                nc.vector.tensor_reduce(smax[:, 0:1], xa[0][:, 0:S], AX.X, ALU.max).then_inc(s["smax0"], 1)
                dve.wait_ge(s["smax0"], a.count())
                nc.vector.tensor_tensor(smax[:, 1:2], smax[:, 0:1], qbk[:, a.p, 1:2], ALU.add).then_inc(s["smax1"], 1)
                dve.wait_ge(s["smax1"], a.count())
                nc.vector.tensor_scalar(ebias[:], smax[:, 1:2], qbk[:, a.p, 1:2], -SCALE, ALU.subtract, ALU.mult).then_inc(s["ebias_ready"], 1)

            def value_heads(b, n):
                dve.wait_ge(s["vrep_ps"], b.count(1) * 2 + (n + 1))
                nc.vector.tensor_tensor(
                    v_heads[:, 2 * n:2 * n + 2, :, :, 0:DH].rearrange("p b c h w -> p (b c) h w"),
                    sa[1][:].rearrange("p (c h w) -> p c h w", h=HQ, w=DH),
                    vhead_mask.unsqueeze(1).unsqueeze(3).broadcast_to([P, 2 * H // HQ, HQ, DH]), ALU.mult).then_inc(s["v_heads_ready"], 1)

            def self_largest(b):
                dve.wait_ge(s["att_ps"], b.count())
                nc.vector.tensor_tensor(att[:], as_heads(sa[0][:], H, T), causal.unsqueeze(1).broadcast_to([P, H, T]),
                                        ALU.add).then_inc(s["att_masked"], 1)
                dve.wait_ge(s["att_masked"], b.count())
                nc.vector.tensor_reduce(att_max[:], att[:], AX.X, ALU.max).then_inc(s["att_max_ready"], 1)

            def logits_largest(c):
                dve.wait_ge(s["logits_ps"], c.count())
                nc.vector.tensor_reduce(logit_bias[:], gp[:, 3 * P:3 * P + E], AX.X, ALU.max, negate=True).then_inc(s["logit_bias_ready"], 1)

            def cross_mix(a):
                dve.wait_ge(s["probs_ready"], a.count())
                nc.vector.reciprocal(ssum[:, 1:2], ssum[:, 0:1]).then_inc(s["recip1"], 1)
                dve.wait_ge(s["mix_ps"], a.count())
                nc.vector.scalar_tensor_tensor(out=mix[:], in0=ctx_last[:, a.p], scalar=probs[:, S - 1:S],
                                               in1=xa[0][:, 0:D], op0=ALU.mult, op1=ALU.add).then_inc(s["mix_ready"], 1)

            def cross_end(a):
                dve.wait_ge(s["recip1"], a.count())
                dve.wait_ge(s["x_bv_ready"], a.count())
                dve.wait_ge(s["xv_ps"], a.count())
                nc.vector.scalar_tensor_tensor(out=x1[:, a.p], in0=xa[1][:, 0:D], scalar=ssum[:, 1:2], in1=x_bv[:, a.p],
                                               op0=ALU.mult, op1=ALU.add).then_inc(s["x1_ready"], 1)
                dve.wait_ge(s["x1_ready"], a.count())
                norm(a, 2, x1[:, a.p])

            def self_scaled(d):
                heads = sa[2][:, 0:H * (DH + 1)].rearrange("p (h w) -> p h w", w=DH + 1)
                dve.wait_ge(s["y_ps"], d.count())
                nc.vector.reciprocal(att_scale[:], heads[:, :, DH]).then_inc(s["att_scale_ready"], 1)
                dve.wait_ge(s["att_scale_ready"], d.count())
                nc.vector.tensor_tensor(as_heads(y[:], H, DH), heads[:, :, 0:DH],
                                        att_scale[:].unsqueeze(2).broadcast_to([P, H, DH]), ALU.mult).then_inc(s["y_ready"], 1)

            def self_end(d):
                dve.wait_ge(s["x1_bo_ready"], d.count())
                dve.wait_ge(s["o_ps"], d.count())
                nc.vector.tensor_tensor(x2[:, d.p], sa[2][:, 0:D], x1_bo[:, d.p], ALU.add).then_inc(s["x2_ready"], 1)
                dve.wait_ge(s["x2_ready"], d.count())
                norm(d, 3, x2[:, d.p])

            def normed2(a):
                normed(a, 2, x1[:, a.p], xn2[:], "xn2_ready")

            def normed3(d):
                if not (isinstance(d.i, int) and d.index() < 2):
                    dve.wait_ge(rows_stored[d.p], d.visits() * 16 - 16)
                normed(d, 3, x2[:, d.p], xn3[:, d.p], "xn3_ready")

            def slot(a, b, d, c, f):
                run((self_scaled, d), (cross_largest, a), (logits_rows, c), (norm1, f), (keys_queries, b), (logits_largest, c),
                    (self_end, d), (lambda g: value_heads(g, 0), b), (cross_mix, a), (normed3, d),
                    (lambda g: value_heads(g, 1), b), (normed1, f), (self_largest, b), (gate_softmax, c),
                    (cross_end, a), (gate_places, c), (normed2, a))
            pipeline(dve, slot)

            dve.wait_ge(s["counts_ps"], 1)
            nc.vector.tensor_copy(counts[:], gp[0:1, 0:E]).then_inc(s["counts_ready"], 1)
            dve.wait_ge(s["counts_ready"], 1)
            nc.vector.tensor_tensor(started[:], counts[:].unsqueeze(2).broadcast_to([1, E, N // P]),
                                    cst[0:1, C_FULL:C_FULL + N // P].unsqueeze(1).broadcast_to([1, E, N // P]),
                                    ALU.is_gt).then_inc(s["started_ready"], 1)
            dve.wait_ge(s["started_ready"], 1)
            nc.vector.tensor_reduce(tile_count[:], started[:], AX.X, ALU.add).then_inc(s["tile_count_ready"], 1)
            dve.wait_ge(s["tile_count_ready"], 1)
            nc.vector.tensor_tensor(up_to[:], tile_count[:].unsqueeze(1).broadcast_to([1, E, E]),
                                    cst[0:1, C_UP_TO:C_UP_TO + E * E].rearrange("p (a b) -> p a b", a=E), ALU.mult).then_inc(s["up_to_ready"], 1)
            dve.wait_ge(s["up_to_ready"], 1)
            nc.vector.tensor_reduce(tile_end[:], up_to[:], AX.X, ALU.add).then_inc(s["tile_end_ready"], 1)
            nc.vector.tensor_scalar(row_skip[:], tile_count[:], -float(P), float(N), ALU.mult, ALU.add).then_inc(s["row_skip_ready"], 1)
            dve.wait_ge(s["tile_end_ready"], 1)
            tile_number = cst[0:1, C_TILE:C_TILE + TABLE]
            nc.vector.tensor_tensor(passed[:], tile_number.unsqueeze(2).broadcast_to([1, TABLE, E]),
                                    tile_end[:].unsqueeze(1).broadcast_to([1, TABLE, E]), ALU.is_ge).then_inc(s["passed_ready"], 1)
            dve.wait_ge(s["passed_ready"], 1)
            dve.wait_ge(s["row_skip_ready"], 1)
            nc.vector.tensor_tensor(passed_rows[:], passed[:], row_skip[:].unsqueeze(1).broadcast_to([1, TABLE, E]),
                                    ALU.mult).then_inc(s["passed_rows_ready"], 1)
            nc.vector.tensor_reduce(tile_expert[:, 0], passed[:], AX.X, ALU.add).then_inc(s["tile_sums"], 1)
            dve.wait_ge(s["passed_rows_ready"], 1)
            nc.vector.tensor_reduce(tile_row[:, 0], passed_rows[:], AX.X, ALU.add).then_inc(s["tile_sums"], 1)
            dve.wait_ge(s["tile_sums"], 2)
            nc.vector.tensor_scalar(table[:, 0], tile_expert[:, 0], float(E - 1), None, ALU.min)
            nc.vector.scalar_tensor_tensor(out=table[:, 1], in0=tile_number, scalar=float(P), in1=tile_row[:, 0],
                                           op0=ALU.mult, op1=ALU.add).then_inc(s["table_ready"], 1)
            dve.wait_ge(s["table_ready"], 1)
            dve.wait_ge(b12_in, 32)

            def expert_of(t):
                return dve.value_load(table[0:1, 0, bass.ds(t.index(), 1)], min_val=0, max_val=E - 1)

            def hidden(t):
                e = expert_of(t)
                dve.wait_ge(s["hid_ps"], t.count())
                nc.vector.tensor_tensor(hid[:, t.pair].unsqueeze(1), xa[t.pair][:].unsqueeze(1), b1_rows[:, bass.ds(e, 1)], ALU.add).then_inc(s["hid_ready"], 1)

            def step(t, following, after):
                if following is not None:
                    hidden(following)
                e = expert_of(t)
                dve.wait_ge(s["exp_ps"], t.count())
                nc.vector.tensor_tensor(exp_out[:, t.pair].unsqueeze(1), exp_bank[t.pair][:, 0:D].unsqueeze(1), b2_rows[:, bass.ds(e, 1)], ALU.add).then_inc(s["exp_out_ready"], 1)
                dve.wait_ge(s["exp_out_ready"], t.count())
                wait(dve, added, t.count(2) * 16)
                nc.vector.tensor_scalar(exp_scaled[:, t.pair], exp_out[:, t.pair], ids[:, t.slot, 1:2].bitcast(F32), None, ALU.mult).then_inc(s["exp_scaled_ready"], 1)

            hidden(Tile(0, 0))
            tiles(dve, step)

        @block.tensor
        def _(pe):
            mm = nc.tensor.matmul

            def transposes(bank, src, n=DC):
                for c in range(n):
                    last = nc.tensor.transpose(bank[:, c * P:(c + 1) * P], src[:, c * P:(c + 1) * P], ident)
                return last

            pe.wait_ge(xw_in, 64)
            for m in range(DC):
                for k in range(DC):
                    mm(xa[0][:, m * D:(m + 1) * D], raw_wq[:, k, m * P:(m + 1) * P], raw_wk[:, k], start=(k == 0), stop=(k == DC - 1))
            for k in range(DC):
                bk_all = raw_b[:, 1, k:k + 1].broadcast_to([P, P])
                mm(xa[1][:, 0:D], bk_all, raw_wq[:, k], start=(k == 0), stop=(k == DC - 1))
            for k in range(DC):
                bk_all = raw_b[:, 1, k:k + 1].broadcast_to([P, P])
                mm(xa[1][:, D:D + 1], bk_all, raw_b[:, 0, k:k + 1], start=(k == 0), stop=(k == DC - 1))
            for m in range(DC):
                for k in range(DC):
                    last = mm(xa[1][:, D + 2 + m:D + 3 + m], raw_wk[:, k, m * P:(m + 1) * P], raw_b[:, 0, k:k + 1],
                              start=(k == 0), stop=(k == DC - 1))
            last.then_inc(fused, 1)
            pe.wait_ge(consts_in, 16)

            def turn_context(g, b):
                if b == 0:
                    pe.wait_ge(ctx_loaded[g.p], g.visits() * 32)
                wait(pe, s["ctxT_ready"], g.count(1) * 5 + (0, 0, 1, 2)[b])
                for c in range(DC):
                    for k in range(SK):
                        last = nc.tensor.transpose(turn[b % 2][:, (c * SK + k) * P:(c * SK + k + 1) * P],
                                                   ctx_in[:, g.p, b, k, c * P:(c + 1) * P], ident)
                last.then_inc(s["turned"], 1)

            def turn_last(g):
                pe.wait_ge(s["ctxT_ready"], g.count(1) * 5 + 3)
                transposes(turn[0], ctx_last[:, g.p]).then_inc(s["turned"], 1)

            for b in range(GB):
                turn_context(Group(0, 0), b)
            turn_last(Group(0, 0))
            pe.wait_ge(fused_copied, 1)
            pe.wait_ge(fused_sum, 2)

            def project(bank, at, w, src):
                for m in range(DC):
                    for k in range(DC):
                        last = mm(bank[:, at + m * P:at + (m + 1) * P], w[:, k, m * P:(m + 1) * P], src[:, k],
                                  start=(k == 0), stop=(k == DC - 1))
                return last

            def norm1T(a):
                pe.wait_ge(s["xn1"], a.count())
                transposes(xa[0], xn1[:, a.p]).then_inc(s["xn1T_ps"], 1)

            def norm2T(b):
                pe.wait_ge(s["xn2_ready"], b.count())
                transposes(sa[0], xn2[:]).then_inc(s["xn2T_ps"], 1)

            def norm3T(c):
                wait(pe, s["places_ready"], c.count(1))
                pe.wait_ge(s["xn3_ready"], c.count())
                transposes(gp, xn3[:, c.p]).then_inc(s["xn3T_ps"], 1)

            def queries(a):
                wait(pe, s["x1_ready"], a.count(1))
                pe.wait_ge(s["xn1T_ready"], a.count())
                project(xa[1], 0, wqk, xn1T).then_inc(s["qkT_ps"], 1)

            def projections(b):
                if isinstance(b.i, int) and b.index() == 0:
                    pe.wait_ge(sw_in, 16 * 8)
                pe.wait_ge(s["xn2T_ready"], b.count())
                project(sa[0], D, w_k, xn2T)
                project(sa[0], 0, w_q, xn2T).then_inc(s["qk_ps"], 1)
                wait(pe, s["v_heads_ready"], b.count(1) * 2)
                project(sa[1], 0, w_v, xn2T).then_inc(s["v_ps"], 1)

            def logits_rows(c):
                if isinstance(c.i, int) and c.index() == 0:
                    pe.wait_ge(gate_in, 16)
                    pe.wait_ge(tri_ready, 1)
                pe.wait_ge(s["xn3T_ready"], c.count())
                for k in range(DC):
                    last = mm(gp[0:E, 2 * P:3 * P], gate_w[:, k], xn3T[:, k], start=(k == 0), stop=(k == DC - 1))
                last.then_inc(s["logitsT_ps"], 1)

            def logits(c):
                wait_apart(pe, s["logitsT_ready"], c.count(), pe_passed)
                nc.tensor.transpose(gp[:, 3 * P:3 * P + E], logitsT[:], ident[0:E, 0:E]).then_inc(s["logits_ps"], 1)

            def ranks(c):
                wait(pe, s["routed_sum"], c.count(1))
                pe.wait_ge(s["routed_ready"], c.count())
                rank = gp[:, 3 * P + E:3 * P + 2 * E]
                mm(rank, earlier[:], routed[:], start=True, stop=False)
                mm(rank, ones[:], routed_before[:, c.p], start=False, stop=True).then_inc(s["rank_ps"], 1)

            def cross_scores(a):
                pe.wait_ge(s["qkT_ready"], a.count())
                pe.wait_ge(s["ctxT_ready"], a.count() * 5)
                for k in range(DC):
                    for j in range(GB):
                        last = mm(xa[0][T * j:T * j + T, 0:S], qkT[:, k, T * j:T * j + T], ctxT[:, a.p, j, k],
                                  start=(k == 0), stop=(k == DC - 1), tile_position=(0, T * j))
                last.then_inc(s["scores"], 1)

            def cross_probsT(a):
                pe.wait_ge(s["probs_ready"], a.count())
                transposes(xa[1], probs[:], SK).then_inc(s["probsT_ps"], 1)

            def cross_mix(a):
                pe.wait_ge(s["probsT_ready"], a.count())
                for k in range(SK):
                    for j in range(GB):
                        last = mm(xa[0][T * j:T * j + T, 0:D], probsT[:, k, T * j:T * j + T], ctx_in[:, a.p, j, k],
                                  start=(k == 0), stop=(k == SK - 1), tile_position=(0, T * j))
                last.then_inc(s["mix_ps"], 1)

            def cross_mixT(a):
                pe.wait_ge(s["mix_ready"], a.count())
                transposes(xa[0], mix[:]).then_inc(s["mixT_ps"], 1)

            def cross_out(a):
                if isinstance(a.i, int) and a.index() == 0:
                    pe.wait_ge(sw_in, 16 * 8)
                pe.wait_ge(s["mixT_ready"], a.count())
                for k in range(DC):
                    last = mm(xa[1][:, 0:D], mixT[:, k], w_xv[:, k], start=(k == 0), stop=(k == DC - 1))
                last.then_inc(s["xv_ps"], 1)

            def spread_values(b, n):
                if n == 0:
                    pe.wait_ge(s["vT_ready"], b.count())
                else:
                    pe.wait_ge(s["v_heads_ready"], b.count(1) * 2 + 1)
                for j in range(2):
                    for k in range(DC):
                        last = nc.tensor.transpose(sa[1][:, j * D + k * P:j * D + (k + 1) * P],
                                                   vT[:, k, 2 * n + j].rearrange("p r t -> p (r t)"), ident)
                last.then_inc(s["vrep_ps"], 1)

            def self_scores(b):
                pe.wait_ge(s["qT_ready"], b.count())
                pe.wait_ge(s["k_heads0"], b.count())
                pe.wait_ge(s["k_heads1"], b.count())
                pe.wait_ge(s["k_heads2"], b.count())
                for k in range(DC):
                    for j in range(GB):
                        last = mm(sa[0][T * j:T * j + T, k * HC * T:(k + 1) * HC * T], qT[:, k, T * j:T * j + T],
                                  k_heads[:, k, j], start=True, stop=True, tile_position=(0, T * j))
                last.then_inc(s["att_ps"], 1)

            def self_weightsT(d):
                wait(pe, s["x2_ready"], d.count(1))
                pe.wait_ge(s["att_exp_ready"], d.count())
                transposes(sa[2], att_exp[:].rearrange("p h k -> p (h k)"), H // HQ).then_inc(s["attT_ps"], 1)

            def self_mix(d):
                pe.wait_ge(s["v_heads_ready"], d.count() * 2)
                pe.wait_ge(s["attT_ready"], d.count())
                w = HQ * (DH + 1)
                for c4 in range(H // HQ):
                    for j in range(GB):
                        last = mm(sa[2][T * j:T * j + T, c4 * w:(c4 + 1) * w], attT[:, c4, T * j:T * j + T],
                                  v_heads[:, j, c4].rearrange("p h w -> p (h w)"), start=True, stop=True, tile_position=(0, T * j))
                last.then_inc(s["y_ps"], 1)

            def self_yT(d):
                pe.wait_ge(s["y_ready"], d.count())
                transposes(sa[2], y[:]).then_inc(s["yT_ps"], 1)

            def self_out(d):
                pe.wait_ge(s["yT_ready"], d.count())
                for k in range(DC):
                    last = mm(sa[2][:, 0:D], yT[:, k], w_o[:, k], start=(k == 0), stop=(k == DC - 1))
                last.then_inc(s["o_ps"], 1)

            def slot(a, b, d, c, f):
                run((norm1T, a), (self_weightsT, d), (queries, a), (norm3T, c), (self_mix, d), (norm2T, b), (cross_scores, a),
                    (logits_rows, c), (self_yT, d), (lambda g: turn_context(g, 0), f), (projections, b), (self_out, d),
                    (logits, c), (cross_probsT, a), (lambda g: turn_context(g, 1), f), (lambda g: spread_values(g, 0), b),
                    (cross_mix, a), (lambda g: turn_context(g, 2), f), (lambda g: spread_values(g, 1), b), (cross_mixT, a),
                    (self_scores, b), (lambda g: turn_context(g, 3), f), (turn_last, f), (cross_out, a), (ranks, c))
            pipeline(pe, slot)

            pe.wait_ge(s["routed_sum"], G)
            pe.wait_ge(s["places_ready"], G)
            mm(gp[0:1, 0:E], ones[:, 0:1], routed_before[:, G % 2], start=True, stop=True).then_inc(s["counts_ps"], 1)
            for sm, n in ((w1_in, DC), (w2_in, HID // P)):
                pe.wait_ge(sm, n * 16)
            pe.wait_ge(s["table_ready"], 1)

            def expert_of(t):
                return pe.value_load(table[0:1, 0, bass.ds(t.index(), 1)], min_val=0, max_val=E - 1)

            def turn_rows(t):
                pe.wait_ge(gathered[t.third], t.third_visits() * 16)
                transposes(turn[t.pair], xg[:, t.third]).then_inc(s["xgT_ps"], 1)

            def up(t):
                e = expert_of(t)
                pe.wait_ge(s["xgT_ready"], t.count())
                for k in range(DC):
                    last = mm(xa[t.pair][:].unsqueeze(1), xgT[:, t.pair, k], w1[:, bass.ds(e, 1), k], start=(k == 0), stop=(k == DC - 1))
                last.then_inc(s["hid_ps"], 1)

            def step(t, following, after):
                pe.wait_ge(s["hid_ready"], t.count())
                transposes(sa[t.pair], hid[:, t.pair], HID // P).then_inc(s["hidT_ps"], 1)
                if following is not None:
                    up(following)
                e = expert_of(t)
                pe.wait_ge(s["hidT_ready"], t.count())
                for k in range(HID // P):
                    last = mm(exp_bank[t.pair][:, 0:D].unsqueeze(1), hidT[:, t.pair, k], w2[:, bass.ds(e, 1), k], start=(k == 0), stop=(k == HID // P - 1))
                last.then_inc(s["exp_ps"], 1)
                if after is not None:
                    turn_rows(after)

            turn_rows(Tile(0, 0))
            turn_rows(Tile(0, 1))
            up(Tile(0, 0))
            tiles(pe, step)


def kernel(x, ctx_1024, L0_xattn_Wq, L0_xattn_bq, L0_xattn_Wk, L0_xattn_bk, L0_xattn_Wv, L0_xattn_bv,
           L0_attn_Wq, L0_attn_bq, L0_attn_Wk, L0_attn_bk, L0_attn_Wv, L0_attn_bv, L0_attn_Wo, L0_attn_bo,
           L0_ffn_gate_W, L0_ffn_W1, L0_ffn_b1, L0_ffn_W2, L0_ffn_b2):
    from concourse import bacc
    from concourse.bass_utils import run_bass_kernel_spmd

    arrays = {
        "x": np.asarray(x).reshape(N, D), "ctx": ctx_1024,
        "consts": shape_constants(), "slots_init": empty_slots(),
        "xWq": L0_xattn_Wq, "xbq": L0_xattn_bq, "xWk": L0_xattn_Wk, "xbk": L0_xattn_bk,
        "xWvT": np.asarray(L0_xattn_Wv).T, "xbv": L0_xattn_bv,
        "WqT": np.asarray(L0_attn_Wq).T, "bq": L0_attn_bq, "WkT": np.asarray(L0_attn_Wk).T, "bk": L0_attn_bk,
        "WvT": np.asarray(L0_attn_Wv).T, "bv": L0_attn_bv, "WoT": np.asarray(L0_attn_Wo).T, "bo": L0_attn_bo,
        "gate_W": L0_ffn_gate_W, "W1": L0_ffn_W1, "b1": L0_ffn_b1, "W2": L0_ffn_W2, "b2": L0_ffn_b2,
    }
    nc = bacc.Bacc("TRN2", target_bir_lowering=False, num_devices=1)
    in_map, args = {}, []
    for name, a in arrays.items():
        a = np.ascontiguousarray(a)
        in_map[f"in_{name}"] = a
        args.append(nc.dram_tensor(f"in_{name}", a.shape, mybir.dt.from_np(a.dtype), kind="ExternalInput").ap())
    out = nc.dram_tensor("out", (N + P, D), F32, kind="ExternalOutput").ap()
    perceiver_layer(nc, *args, out)
    r = run_bass_kernel_spmd(nc, [in_map], core_ids=[0])
    return r.results[0]["out"][:N].reshape(B, T, D)
```

```python
from contextlib import ExitStack

import numpy as np

import concourse.bass as bass
from concourse import mybir

ALU = mybir.AluOpType
ACT = mybir.ActivationFunctionType
AX = mybir.AxisListType
F32 = mybir.dt.float32
BF16 = mybir.dt.bfloat16
I32 = mybir.dt.int32
U32 = mybir.dt.uint32

P = 128
B, T, D = 64, 32, 256
S = 257
H, DH = 16, 16
E, HID = 8, 512
N = B * T
GB = P // T
G = N // P
DC = D // P
SK = (S - 1) // P
HC = P // DH
HQ = P // T
TOP = 2
TILES = (N * TOP - E) // P + E
LOOK = 8
RING = 4
TABLE = -(-TILES // LOOK) * LOOK
SLOTS = E * N + TABLE * P
ROPE_BASE = 10000.0
LN_EPS = 1e-5
MASKED = -1e30

C_IDENT = 0
C_ROPE = C_IDENT + P
C_HEAD = C_ROPE + T
C_VHEAD = C_HEAD + HC
C_CAUSAL = C_VHEAD + HQ
C_EXPERT = C_CAUSAL + T
C_FIRST = C_EXPERT + E
C_TOKEN = C_FIRST + E
C_TILE = C_TOKEN + 1
C_FULL = C_TILE + TABLE
C_EARLIER = C_FULL + N // P
C_UP_TO = C_EARLIER + P
C_END = C_UP_TO + E * E


def shape_constants():
    c = np.zeros((P, C_END), np.float32)
    p = np.arange(P)
    c[:, C_IDENT:C_IDENT + P] = np.eye(P)
    t = np.arange(T)[None, :]
    theta = t * ROPE_BASE ** (-2.0 * (p % (DH // 2))[:, None] / DH)
    c[:, C_ROPE:C_ROPE + T] = np.cos(theta) + np.sin(theta)
    c[:, C_HEAD:C_HEAD + HC] = (p // DH)[:, None] == np.arange(HC)[None, :]
    c[:, C_VHEAD:C_VHEAD + HQ] = (p // T)[:, None] == np.arange(HQ)[None, :]
    c[:, C_CAUSAL:C_CAUSAL + T] = np.where(np.arange(T)[None, :] > (p % T)[:, None], MASKED, 0.0)
    c[:, C_EXPERT:C_EXPERT + E] = np.arange(E)
    c[:, C_FIRST:C_FIRST + E] = np.arange(E) * N
    c[:, C_TOKEN] = p
    c[:, C_TILE:C_TILE + TABLE] = np.arange(TABLE)
    c[:, C_FULL:C_FULL + N // P] = np.arange(N // P) * P
    c[:, C_EARLIER:C_EARLIER + P] = p[:, None] < p[None, :]
    c[:, C_UP_TO:C_END] = np.tri(E).reshape(1, E * E)
    return c


def empty_slots():
    slots = np.zeros((SLOTS, 2), np.int32)
    slots[:, 0] = N + np.arange(SLOTS) % P
    return slots


class Group:

    def __init__(self, i, c):
        self.i, self.c, self.p = i, c, c % 2

    def count(self, before=0):
        return self.i * 2 + (self.c + 1 - before)

    def visits(self):
        return self.i + (self.c // 2 + 1)

    def index(self):
        return self.i * 2 + self.c


class Tile:

    def __init__(self, i, c):
        self.i, self.c, self.pair, self.ring, self.slot = i, c, c % 2, c % RING, c % LOOK

    def index(self):
        return self.i * LOOK + self.c

    def count(self, before=0):
        return self.i * LOOK + (self.c + 1 - before)

    def ring_visits(self):
        return self.i * (LOOK // RING) + (self.c // RING + 1)

    def slot_visits(self):
        return self.i + (self.c // LOOK + 1)

    def ahead(self, n):
        return Tile(self.i, self.c + n)


def tiles(engine, step):
    whole = (TILES - RING) // LOOK
    for c in range(LOOK):
        t = Tile(0, c)
        step(t, *(t.ahead(k) for k in (1, 2, RING)))
    with engine.Fori(1, whole) as i:
        for c in range(LOOK):
            t = Tile(i, c)
            step(t, *(t.ahead(k) for k in (1, 2, RING)))
    for n in range(whole * LOOK, TILES):
        t = Tile(n // LOOK, n % LOOK)
        step(t, *(t.ahead(k) if n + k < TILES else None for k in (1, 2, RING)))


def wait(engine, semaphore, value):
    if not (isinstance(value, int) and value <= 0):
        engine.wait_ge(semaphore, value)


def pipeline(engine, slot):
    def groups(i, u, known):
        return [Group(i, u - lag) if not known or 0 <= 2 * i + u - lag < G else None for lag in (0, 1, 2, 3, -1)]

    for t in range(4):
        slot(*groups(t // 2, t % 2, True))
    with engine.Fori(2, G // 2 - 1) as i:
        for u in range(2):
            slot(*groups(i, u, False))
    for t in range(G - 2, G + 3):
        slot(*groups(t // 2, t % 2, True))


def run(*steps):
    for step, group in steps:
        if group is not None:
            step(group)


def wait_apart(engine, semaphore, value, passed):
    wait(engine, semaphore, value)
    if not isinstance(value, int):
        engine.sem_inc(passed, 1)


def perceiver_layer(nc, x, ctx, consts, slots_init, xWq, xbq, xWk, xbk, xWvT, xbv, WqT, bq, WkT, bk, WvT, bv, WoT, bo,
                    gate_W, W1, b1, W2, b2, out):
    SCALE = float(D) ** -0.5
    ATT_SCALE = float(DH) ** -0.5

    with ExitStack() as stack:
        slots = nc.dram_tensor("slots", (SLOTS, 2), I32, kind="Internal").ap()
        normed_rows = nc.dram_tensor("normed_rows", (N + P, D), F32, kind="Internal").ap()

        def sb(name, shape, dt=F32):
            return stack.enter_context(nc.sbuf_tensor(name, shape, dt))

        def ps(name, shape=(P, 512), dt=F32):
            return stack.enter_context(nc.psum_tensor(name, list(shape), dt))

        def sem(name):
            return stack.enter_context(nc.semaphore(name))

        cst = sb("cst", [P, C_END])
        ident = cst[:, C_IDENT:C_IDENT + P]
        rope = cst[:, C_ROPE:C_ROPE + T]
        head_mask = cst[:, C_HEAD:C_HEAD + HC]
        vhead_mask = cst[:, C_VHEAD:C_VHEAD + HQ]
        causal = cst[:, C_CAUSAL:C_CAUSAL + T]
        raw_wq = sb("raw_wq", [P, DC, D])
        raw_wk = sb("raw_wk", [P, DC, D])
        raw_b = sb("raw_b", [P, 2, DC])
        wqk = sb("wqk", [P, DC, D])
        wqbk_rows = sb("wqbk_rows", [P, D])
        bqbk = sb("bqbk", [P, 1])
        bqk = sb("bqk", [P, DC])
        w_xv = sb("w_xv", [P, DC, D])
        w_q = sb("w_q", [P, DC, D])
        w_k = sb("w_k", [P, DC, D])
        w_v = sb("w_v", [P, DC, D])
        w_o = sb("w_o", [P, DC, D])
        b_cols = sb("b_cols", [P, 3, DC])
        xbv_rows = sb("xbv_rows", [P, D])
        bo_rows = sb("bo_rows", [P, D])
        power = sb("power", [P, 1])
        eps = sb("eps", [P, 1])

        x_in = sb("x_in", [P, 2, D])
        ctx_in = sb("ctx_in", [P, 2, GB, SK, D])
        ctx_last = sb("ctx_last", [P, 2, D])
        stats = sb("stats", [P, 3, 6])
        mean_var = sb("mean_var", [P, 3, 2])
        var_eps = sb("var_eps", [P, 3, 1])
        rstd = sb("rstd", [P, 3, 1])
        xn1 = sb("xn1", [P, 2, D])
        xn1T = sb("xn1T", [P, DC, P])
        x_bv = sb("x_bv", [P, 2, D])
        xn1_bk = sb("xn1_bk", [P, D])
        qbk = sb("qbk", [P, 2, 2])
        qkT = sb("qkT", [P, DC, P])
        ctxT = sb("ctxT", [P, 2, GB, DC, S])
        smax = sb("smax", [P, 1])
        ebias = sb("ebias", [P, 1])
        probs = sb("probs", [P, S])
        ssum = sb("ssum", [P, 2])
        probsT = sb("probsT", [P, SK, P])
        mix = sb("mix", [P, D])
        mixT = sb("mixT", [P, DC, P])
        x1 = sb("x1", [P, 2, D])
        xn2 = sb("xn2", [P, D])
        xn2T = sb("xn2T", [P, DC, P])
        x1_bo = sb("x1_bo", [P, 2, D])
        qT = sb("qT", [P, DC, P])
        kT = sb("kT", [P, DC, P])
        vT = sb("vT", [P, DC, GB, HQ, T])
        k_heads = sb("k_heads", [P, DC, GB, HC * T])
        v_heads = sb("v_heads", [P, GB, H // HQ, HQ, DH + 1])
        att = sb("att", [P, H, T])
        att_max = sb("att_max", [P, H])
        att_sub = sb("att_sub", [P, H, T])
        att_exp = sb("att_exp", [P, H, T])
        att_scale = sb("att_scale", [P, H])
        attT = sb("attT", [P, H // HQ, P])
        y = sb("y", [P, D])
        yT = sb("yT", [P, DC, P])
        x2 = sb("x2", [P, 2, D])
        xn3 = sb("xn3", [P, 2, D])
        x3 = sb("x3", [P, 2, D])

        xn3T = sb("xn3T", [P, DC, P])
        gate_w = sb("gate_w", [P, DC, E])
        logitsT = sb("logitsT", [E, P])
        logit_bias = sb("logit_bias", [P, 1])
        gate_exp = sb("gate_exp", [P, E])
        gate_sum = sb("gate_sum", [P, 2])
        gates = sb("gates", [P, E])
        top_gates = sb("top_gates", [P, 8])
        top_experts = sb("top_experts", [P, 8], U32)
        top_expert = sb("top_expert", [P, TOP])
        top_sum = sb("top_sum", [P, 2])
        chosen = sb("chosen", [P, TOP, E])
        routed = sb("routed", [P, E], BF16)
        routed_before = sb("routed_before", [P, 2, E], BF16)
        earlier = sb("earlier", [P, P], BF16)
        ones = sb("ones", [P, P], BF16)
        places = sb("places", [P, E])
        own_place = sb("own_place", [P, TOP, E])
        place = sb("place", [P, TOP])
        place_slot = sb("place_slot", [P, TOP], I32)
        token = sb("token", [P, 2])
        slot_row = sb("slot_row", [P, TOP, 2], I32)
        counts = sb("counts", [1, E])
        started = sb("started", [1, E, N // P])
        tile_count = sb("tile_count", [1, E])
        up_to = sb("up_to", [1, E, E])
        tile_end = sb("tile_end", [1, E])
        row_skip = sb("row_skip", [1, E])
        passed = sb("passed", [1, TABLE, E])
        passed_rows = sb("passed_rows", [1, TABLE, E])
        tile_expert = sb("tile_expert", [1, 2, TABLE])
        tile_row = sb("tile_row", [1, 2, TABLE])
        table = sb("table", [1, 2, TABLE], I32)
        w1 = sb("w1", [P, E, DC, HID])
        w2 = sb("w2", [P, E, HID // P, D])
        b1_cols = sb("b1_cols", [P, E, HID // P])
        w1_now = sb("w1_now", [P, 2, DC, HID])
        b2_rows = sb("b2_rows", [P, E, D])
        ids = sb("ids", [P, LOOK, 2], I32)
        reused = ctxT[:].rearrange("p g b c s -> p (g b c s)")
        widths = (RING * D, 2 * D, 2 * D, 2 * HID, 2 * HID)
        xg, xgT, exp_out, hid, hid_relu = (reused[:, sum(widths[:n]):sum(widths[:n + 1])] for n in range(len(widths)))
        xg = xg.rearrange("p (t d) -> p t d", t=RING)
        xgT = xgT.rearrange("p (t c n) -> p t c n", t=2, c=DC)
        exp_out = exp_out.rearrange("p (t d) -> p t d", t=2)
        hid = hid.rearrange("p (t c n) -> p t c n", t=2, c=HID // P)
        hid_relu = hid_relu.rearrange("p (t c n) -> p t c n", t=2, c=HID // P)
        exp_scaled = sb("exp_scaled", [P, 2, D])

        turn = [ps("turn0"), ps("turn1")]
        xa = [ps("xa0"), ps("xa1")]
        sa = [ps("sa0"), ps("sa1"), ps("sa2")]
        gp = ps("gp")
        exp_bank = [sa[2], gp]

        consts_in, xw_in, xb_in, sw_in, rows_in = (sem(n) for n in ("consts_in", "xw_in", "xb_in", "sw_in", "rows_in"))
        x_loaded = [sem("x_loaded0"), sem("x_loaded1")]
        ctx_loaded = [sem("ctx_loaded0"), sem("ctx_loaded1")]
        out_stored = [sem("out_stored0"), sem("out_stored1")]
        ones_set, power_set, fused, fused_copied, fused_bias, bias_copied = (
            sem(n) for n in ("ones_set", "power_set", "fused", "fused_copied", "fused_bias", "bias_copied"))
        names = ("stats1 mv1 eps1 rstd1 xn1 xn1T_ps xn1T_ready x_bv_ready qbk0 qbk_ready qkT_ps qkT_ready "
                 "turned ctxT_ready scores smax_ready ebias_ready probs_ready recip1 probsT_ps probsT_ready "
                 "mix_ps mix_ready mixT_ps mixT_ready xv_ps x1_ready "
                 "stats2 mv2 eps2 rstd2 xn2_ready xn2T_ps xn2T_ready x1_bo_ready qk_ps v_ps qT_ready kT_ready vT_ready "
                 "k_heads0 k_heads1 k_heads2 vrep_ps v_heads_ready att_ps att_masked att_max_ready att_sub_ready att_exp_ready "
                 "att_scale_ready attT_ps attT_ready y_ps y_ready yT_ps yT_ready o_ps x2_ready "
                 "stats3 mv3 eps3 rstd3 xn3_ready x3_ready "
                 "xn3T_ps xn3T_ready logitsT_ps logitsT_ready logits_ps logit_bias_ready gate_exp_ready "
                 "gate_recip gates_ready top_gates_ready top_index top_expert_ready chosen_ready routed_ready "
                 "routed_sum rank_ps places_ready place_ready place_slot_ready top_sum_ready top_recip row_ready token_ready "
                 "counts_ps counts_ready started_ready tile_count_ready up_to_ready tile_end_ready row_skip_ready passed_ready "
                 "passed_rows_ready tile_sums table_ready "
                 "xgT_ps xgT_ready w1_ready hid_ps hid_biased hid_ready exp_ps exp_out_ready exp_scaled_ready")
        rows_stored = [sem("rows_stored0"), sem("rows_stored1")]
        slots_empty, spare_set, spare_stored, gate_in, w1_in, w2_in, exp_b_in, tri_ready = (
            sem(n) for n in ("slots_empty", "spare_set", "spare_stored", "gate_in", "w1_in", "w2_in", "exp_b_in", "tri_ready"))
        scattered = sem("scattered")
        ids_loaded = [sem(f"ids_loaded{n}") for n in range(LOOK)]
        gathered = [sem(f"gathered{n}") for n in range(RING)]
        added = sem("added")
        dve_passed, pool_passed, pe_passed = sem("dve_passed"), sem("pool_passed"), sem("pe_passed")
        s = {n: sem(n) for n in names.split()}
        block = stack.enter_context(nc.Block())

        def as_heads(ap, h, w):
            return ap.rearrange("p (h w) -> p h w", h=h, w=w)

        @block.sync
        def _(sp):
            sp.dma_start(raw_wq[:], xWq.rearrange("(c p) d -> p c d", p=P)).then_inc(xw_in, 16)
            sp.dma_start(raw_wk[:], xWk.rearrange("(c p) d -> p c d", p=P)).then_inc(xw_in, 16)

            def load_x(g):
                sp.dma_start(x_in[:, g.p], x[bass.ds(g.index() * P, P)]).then_inc(x_loaded[g.p], 16)

            def load_context(g):
                src = ctx[bass.ds(g.index() * GB, GB)]
                sp.dma_start(ctx_in[:, g.p].rearrange("p b s d -> p b (s d)"),
                             src[:, 0:S - 1].rearrange("b (p s) d -> p b (s d)", s=SK)).then_inc(ctx_loaded[g.p], 16)
                sp.dma_start(ctx_last[:, g.p],
                             src[:, S - 1:S].broadcast_to([GB, T, D])).then_inc(ctx_loaded[g.p], 16)

            def load(g):
                if not (isinstance(g.i, int) and g.index() < 2):
                    sp.wait_ge(s["x1_ready"], g.count(2))
                load_x(g)
                load_context(g)

            with nc.allow_non_contiguous_dma(reason="bias columns"):
                sp.dma_start(raw_b[:, 0], xbq.rearrange("(c p) -> p c", p=P)).then_inc(xb_in, 16)
                sp.dma_start(raw_b[:, 1], xbk.rearrange("(c p) -> p c", p=P)).then_inc(xb_in, 16)
            load_x(Group(0, 0))
            sp.dma_start(cst[:], consts).then_inc(consts_in, 16)
            load_context(Group(0, 0))
            for w, src in ((w_xv, xWvT), (w_q, WqT), (w_k, WkT), (w_v, WvT), (w_o, WoT)):
                sp.dma_start(w[:], src.rearrange("(c p) d -> p c d", p=P)).then_inc(sw_in, 16)
            with nc.allow_non_contiguous_dma(reason="bias columns"):
                for j, src in enumerate((bq, bk, bv)):
                    sp.dma_start(b_cols[:, j], src.rearrange("(c p) -> p c", p=P)).then_inc(sw_in, 16)
            sp.dma_start(xbv_rows[:], xbv.unsqueeze(0).broadcast_to([P, D])).then_inc(rows_in, 16)
            sp.dma_start(bo_rows[:], bo.unsqueeze(0).broadcast_to([P, D])).then_inc(rows_in, 16)
            sp.dma_start(gate_w[:], gate_W.rearrange("(c p) e -> p c e", p=P)).then_inc(gate_in, 16)
            sp.dma_start(slots.rearrange("(a b) c -> a (b c)", a=P), slots_init.rearrange("(a b) c -> a (b c)", a=P)).then_inc(slots_empty, 16)
            load(Group(0, 1))
            with nc.allow_non_contiguous_dma(reason="bias columns"):
                for m in range(HID // P):
                    sp.dma_start(b1_cols[:, :, m], b1[:, m * P:(m + 1) * P].rearrange("e p -> p e")).then_inc(exp_b_in, 16)
            sp.wait_ge(spare_set, 1)
            sp.dma_start(out[N:N + P], exp_scaled[:, 0]).then_inc(spare_stored, 16)
            sp.dma_start(normed_rows[N:N + P], exp_scaled[:, 0]).then_inc(spare_stored, 16)

            def store(d):
                sp.wait_ge(s["xn3_ready"], d.count())
                sp.dma_start(normed_rows[bass.ds(d.index() * P, P)], xn3[:, d.p]).then_inc(rows_stored[d.p], 16)
                sp.wait_ge(s["x3_ready"], d.count())
                sp.dma_start(out[bass.ds(d.index() * P, P)], x3[:, d.p]).then_inc(out_stored[d.p], 16)

            def load_expert(a):
                src, w, weights_in = (W1, w1, w1_in) if a.p == 0 else (W2, w2, w2_in)
                e = bass.ds(a.i + a.c // 2, 1)
                sp.dma_start(w[:, e].rearrange("p e c n -> p (e c) n"), src[e].rearrange("e (c p) n -> p (e c) n", p=P)).then_inc(weights_in, 16)
                if a.p == 1:
                    sp.dma_start(b2_rows[:, e].rearrange("p e n -> p (e n)"), b2[e].broadcast_to([P, D])).then_inc(exp_b_in, 16)

            def slot(a, b, d, c, f):
                run((store, d))
                if a is not None and not (isinstance(a.i, int) and a.index() + 2 >= G):
                    load(Group(a.i, a.c + 2))
                run((load_expert, a))
            pipeline(sp, slot)

            sp.wait_ge(s["table_ready"], 1)

            def first_slot(t):
                return sp.value_load(table[0:1, 1, bass.ds(t.index(), 1)], min_val=0, max_val=SLOTS - P)

            def load_ids(t, first):
                sp.dma_start(ids[:, t.slot], slots[bass.ds(first, P)]).then_inc(ids_loaded[t.slot], 16)

            first = first_slot(Tile(0, 0))
            sp.wait_ge(scattered, 16 * TOP * G)
            load_ids(Tile(0, 0), first)
            for n in range(1, LOOK):
                load_ids(Tile(0, n), first_slot(Tile(0, n)))

            with sp.Fori(0, (TABLE - LOOK) // LOOK) as i:
                for c in range(LOOK):
                    t = Tile(i, c)
                    sp.wait_ge(added, t.count() * 16)
                    load_ids(t.ahead(LOOK), first_slot(t.ahead(LOOK)))
            for n in range(TILES, TABLE):
                sp.wait_ge(ids_loaded[n % LOOK], 16 * (TABLE // LOOK))
            sp.wait_ge(added, 16 * TILES)

        @block.gpsimd
        def _(pool):
            nc.gpsimd.memset(ones[:], 1.0).then_inc(ones_set, 1)
            nc.gpsimd.memset(eps[:], LN_EPS)
            nc.gpsimd.memset(power[:], -0.5).then_inc(power_set, 1)
            pool.wait_ge(power_set, 1)
            nc.gpsimd.memset(exp_scaled[:, 0], 0.0).then_inc(spare_set, 1)
            nc.gpsimd.memset(routed_before[:], 0.0)
            pool.wait_ge(consts_in, 16)
            nc.gpsimd.tensor_copy(earlier[:], cst[:, C_EARLIER:C_EARLIER + P]).then_inc(tri_ready, 1)

            def rstd_of(g, n):
                pool.wait_ge(s[f"mv{n}"], g.count())
                nc.gpsimd.tensor_tensor(var_eps[:, n - 1], mean_var[:, n - 1, 1:2], eps[:], ALU.add).then_inc(s[f"eps{n}"], 1)
                pool.wait_ge(s[f"eps{n}"], g.count())
                nc.gpsimd.tensor_tensor(rstd[:, n - 1], var_eps[:, n - 1], power[:], ALU.pow).then_inc(s[f"rstd{n}"], 1)

            def residual1(g):
                pool.wait_ge(x_loaded[g.p], g.visits() * 16)
                nc.gpsimd.tensor_tensor(x_bv[:, g.p], x_in[:, g.p], xbv_rows[:], ALU.add).then_inc(s["x_bv_ready"], 1)

            rstd_of(Group(0, 0), 1)
            pool.wait_ge(rows_in, 32)
            residual1(Group(0, 0))

            def key_heads(b):
                pool.wait_ge(s["kT_ready"], b.count())
                nc.gpsimd.tensor_tensor(
                    k_heads[:, 1].rearrange("p b (h k) -> p b h k", h=HC)[:, :, 0:HC // 2],
                    kT[:, 1].rearrange("p (b k) -> p b k", b=GB).unsqueeze(2).broadcast_to([P, GB, HC // 2, T]),
                    head_mask[:, 0:HC // 2].unsqueeze(1).unsqueeze(3).broadcast_to([P, GB, HC // 2, T]), ALU.mult).then_inc(s["k_heads1"], 1)

            def less_largest(b):
                pool.wait_ge(s["att_max_ready"], b.count())
                nc.gpsimd.tensor_tensor(att_sub[:], att[:], att_max[:].unsqueeze(2).broadcast_to([P, H, T]),
                                        ALU.subtract).then_inc(s["att_sub_ready"], 1)

            def residual2(a):
                pool.wait_ge(s["x1_ready"], a.count())
                nc.gpsimd.tensor_tensor(x1_bo[:, a.p], x1[:, a.p], bo_rows[:], ALU.add).then_inc(s["x1_bo_ready"], 1)

            def residual3(d):
                pool.wait_ge(s["xn3_ready"], d.count())
                if not (isinstance(d.i, int) and d.index() < 2):
                    pool.wait_ge(out_stored[d.p], d.visits() * 16 - 16)
                nc.gpsimd.tensor_tensor(x3[:, d.p], x2[:, d.p], xn3[:, d.p], ALU.add).then_inc(s["x3_ready"], 1)

            def scatter(c):
                if isinstance(c.i, int) and c.index() == 0:
                    pool.wait_ge(slots_empty, 16)
                pool.wait_ge(s["row_ready"], c.count())
                wait_apart(pool, s["place_slot_ready"], c.count(), pool_passed)
                for k in range(TOP):
                    nc.gpsimd.indirect_dma_start(
                        out=slots, out_offset=bass.IndirectOffsetOnAxis(ap=place_slot[:, k:k + 1], axis=0),
                        in_=slot_row[:, k], in_offset=None).then_inc(scattered, 16)

            def slot(a, b, d, c, f):
                run((key_heads, b), (lambda g: rstd_of(g, 1), f), (lambda g: rstd_of(g, 3), d), (less_largest, b), (residual3, d),
                    (residual1, f), (lambda g: rstd_of(g, 2), a), (residual2, a), (scatter, c))
            pipeline(pool, slot)

            for sm in rows_stored + out_stored:
                pool.wait_ge(sm, 16 * (G // 2))
            pool.wait_ge(spare_stored, 32)

            def gather(t):
                wait_apart(pool, ids_loaded[t.slot], t.slot_visits() * 16, pool_passed)
                nc.gpsimd.indirect_dma_start(
                    out=xg[:, t.ring], out_offset=None, in_=normed_rows,
                    in_offset=bass.IndirectOffsetOnAxis(ap=ids[:, t.slot, 0:1], axis=0)).then_inc(gathered[t.ring], 16)

            for n in range(RING):
                gather(Tile(0, n))

            def step(t, following, after, ahead):
                if ahead is not None:
                    pool.wait_ge(s["xgT_ps"], t.count())
                    gather(ahead)
                pool.wait_ge(s["exp_scaled_ready"], t.count())
                wait_apart(pool, added, t.count(1) * 16, pool_passed)
                nc.gpsimd.indirect_dma_start(
                    out=out, out_offset=bass.IndirectOffsetOnAxis(ap=ids[:, t.slot, 0:1], axis=0),
                    in_=exp_scaled[:, t.pair], in_offset=None, compute_op=ALU.add).then_inc(added, 16)
            tiles(pool, step)

        @block.scalar
        def _(act):
            act.wait_ge(fused, 1)
            nc.scalar.activation(wqk[:], xa[0][:].rearrange("p (c d) -> p c d", c=DC), ACT.Copy, scale=SCALE).then_inc(fused_copied, 1)

            def copy_out(dst, bank, cols, ready, done, g):
                act.wait_ge(s[ready], g.count())
                nc.scalar.copy(dst, bank[:, 0:cols]).then_inc(s[done], 1)

            def with_bias(dst, bank, bias, ready, done, g):
                act.wait_ge(s[ready], g.count())
                for c in range(DC):
                    last = nc.scalar.activation(dst[:, c], bank[:, c * P:(c + 1) * P], ACT.Identity, bias=bias[:, c:c + 1])
                last.then_inc(s[done], 1)

            def turned(g, b):
                act.wait_ge(s["turned"], g.count(1) * 5 + (b + 1))
                nc.scalar.copy(ctxT[:, g.p, b, :, 0:S - 1], turn[b % 2][:].rearrange("p (c k) -> p c k", c=DC)).then_inc(s["ctxT_ready"], 1)

            def turned_last(g):
                act.wait_ge(s["turned"], g.count(1) * 5 + 5)
                nc.scalar.copy(ctxT[:, g.p, :, :, S - 1],
                               turn[0][:, 0:2 * P].rearrange("p (c b t) -> p b c t", c=DC, b=GB)[:, :, :, 0]).then_inc(s["ctxT_ready"], 1)

            for b in range(GB):
                turned(Group(0, 0), b)
            turned_last(Group(0, 0))

            def flat(ap):
                return ap[:].rearrange("p c t -> p (c t)")

            def norm1T(a):
                copy_out(flat(xn1T), xa[0], D, "xn1T_ps", "xn1T_ready", a)

            def norm2T(b):
                copy_out(flat(xn2T), sa[0], D, "xn2T_ps", "xn2T_ready", b)

            def norm3T(c):
                copy_out(flat(xn3T), gp, D, "xn3T_ps", "xn3T_ready", c)

            def queries(a):
                if isinstance(a.i, int) and a.index() == 0:
                    act.wait_ge(bias_copied, 3)
                with_bias(qkT, xa[1], bqk, "qkT_ps", "qkT_ready", a)

            def values(b):
                if isinstance(b.i, int) and b.index() == 0:
                    act.wait_ge(sw_in, 16 * 8)
                act.wait_ge(s["v_ps"], b.count())
                for k in range(DC):
                    last = nc.scalar.activation(
                        vT[:, k], sa[1][:, k * P:(k + 1) * P].rearrange("p (b t) -> p b t", b=GB).unsqueeze(2).broadcast_to([P, GB, HQ, T]),
                        ACT.Identity, bias=b_cols[:, 2, k:k + 1])
                last.then_inc(s["vT_ready"], 1)

            def key_heads(b):
                act.wait_ge(s["kT_ready"], b.count())
                for h in range(HC // 2, HC):
                    last = nc.scalar.activation(k_heads[:, 1, :, h * T:(h + 1) * T], kT[:, 1].rearrange("p (b k) -> p b k", b=GB),
                                                ACT.Copy, scale=head_mask[:, h:h + 1])
                last.then_inc(s["k_heads2"], 1)

            def cross_exp(a):
                act.wait_ge(s["ebias_ready"], a.count())
                nc.scalar.activation(probs[:], xa[0][:, 0:S], ACT.Exp, bias=ebias[:],
                                     accum_out=ssum[:, 0:1]).then_inc(s["probs_ready"], 1)

            def cross_probsT(a):
                copy_out(flat(probsT), xa[1], D, "probsT_ps", "probsT_ready", a)

            def cross_mixT(a):
                copy_out(flat(mixT), xa[0], D, "mixT_ps", "mixT_ready", a)

            def gates_exp(c):
                act.wait_ge(s["logit_bias_ready"], c.count())
                nc.scalar.activation(gate_exp[:], gp[:, 3 * P:3 * P + E], ACT.Exp, bias=logit_bias[:],
                                     accum_out=gate_sum[:, 0:1]).then_inc(s["gate_exp_ready"], 1)

            def self_exp(b):
                act.wait_ge(s["att_sub_ready"], b.count())
                nc.scalar.activation(att_exp[:], att_sub[:], ACT.Exp, scale=ATT_SCALE).then_inc(s["att_exp_ready"], 1)

            def self_weightsT(d):
                copy_out(flat(attT), sa[2], 512, "attT_ps", "attT_ready", d)

            def self_yT(d):
                copy_out(flat(yT), sa[2], D, "yT_ps", "yT_ready", d)

            def slot(a, b, d, c, f):
                run((norm1T, a), (norm3T, c), (self_weightsT, d), (queries, a), (norm2T, b), (gates_exp, c), (self_yT, d),
                    (cross_exp, a), (values, b), (cross_probsT, a), (key_heads, b), (lambda g: turned(g, 0), f),
                    (lambda g: turned(g, 1), f), (cross_mixT, a), (lambda g: turned(g, 2), f), (lambda g: turned(g, 3), f),
                    (self_exp, b), (turned_last, f))
            pipeline(act, slot)

            def step(t, following, after, ahead):
                act.wait_ge(s["hid_biased"], t.count())
                nc.scalar.activation(hid_relu[:, t.pair], hid[:, t.pair], ACT.Relu).then_inc(s["hid_ready"], 1)
                if after is not None:
                    current_w1(after)
                    expert_xT(after)

            def current_w1(t):
                e = act.value_load(table[0:1, 0, bass.ds(t.index(), 1)], min_val=0, max_val=E - 1)
                wait(act, s["hid_ps"], t.count(2))
                nc.scalar.copy(w1_now[:, t.pair].unsqueeze(1), w1[:, bass.ds(e, 1)]).then_inc(s["w1_ready"], 1)

            def expert_xT(t):
                act.wait_ge(s["xgT_ps"], t.count())
                nc.scalar.copy(xgT[:, t.pair], turn[t.pair][:, 0:D].rearrange("p (c t) -> p c t", c=DC)).then_inc(s["xgT_ready"], 1)

            act.wait_ge(w1_in, E * 16)
            act.wait_ge(s["table_ready"], 1)
            current_w1(Tile(0, 0))
            current_w1(Tile(0, 1))
            expert_xT(Tile(0, 0))
            expert_xT(Tile(0, 1))
            tiles(act, step)

        @block.vector
        def _(dve):
            dve.wait_ge(consts_in, 16)
            nc.vector.tensor_copy(v_heads[:, :, :, :, DH].rearrange("p b c h -> p (b c) h"),
                                  vhead_mask.unsqueeze(1).broadcast_to([P, GB * H // HQ, HQ]))

            def norm(g, n, src):
                nc.vector.bn_stats(stats[:, n - 1], src).then_inc(s[f"stats{n}"], 1)

            def mean_of(g, n):
                wait_apart(dve, s[f"stats{n}"], g.count(), dve_passed)
                nc.vector.bn_aggr(mean_var[:, n - 1], stats[:, n - 1]).then_inc(s[f"mv{n}"], 1)

            def normed(g, n, src, dst, done):
                dve.wait_ge(s[f"rstd{n}"], g.count())
                nc.vector.tensor_scalar(dst, src, mean_var[:, n - 1, 0:1], rstd[:, n - 1], ALU.subtract, ALU.mult).then_inc(s[done], 1)

            def norm1(g):
                dve.wait_ge(x_loaded[g.p], g.visits() * 16)
                norm(g, 1, x_in[:, g.p])

            def normed1(g):
                normed(g, 1, x_in[:, g.p], xn1[:, g.p], "xn1")

            def bias_score(g):
                dve.wait_ge(s["xn1"], g.count())
                nc.vector.tensor_tensor_reduce(out=xn1_bk[:], in0=xn1[:, g.p], in1=wqbk_rows[:], scale=1.0, scalar=0.0,
                                               op0=ALU.mult, op1=ALU.add, accum_out=qbk[:, g.p, 0:1]).then_inc(s["qbk0"], 1)

            def bias_score_end(g):
                dve.wait_ge(s["qbk0"], g.count())
                nc.vector.tensor_tensor(qbk[:, g.p, 1:2], qbk[:, g.p, 0:1], bqbk[:], ALU.add).then_inc(s["qbk_ready"], 1)

            norm1(Group(0, 0))
            mean_of(Group(0, 0), 1)
            normed1(Group(0, 0))
            dve.wait_ge(fused_bias, 1)
            for dst, at, n in ((wqbk_rows, 0, D), (bqbk, D, 1), (bqk, D + 2, DC)):
                nc.vector.tensor_scalar(dst[:], gp[:, at:at + n], SCALE, None, ALU.mult).then_inc(bias_copied, 1)
            dve.wait_ge(bias_copied, 3)
            bias_score(Group(0, 0))
            bias_score_end(Group(0, 0))

            def rotated(g, bank, at, j, dst, done):
                for c in range(DC):
                    last = nc.vector.scalar_tensor_tensor(
                        out=dst[:, c].rearrange("p (b t) -> p b t", b=GB),
                        in0=bank[:, at + c * P:at + (c + 1) * P].rearrange("p (b t) -> p b t", b=GB),
                        scalar=b_cols[:, j, c:c + 1], in1=rope.unsqueeze(1).broadcast_to([P, GB, T]),
                        op0=ALU.add, op1=ALU.mult)
                last.then_inc(s[done], 1)

            def gate_sum_of(c):
                dve.wait_ge(s["gate_exp_ready"], c.count())
                nc.vector.reciprocal(gate_sum[:, 1:2], gate_sum[:, 0:1]).then_inc(s["gate_recip"], 1)

            def gates_of(c):
                dve.wait_ge(s["gate_recip"], c.count())
                nc.vector.tensor_scalar(gates[:], gate_exp[:], gate_sum[:, 1:2], None, ALU.mult).then_inc(s["gates_ready"], 1)

            def largest_gates(c):
                wait_apart(dve, s["gates_ready"], c.count(), dve_passed)
                nc.vector.max(top_gates[:], gates[:]).then_inc(s["top_gates_ready"], 1)

            def largest_experts(c):
                wait_apart(dve, s["top_gates_ready"], c.count(), dve_passed)
                nc.vector.max_index(top_experts[:], top_gates[:], gates[:]).then_inc(s["top_index"], 1)
                nc.vector.tensor_scalar(top_sum[:, 0:1], top_gates[:, 0:1], top_gates[:, 1:2], 1e-8, ALU.add, ALU.add).then_inc(s["top_sum_ready"], 1)

            def weights_sum(c):
                dve.wait_ge(s["top_index"], c.count())
                nc.vector.tensor_copy(top_expert[:], top_experts[:, 0:TOP]).then_inc(s["top_expert_ready"], 1)
                dve.wait_ge(s["top_sum_ready"], c.count())
                nc.vector.reciprocal(top_sum[:, 1:2], top_sum[:, 0:1]).then_inc(s["top_recip"], 1)

            def chosen_rows(c):
                dve.wait_ge(s["top_expert_ready"], c.count())
                for k in range(TOP):
                    nc.vector.tensor_scalar(chosen[:, k], cst[:, C_EXPERT:C_EXPERT + E], top_expert[:, k:k + 1], None,
                                            ALU.is_equal).then_inc(s["chosen_ready"], 1)

            def routed_rows(c):
                dve.wait_ge(s["chosen_ready"], c.count() * TOP)
                nc.vector.tensor_tensor(routed[:], chosen[:, 0], chosen[:, 1], ALU.add).then_inc(s["routed_ready"], 1)

            def slot_rows(c):
                wait(dve, scattered, c.count(1) * (16 * TOP))
                dve.wait_ge(s["top_recip"], c.count())
                nc.vector.tensor_scalar(slot_row[:, :, 1].bitcast(F32), top_gates[:, 0:TOP], top_sum[:, 1:2], None, ALU.mult)
                nc.vector.tensor_copy(slot_row[:, :, 0], token[:, 0:1].broadcast_to([P, TOP])).then_inc(s["row_ready"], 1)
                dve.wait_ge(s["routed_ready"], c.count())
                nc.vector.tensor_tensor(routed_before[:, 1 - c.p], routed_before[:, c.p], routed[:], ALU.add).then_inc(s["routed_sum"], 1)
                dve.wait_ge(s["row_ready"], c.count())
                nc.vector.tensor_scalar(token[:, 0:1], token[:, 0:1], float(P), None, ALU.add).then_inc(s["token_ready"], 1)

            def gate_places(c):
                dve.wait_ge(s["rank_ps"], c.count())
                nc.vector.tensor_tensor(places[:], gp[:, 3 * P + E:3 * P + 2 * E], cst[:, C_FIRST:C_FIRST + E], ALU.add).then_inc(s["places_ready"], 1)

            def own_places(c):
                dve.wait_ge(s["places_ready"], c.count())
                for k in range(TOP):
                    nc.vector.tensor_tensor_reduce(out=own_place[:, k], in0=chosen[:, k], in1=places[:], scale=1.0, scalar=0.0,
                                                   op0=ALU.mult, op1=ALU.add, accum_out=place[:, k:k + 1]).then_inc(s["place_ready"], 1)

            def own_slots(c):
                dve.wait_ge(s["place_ready"], c.count() * TOP)
                nc.vector.tensor_copy(place_slot[:], place[:]).then_inc(s["place_slot_ready"], 1)

            nc.vector.tensor_copy(token[:, 0:1], cst[:, C_TOKEN:C_TOKEN + 1]).then_inc(s["token_ready"], 1)

            def keys_queries(b):
                if isinstance(b.i, int) and b.index() == 0:
                    dve.wait_ge(sw_in, 16 * 8)
                dve.wait_ge(s["qk_ps"], b.count())
                rotated(b, sa[0], D, 1, kT, "kT_ready")
                rotated(b, sa[0], 0, 0, qT, "qT_ready")

            def key_heads(b):
                dve.wait_ge(s["kT_ready"], b.count())
                nc.vector.tensor_tensor(
                    k_heads[:, 0].rearrange("p b (h k) -> p b h k", h=HC),
                    kT[:, 0].rearrange("p (b k) -> p b k", b=GB).unsqueeze(2).broadcast_to([P, GB, HC, T]),
                    head_mask.unsqueeze(1).unsqueeze(3).broadcast_to([P, GB, HC, T]), ALU.mult).then_inc(s["k_heads0"], 1)

            def logits_rows(c):
                dve.wait_ge(s["logitsT_ps"], c.count())
                nc.vector.tensor_copy(logitsT[:], gp[0:E, 2 * P:3 * P]).then_inc(s["logitsT_ready"], 1)

            def cross_largest(a):
                dve.wait_ge(s["scores"], a.count())
                nc.vector.tensor_reduce(smax[:], xa[0][:, 0:S], AX.X, ALU.max, negate=True).then_inc(s["smax_ready"], 1)

            def cross_bias(a):
                dve.wait_ge(s["smax_ready"], a.count())
                nc.vector.tensor_scalar(ebias[:], smax[:], qbk[:, a.p, 1:2], qbk[:, a.p, 1:2], ALU.subtract, ALU.add).then_inc(s["ebias_ready"], 1)

            def value_heads(b, n):
                dve.wait_ge(s["vrep_ps"], b.count(1) * 2 + (n + 1))
                nc.vector.tensor_tensor(
                    v_heads[:, 2 * n:2 * n + 2, :, :, 0:DH].rearrange("p b c h w -> p (b c) h w"),
                    sa[1][:].rearrange("p (c h w) -> p c h w", h=HQ, w=DH),
                    vhead_mask.unsqueeze(1).unsqueeze(3).broadcast_to([P, 2 * H // HQ, HQ, DH]), ALU.mult).then_inc(s["v_heads_ready"], 1)

            def self_masked(b):
                dve.wait_ge(s["att_ps"], b.count())
                nc.vector.tensor_tensor(att[:], as_heads(sa[0][:], H, T), causal.unsqueeze(1).broadcast_to([P, H, T]),
                                        ALU.add).then_inc(s["att_masked"], 1)

            def self_largest(b):
                dve.wait_ge(s["att_masked"], b.count())
                nc.vector.tensor_reduce(att_max[:], att[:], AX.X, ALU.max).then_inc(s["att_max_ready"], 1)

            def logits_largest(c):
                dve.wait_ge(s["logits_ps"], c.count())
                nc.vector.tensor_reduce(logit_bias[:], gp[:, 3 * P:3 * P + E], AX.X, ALU.max, negate=True).then_inc(s["logit_bias_ready"], 1)

            def cross_sum(a):
                dve.wait_ge(s["probs_ready"], a.count())
                nc.vector.reciprocal(ssum[:, 1:2], ssum[:, 0:1]).then_inc(s["recip1"], 1)

            def cross_mix(a):
                dve.wait_ge(s["mix_ps"], a.count())
                nc.vector.scalar_tensor_tensor(out=mix[:], in0=ctx_last[:, a.p], scalar=probs[:, S - 1:S],
                                               in1=xa[0][:, 0:D], op0=ALU.mult, op1=ALU.add).then_inc(s["mix_ready"], 1)

            def cross_end(a):
                dve.wait_ge(s["recip1"], a.count())
                dve.wait_ge(s["x_bv_ready"], a.count())
                dve.wait_ge(s["xv_ps"], a.count())
                nc.vector.scalar_tensor_tensor(out=x1[:, a.p], in0=xa[1][:, 0:D], scalar=ssum[:, 1:2], in1=x_bv[:, a.p],
                                               op0=ALU.mult, op1=ALU.add).then_inc(s["x1_ready"], 1)

            def norm2(a):
                dve.wait_ge(s["x1_ready"], a.count())
                norm(a, 2, x1[:, a.p])

            def self_sums(d):
                heads = sa[2][:, 0:H * (DH + 1)].rearrange("p (h w) -> p h w", w=DH + 1)
                dve.wait_ge(s["y_ps"], d.count())
                nc.vector.reciprocal(att_scale[:], heads[:, :, DH]).then_inc(s["att_scale_ready"], 1)

            def self_scaled(d):
                heads = sa[2][:, 0:H * (DH + 1)].rearrange("p (h w) -> p h w", w=DH + 1)
                dve.wait_ge(s["att_scale_ready"], d.count())
                nc.vector.tensor_tensor(as_heads(y[:], H, DH), heads[:, :, 0:DH],
                                        att_scale[:].unsqueeze(2).broadcast_to([P, H, DH]), ALU.mult).then_inc(s["y_ready"], 1)

            def self_end(d):
                dve.wait_ge(s["x1_bo_ready"], d.count())
                dve.wait_ge(s["o_ps"], d.count())
                nc.vector.tensor_tensor(x2[:, d.p], sa[2][:, 0:D], x1_bo[:, d.p], ALU.add).then_inc(s["x2_ready"], 1)

            def norm3(d):
                dve.wait_ge(s["x2_ready"], d.count())
                norm(d, 3, x2[:, d.p])

            def normed2(a):
                normed(a, 2, x1[:, a.p], xn2[:], "xn2_ready")

            def normed3(d):
                if not (isinstance(d.i, int) and d.index() < 2):
                    dve.wait_ge(rows_stored[d.p], d.visits() * 16 - 16)
                normed(d, 3, x2[:, d.p], xn3[:, d.p], "xn3_ready")

            def slot(a, b, d, c, f):
                run((logits_rows, c), (self_sums, d), (self_scaled, d), (logits_largest, c), (gate_sum_of, c), (gates_of, c),
                    (largest_gates, c), (cross_largest, a), (norm1, f), (cross_bias, a), (largest_experts, c), (weights_sum, c),
                    (chosen_rows, c), (keys_queries, b), (self_end, d), (key_heads, b), (lambda g: value_heads(g, 0), b),
                    (norm3, d), (cross_sum, a), (cross_mix, a), (lambda g: mean_of(g, 1), f), (lambda g: mean_of(g, 3), d),
                    (self_masked, b), (routed_rows, c), (self_largest, b), (lambda g: value_heads(g, 1), b), (slot_rows, c),
                    (gate_places, c), (normed3, d), (normed1, f), (cross_end, a), (norm2, a), (bias_score, f), (bias_score_end, f),
                    (lambda g: mean_of(g, 2), a), (own_places, c), (own_slots, c), (normed2, a))
            pipeline(dve, slot)

            dve.wait_ge(s["counts_ps"], 1)
            nc.vector.tensor_copy(counts[:], sa[0][0:1, 0:E]).then_inc(s["counts_ready"], 1)
            dve.wait_ge(s["counts_ready"], 1)
            nc.vector.tensor_tensor(started[:], counts[:].unsqueeze(2).broadcast_to([1, E, N // P]),
                                    cst[0:1, C_FULL:C_FULL + N // P].unsqueeze(1).broadcast_to([1, E, N // P]),
                                    ALU.is_gt).then_inc(s["started_ready"], 1)
            dve.wait_ge(s["started_ready"], 1)
            nc.vector.tensor_reduce(tile_count[:], started[:], AX.X, ALU.add).then_inc(s["tile_count_ready"], 1)
            dve.wait_ge(s["tile_count_ready"], 1)
            nc.vector.tensor_tensor(up_to[:], tile_count[:].unsqueeze(1).broadcast_to([1, E, E]),
                                    cst[0:1, C_UP_TO:C_UP_TO + E * E].rearrange("p (a b) -> p a b", a=E), ALU.mult).then_inc(s["up_to_ready"], 1)
            dve.wait_ge(s["up_to_ready"], 1)
            nc.vector.tensor_reduce(tile_end[:], up_to[:], AX.X, ALU.add).then_inc(s["tile_end_ready"], 1)
            nc.vector.tensor_scalar(row_skip[:], tile_count[:], -float(P), float(N), ALU.mult, ALU.add).then_inc(s["row_skip_ready"], 1)
            dve.wait_ge(s["tile_end_ready"], 1)
            tile_number = cst[0:1, C_TILE:C_TILE + TABLE]
            nc.vector.tensor_tensor(passed[:], tile_number.unsqueeze(2).broadcast_to([1, TABLE, E]),
                                    tile_end[:].unsqueeze(1).broadcast_to([1, TABLE, E]), ALU.is_ge).then_inc(s["passed_ready"], 1)
            dve.wait_ge(s["passed_ready"], 1)
            dve.wait_ge(s["row_skip_ready"], 1)
            nc.vector.tensor_tensor(passed_rows[:], passed[:], row_skip[:].unsqueeze(1).broadcast_to([1, TABLE, E]),
                                    ALU.mult).then_inc(s["passed_rows_ready"], 1)
            nc.vector.tensor_reduce(tile_expert[:, 0], passed[:], AX.X, ALU.add).then_inc(s["tile_sums"], 1)
            dve.wait_ge(s["passed_rows_ready"], 1)
            nc.vector.tensor_reduce(tile_row[:, 0], passed_rows[:], AX.X, ALU.add).then_inc(s["tile_sums"], 1)
            dve.wait_ge(s["tile_sums"], 2)
            nc.vector.tensor_scalar(table[:, 0], tile_expert[:, 0], float(E - 1), None, ALU.min)
            nc.vector.scalar_tensor_tensor(out=table[:, 1], in0=tile_number, scalar=float(P), in1=tile_row[:, 0],
                                           op0=ALU.mult, op1=ALU.add).then_inc(s["table_ready"], 1)
            dve.wait_ge(s["table_ready"], 1)
            dve.wait_ge(exp_b_in, (E + HID // P) * 16)

            def expert_of(t):
                return dve.value_load(table[0:1, 0, bass.ds(t.index(), 1)], min_val=0, max_val=E - 1)

            def hidden(t):
                e = expert_of(t)
                dve.wait_ge(s["hid_ps"], t.count())
                nc.vector.tensor_tensor(hid[:, t.pair].unsqueeze(1), xa[t.pair][:].rearrange("p (e c n) -> p e c n", e=1, c=HID // P),
                                        b1_cols[:, bass.ds(e, 1)].unsqueeze(3).broadcast_to([P, 1, HID // P, P]), ALU.add).then_inc(s["hid_biased"], 1)

            def step(t, following, after, ahead):
                if following is not None:
                    hidden(following)
                e = expert_of(t)
                dve.wait_ge(s["exp_ps"], t.count())
                nc.vector.tensor_tensor(exp_out[:, t.pair].unsqueeze(1), exp_bank[t.pair][:, 0:D].unsqueeze(1), b2_rows[:, bass.ds(e, 1)], ALU.add).then_inc(s["exp_out_ready"], 1)
                dve.wait_ge(s["exp_out_ready"], t.count())
                wait(dve, added, t.count(2) * 16)
                nc.vector.tensor_scalar(exp_scaled[:, t.pair], exp_out[:, t.pair], ids[:, t.slot, 1:2].bitcast(F32), None, ALU.mult).then_inc(s["exp_scaled_ready"], 1)

            hidden(Tile(0, 0))
            tiles(dve, step)

        @block.tensor
        def _(pe):
            mm = nc.tensor.matmul

            def transposes(bank, src, n=DC):
                for c in range(n):
                    last = nc.tensor.transpose(bank[:, c * P:(c + 1) * P], src[:, c * P:(c + 1) * P], ident)
                return last

            pe.wait_ge(ones_set, 1)
            for _ in range(25):
                mm(turn[1][:, 0:P], ones[:], ones[:], start=True, stop=True)
            pe.wait_ge(xw_in, 32)
            for m in range(DC):
                for k in range(DC):
                    last = mm(xa[0][:, m * D:(m + 1) * D], raw_wq[:, k, m * P:(m + 1) * P], raw_wk[:, k], start=(k == 0), stop=(k == DC - 1))
            last.then_inc(fused, 1)
            pe.wait_ge(consts_in, 16)

            def turn_context(g, b):
                if b == 0:
                    pe.wait_ge(ctx_loaded[g.p], g.visits() * 32)
                wait(pe, s["ctxT_ready"], g.count(1) * 5 + (0, 0, 1, 2)[b])
                for c in range(DC):
                    for k in range(SK):
                        last = nc.tensor.transpose(turn[b % 2][:, (c * SK + k) * P:(c * SK + k + 1) * P],
                                                   ctx_in[:, g.p, b, k, c * P:(c + 1) * P], ident)
                last.then_inc(s["turned"], 1)

            def turn_last(g):
                pe.wait_ge(s["ctxT_ready"], g.count(1) * 5 + 3)
                transposes(turn[0], ctx_last[:, g.p]).then_inc(s["turned"], 1)

            pe.wait_ge(xb_in, 32)
            for k in range(DC):
                bk_all = raw_b[:, 1, k:k + 1].broadcast_to([P, P])
                mm(gp[:, 0:D], bk_all, raw_wq[:, k], start=(k == 0), stop=(k == DC - 1))
            for k in range(DC):
                bk_all = raw_b[:, 1, k:k + 1].broadcast_to([P, P])
                mm(gp[:, D:D + 1], bk_all, raw_b[:, 0, k:k + 1], start=(k == 0), stop=(k == DC - 1))
            for m in range(DC):
                for k in range(DC):
                    last = mm(gp[:, D + 2 + m:D + 3 + m], raw_wk[:, k, m * P:(m + 1) * P], raw_b[:, 0, k:k + 1],
                              start=(k == 0), stop=(k == DC - 1))
            last.then_inc(fused_bias, 1)
            for b in range(GB):
                turn_context(Group(0, 0), b)
            turn_last(Group(0, 0))
            pe.wait_ge(fused_copied, 1)

            def project(bank, at, w, src):
                for m in range(DC):
                    for k in range(DC):
                        last = mm(bank[:, at + m * P:at + (m + 1) * P], w[:, k, m * P:(m + 1) * P], src[:, k],
                                  start=(k == 0), stop=(k == DC - 1))
                return last

            def norm1T(a):
                pe.wait_ge(s["xn1"], a.count())
                transposes(xa[0], xn1[:, a.p]).then_inc(s["xn1T_ps"], 1)

            def norm2T(b):
                pe.wait_ge(s["xn2_ready"], b.count())
                transposes(sa[0], xn2[:]).then_inc(s["xn2T_ps"], 1)

            def norm3T(c):
                wait(pe, s["places_ready"], c.count(1))
                pe.wait_ge(s["xn3_ready"], c.count())
                transposes(gp, xn3[:, c.p]).then_inc(s["xn3T_ps"], 1)

            def queries(a):
                wait(pe, s["x1_ready"], a.count(1))
                pe.wait_ge(s["xn1T_ready"], a.count())
                project(xa[1], 0, wqk, xn1T).then_inc(s["qkT_ps"], 1)

            def projections(b):
                if isinstance(b.i, int) and b.index() == 0:
                    pe.wait_ge(sw_in, 16 * 8)
                pe.wait_ge(s["xn2T_ready"], b.count())
                project(sa[0], D, w_k, xn2T)
                project(sa[0], 0, w_q, xn2T).then_inc(s["qk_ps"], 1)
                wait(pe, s["v_heads_ready"], b.count(1) * 2)
                project(sa[1], 0, w_v, xn2T).then_inc(s["v_ps"], 1)

            def logits_rows(c):
                if isinstance(c.i, int) and c.index() == 0:
                    pe.wait_ge(gate_in, 16)
                    pe.wait_ge(tri_ready, 1)
                pe.wait_ge(s["xn3T_ready"], c.count())
                for k in range(DC):
                    last = mm(gp[0:E, 2 * P:3 * P], gate_w[:, k], xn3T[:, k], start=(k == 0), stop=(k == DC - 1))
                last.then_inc(s["logitsT_ps"], 1)

            def logits(c):
                wait_apart(pe, s["logitsT_ready"], c.count(), pe_passed)
                nc.tensor.transpose(gp[:, 3 * P:3 * P + E], logitsT[:], ident[0:E, 0:E]).then_inc(s["logits_ps"], 1)

            def ranks(c):
                wait(pe, s["routed_sum"], c.count(1))
                pe.wait_ge(s["routed_ready"], c.count())
                rank = gp[:, 3 * P + E:3 * P + 2 * E]
                mm(rank, earlier[:], routed[:], start=True, stop=False)
                mm(rank, ones[:], routed_before[:, c.p], start=False, stop=True).then_inc(s["rank_ps"], 1)

            def cross_scores(a):
                pe.wait_ge(s["qkT_ready"], a.count())
                pe.wait_ge(s["ctxT_ready"], a.count() * 5)
                for k in range(DC):
                    for j in range(GB):
                        last = mm(xa[0][T * j:T * j + T, 0:S], qkT[:, k, T * j:T * j + T], ctxT[:, a.p, j, k],
                                  start=(k == 0), stop=(k == DC - 1), tile_position=(0, T * j))
                last.then_inc(s["scores"], 1)

            def cross_probsT(a):
                pe.wait_ge(s["probs_ready"], a.count())
                transposes(xa[1], probs[:], SK).then_inc(s["probsT_ps"], 1)

            def cross_mix(a):
                pe.wait_ge(s["probsT_ready"], a.count())
                for k in range(SK):
                    for j in range(GB):
                        last = mm(xa[0][T * j:T * j + T, 0:D], probsT[:, k, T * j:T * j + T], ctx_in[:, a.p, j, k],
                                  start=(k == 0), stop=(k == SK - 1), tile_position=(0, T * j))
                last.then_inc(s["mix_ps"], 1)

            def cross_mixT(a):
                pe.wait_ge(s["mix_ready"], a.count())
                transposes(xa[0], mix[:]).then_inc(s["mixT_ps"], 1)

            def cross_out(a):
                if isinstance(a.i, int) and a.index() == 0:
                    pe.wait_ge(sw_in, 16 * 8)
                pe.wait_ge(s["mixT_ready"], a.count())
                for k in range(DC):
                    last = mm(xa[1][:, 0:D], mixT[:, k], w_xv[:, k], start=(k == 0), stop=(k == DC - 1))
                last.then_inc(s["xv_ps"], 1)

            def spread_values(b, n):
                if n == 0:
                    pe.wait_ge(s["vT_ready"], b.count())
                else:
                    pe.wait_ge(s["v_heads_ready"], b.count(1) * 2 + 1)
                for j in range(2):
                    for k in range(DC):
                        last = nc.tensor.transpose(sa[1][:, j * D + k * P:j * D + (k + 1) * P],
                                                   vT[:, k, 2 * n + j].rearrange("p r t -> p (r t)"), ident)
                last.then_inc(s["vrep_ps"], 1)

            def self_scores(b):
                pe.wait_ge(s["qT_ready"], b.count())
                pe.wait_ge(s["k_heads0"], b.count())
                pe.wait_ge(s["k_heads1"], b.count())
                pe.wait_ge(s["k_heads2"], b.count())
                for k in range(DC):
                    for j in range(GB):
                        last = mm(sa[0][T * j:T * j + T, k * HC * T:(k + 1) * HC * T], qT[:, k, T * j:T * j + T],
                                  k_heads[:, k, j], start=True, stop=True, tile_position=(0, T * j))
                last.then_inc(s["att_ps"], 1)

            def self_weightsT(d):
                wait(pe, s["x2_ready"], d.count(1))
                pe.wait_ge(s["att_exp_ready"], d.count())
                transposes(sa[2], att_exp[:].rearrange("p h k -> p (h k)"), H // HQ).then_inc(s["attT_ps"], 1)

            def self_mix(d):
                pe.wait_ge(s["v_heads_ready"], d.count() * 2)
                pe.wait_ge(s["attT_ready"], d.count())
                w = HQ * (DH + 1)
                for c4 in range(H // HQ):
                    for j in range(GB):
                        last = mm(sa[2][T * j:T * j + T, c4 * w:(c4 + 1) * w], attT[:, c4, T * j:T * j + T],
                                  v_heads[:, j, c4].rearrange("p h w -> p (h w)"), start=True, stop=True, tile_position=(0, T * j))
                last.then_inc(s["y_ps"], 1)

            def self_yT(d):
                pe.wait_ge(s["y_ready"], d.count())
                transposes(sa[2], y[:]).then_inc(s["yT_ps"], 1)

            def self_out(d):
                pe.wait_ge(s["yT_ready"], d.count())
                for k in range(DC):
                    last = mm(sa[2][:, 0:D], yT[:, k], w_o[:, k], start=(k == 0), stop=(k == DC - 1))
                last.then_inc(s["o_ps"], 1)

            def slot(a, b, d, c, f):
                run((norm1T, a), (norm3T, c), (self_weightsT, d), (queries, a), (logits_rows, c), (self_mix, d), (norm2T, b),
                    (logits, c), (cross_scores, a), (self_yT, d), (projections, b), (self_out, d), (cross_probsT, a),
                    (lambda g: turn_context(g, 0), f), (lambda g: spread_values(g, 0), b), (cross_mix, a), (self_scores, b),
                    (lambda g: turn_context(g, 1), f), (cross_mixT, a), (lambda g: spread_values(g, 1), b),
                    (lambda g: turn_context(g, 2), f), (lambda g: turn_context(g, 3), f), (ranks, c), (cross_out, a), (turn_last, f))
            pipeline(pe, slot)

            pe.wait_ge(s["routed_sum"], G)
            mm(sa[0][0:1, 0:E], ones[:, 0:1], routed_before[:, G % 2], start=True, stop=True).then_inc(s["counts_ps"], 1)
            pe.wait_ge(w2_in, E * 16)
            pe.wait_ge(s["table_ready"], 1)

            def expert_of(t):
                return pe.value_load(table[0:1, 0, bass.ds(t.index(), 1)], min_val=0, max_val=E - 1)

            for _ in range(25):
                nc.tensor.transpose(turn[1][:, 0:P], ident, ident)

            def turn_rows(t):
                pe.wait_ge(gathered[t.ring], t.ring_visits() * 16)
                transposes(turn[t.pair], xg[:, t.ring]).then_inc(s["xgT_ps"], 1)

            def up(t):
                pe.wait_ge(s["w1_ready"], t.count())
                pe.wait_ge(s["xgT_ready"], t.count())
                for m in range(HID // P):
                    for k in range(DC):
                        last = mm(xa[t.pair][:, m * P:(m + 1) * P], w1_now[:, t.pair, k, m * P:(m + 1) * P], xgT[:, t.pair, k],
                                  start=(k == 0), stop=(k == DC - 1))
                last.then_inc(s["hid_ps"], 1)

            def step(t, following, after, ahead):
                if following is not None:
                    up(following)
                if after is not None:
                    turn_rows(after)
                e = expert_of(t)
                pe.wait_ge(s["hid_ready"], t.count())
                for k in range(HID // P):
                    last = mm(exp_bank[t.pair][:, 0:D].unsqueeze(1), hid_relu[:, t.pair, k], w2[:, bass.ds(e, 1), k], start=(k == 0), stop=(k == HID // P - 1))
                last.then_inc(s["exp_ps"], 1)

            turn_rows(Tile(0, 0))
            up(Tile(0, 0))
            turn_rows(Tile(0, 1))
            tiles(pe, step)


def kernel(x, ctx_1024, L0_xattn_Wq, L0_xattn_bq, L0_xattn_Wk, L0_xattn_bk, L0_xattn_Wv, L0_xattn_bv,
           L0_attn_Wq, L0_attn_bq, L0_attn_Wk, L0_attn_bk, L0_attn_Wv, L0_attn_bv, L0_attn_Wo, L0_attn_bo,
           L0_ffn_gate_W, L0_ffn_W1, L0_ffn_b1, L0_ffn_W2, L0_ffn_b2):
    from concourse import bacc
    from concourse.bass_utils import run_bass_kernel_spmd

    arrays = {
        "x": np.asarray(x).reshape(N, D), "ctx": ctx_1024,
        "consts": shape_constants(), "slots_init": empty_slots(),
        "xWq": L0_xattn_Wq, "xbq": L0_xattn_bq, "xWk": L0_xattn_Wk, "xbk": L0_xattn_bk,
        "xWvT": np.asarray(L0_xattn_Wv).T, "xbv": L0_xattn_bv,
        "WqT": np.asarray(L0_attn_Wq).T, "bq": L0_attn_bq, "WkT": np.asarray(L0_attn_Wk).T, "bk": L0_attn_bk,
        "WvT": np.asarray(L0_attn_Wv).T, "bv": L0_attn_bv, "WoT": np.asarray(L0_attn_Wo).T, "bo": L0_attn_bo,
        "gate_W": L0_ffn_gate_W, "W1": L0_ffn_W1, "b1": L0_ffn_b1, "W2": L0_ffn_W2, "b2": L0_ffn_b2,
    }
    nc = bacc.Bacc("TRN2", target_bir_lowering=False, num_devices=1)
    in_map, args = {}, []
    for name, a in arrays.items():
        a = np.ascontiguousarray(a)
        in_map[f"in_{name}"] = a
        args.append(nc.dram_tensor(f"in_{name}", a.shape, mybir.dt.from_np(a.dtype), kind="ExternalInput").ap())
    out = nc.dram_tensor("out", (N + P, D), F32, kind="ExternalOutput").ap()
    perceiver_layer(nc, *args, out)
    r = run_bass_kernel_spmd(nc, [in_map], core_ids=[0])
    return r.results[0]["out"][:N].reshape(B, T, D)
```
